# Optimizing a Trainium2 kernel written in Bass

```python
import numpy as np
import jax
import jax.numpy as jnp

def _softmax(x, axis=-1):
    return jax.nn.softmax(x, axis=axis)

def _gelu(x):
    return jax.nn.gelu(x, approximate=True)

def _silu(x):
    return jax.nn.silu(x)

def _sigmoid(x):
    return jax.nn.sigmoid(x)

def _layernorm(x, axis=-1, eps=1e-05):
    m = jnp.mean(x, axis=axis, keepdims=True)
    v = jnp.var(x, axis=axis, keepdims=True)
    return (x - m) / jnp.sqrt(v + eps)

def _scatter_add(tgt, idx, src, axis=0):
    return tgt.at[idx].add(src)

def _segment_sum(src, seg, n):
    return jax.ops.segment_sum(src, seg, n)
kernel_name = 'mk_decoder_preln_d1_seqx_r8_2adb53'

def setup_inputs(seed: int=0):
    np.random.seed(seed)
    _w = jnp.asarray

    def _rec_inputs():
        import jax
        import jax.numpy as jnp
        _rk = jax.random.key(seed)
        x = -0.0003929 + 0.9999 * jax.random.normal(jax.random.fold_in(_rk, 1), (32, 64, 512), jnp.float32)
        _lenS = 64 - jax.random.randint(jax.random.fold_in(_rk, 7), (32,), 0, max(1, 64 // 4) + 1, jnp.int32)
        _lenS2 = 64 - jax.random.randint(jax.random.fold_in(_rk, 8), (32,), 0, max(1, 64 // 4) + 1, jnp.int32)
        _ctx_4096P = jax.random.normal(jax.random.fold_in(_rk, 11), (32, 16, 512), jnp.float32)
        _ctx_4096c = jax.random.dirichlet(jax.random.fold_in(_rk, 511), 0.3 * jnp.ones((16,), jnp.float32), (32, 64))
        _ctx_4096t = jnp.einsum('bsk,bkd->bsd', _ctx_4096c, _ctx_4096P)
        _ctx_4096t = _ctx_4096t * jax.lax.rsqrt(jnp.mean(jnp.square(_ctx_4096t)) + 1e-12) * 0.953939
        ctx_4096 = 2.81802e-05 + 1.00001 * (_ctx_4096t + 0.3 * jax.random.normal(jax.random.fold_in(_rk, 611), (32, 64, 512), jnp.float32))
        pos_BxS2 = jnp.broadcast_to(jnp.arange(64, dtype=jnp.int32), (32, 64))
        _validS = jnp.arange(64)[None, :] < _lenS[:, None]
        _validS2 = jnp.arange(64)[None, :] < _lenS2[:, None]
        _causal = jnp.tril(jnp.ones((64, 64), dtype=bool))
        mask_BxSxS2_ik0 = jnp.where(jnp.broadcast_to(_validS2[:, None, :], (32, 64, 64)), 0, 1).astype(jnp.int32)
        return (x, ctx_4096, pos_BxS2, mask_BxSxS2_ik0)
    x, ctx_4096, pos_BxS2, mask_BxSxS2_ik0 = _rec_inputs()

    def _L0_attn_setup():
        import jax, jax.numpy as jnp
        import numpy as np
        from jax import lax
        H = 512
        DIN = 1024
        N = 16
        K = 4
        R = 32
        B_SZ = 2
        L = 256
        EPS = 1e-06

        def rmsnorm(x, w):
            return x * lax.rsqrt(jnp.mean(x * x, axis=-1, keepdims=True) + EPS) * w

        def _selective_scan(x, dt, A, Bm, Cm):
            xT = jnp.transpose(x, (2, 0, 1))
            dtT = jnp.transpose(dt, (2, 0, 1))
            BT = jnp.transpose(Bm, (2, 0, 1))
            CT = jnp.transpose(Cm, (2, 0, 1))

            def step(h, inp):
                x_t, dt_t, B_t, C_t = inp
                dA = jnp.exp(dt_t[..., None] * A)
                dBx = dt_t[..., None] * B_t[:, None, :] * x_t[..., None]
                h = dA * h + dBx
                y = jnp.einsum('bdn,bn->bd', h, C_t)
                return (h, y)
            h0 = jnp.zeros((x.shape[0], x.shape[1], A.shape[1]), dtype=x.dtype)
            _, ys = lax.scan(step, h0, (xT, dtT, BT, CT))
            return jnp.transpose(ys, (1, 2, 0))
        key = jax.random.key(seed)
        ks = jax.random.split(key, 8)
        hidden_states = jax.random.normal(ks[0], (B_SZ, L, H), dtype=jnp.float32)
        s = 0.02
        in_proj_w = jax.random.normal(ks[1], (H, 2 * DIN), dtype=jnp.float32) * s
        conv_w = jax.random.normal(ks[2], (DIN, K), dtype=jnp.float32) * 0.2
        conv_b = jax.random.normal(ks[3], (DIN,), dtype=jnp.float32) * 0.02
        x_proj_w = jax.random.normal(ks[4], (R + 2 * N, DIN), dtype=jnp.float32) * s
        dt_proj_w = jax.random.normal(ks[5], (DIN, R), dtype=jnp.float32) * s
        dt_bias = jax.random.normal(ks[6], (DIN,), dtype=jnp.float32) * 0.5 - 4.0
        A_log = jnp.log(jnp.broadcast_to(jnp.arange(1, N + 1, dtype=jnp.float32)[None, :], (DIN, N)))
        D_param = jnp.ones((DIN,), dtype=jnp.float32)
        out_proj_w = jax.random.normal(ks[7], (H, DIN), dtype=jnp.float32) * s
        dt_ln_w = jnp.ones((R,), dtype=jnp.float32)
        B_ln_w = jnp.ones((N,), dtype=jnp.float32)
        C_ln_w = jnp.ones((N,), dtype=jnp.float32)
        return dict(hidden_states=hidden_states, in_proj_w=in_proj_w, conv_w=conv_w, conv_b=conv_b, x_proj_w=x_proj_w, dt_proj_w=dt_proj_w, dt_bias=dt_bias, A_log=A_log, D_param=D_param, out_proj_w=out_proj_w, dt_ln_w=dt_ln_w, B_ln_w=B_ln_w, C_ln_w=C_ln_w)
    _L0_attn_all = _L0_attn_setup()
    _L0_attn_in = {k: v for k, v in _L0_attn_all.items() if k in ('in_proj_w', 'conv_w', 'conv_b', 'x_proj_w', 'dt_proj_w', 'dt_bias', 'A_log', 'D_param', 'out_proj_w', 'dt_ln_w', 'B_ln_w', 'C_ln_w')}
    del _L0_attn_all

    def _L0_xattn_setup():
        import jax, jax.numpy as jnp
        import numpy as np
        B, S, E = (2, 256, 512)
        H, KVH, D = (32, 8, 128)
        GROUPS = H // KVH
        MAX_POS = 512
        ROPE_THETA = 10000.0

        def _rope_tables(max_pos, dim, theta):
            inv_freq = 1.0 / theta ** (jnp.arange(0, dim, 2, dtype=jnp.float32) / dim)
            t = jnp.arange(max_pos, dtype=jnp.float32)
            freqs = jnp.einsum('i,j->ij', t, inv_freq)
            emb = jnp.concatenate([freqs, freqs], axis=-1)
            return (jnp.cos(emb), jnp.sin(emb))

        def _rotate_half(x):
            x1, x2 = (x[..., :x.shape[-1] // 2], x[..., x.shape[-1] // 2:])
            return jnp.concatenate([-x2, x1], axis=-1)
        key = jax.random.key(seed)
        ks = jax.random.split(key, 8)
        scale_w = 1.0 / np.sqrt(E)
        query = jax.random.normal(ks[0], (B, S, E), dtype=jnp.float32)
        k_in = jax.random.normal(ks[1], (B, S, E), dtype=jnp.float32)
        v_in = jax.random.normal(ks[2], (B, S, E), dtype=jnp.float32)
        position_ids = jnp.broadcast_to(jnp.arange(S, dtype=jnp.int64), (B, S))
        src_mask = jnp.tril(jnp.ones((S, S), dtype=jnp.int32))
        src_mask = jnp.broadcast_to(src_mask, (B, S, S))
        Wq = jax.random.normal(ks[3], (E, H * D), dtype=jnp.float32) * scale_w
        Wk = jax.random.normal(ks[4], (E, KVH * D), dtype=jnp.float32) * scale_w
        Wv = jax.random.normal(ks[5], (E, KVH * D), dtype=jnp.float32) * scale_w
        Wo = jax.random.normal(ks[6], (H * D, E), dtype=jnp.float32) * scale_w
        return {'query': query, 'key': k_in, 'value': v_in, 'position_ids': position_ids, 'src_mask': src_mask, 'Wq': Wq, 'Wk': Wk, 'Wv': Wv, 'Wo': Wo}
    _L0_xattn_all = _L0_xattn_setup()
    _L0_xattn_in = {k: v for k, v in _L0_xattn_all.items() if k in ('Wq', 'Wk', 'Wv', 'Wo')}
    del _L0_xattn_all

    def _L0_ffn_setup():
        import jax, jax.numpy as jnp
        import numpy as np
        IN_F = 512
        OUT_F = 512
        RANK = 8
        NUM_EXPERTS = 64
        TOP_K = 16
        ROUTER_DIM = 16
        ALPHA = 32
        SCALING = ALPHA / TOP_K
        BOTTLENECK = NUM_EXPERTS * RANK
        key = jax.random.key(seed)
        ks = jax.random.split(key, 5)
        x = jax.random.normal(ks[0], (4, 512, IN_F), dtype=jnp.float32)
        bound_a = float(np.sqrt(6.0 / IN_F))
        A_w = jax.random.uniform(ks[1], (BOTTLENECK, IN_F), jnp.float32, -bound_a, bound_a)
        B_w = jax.random.normal(ks[2], (OUT_F, BOTTLENECK), dtype=jnp.float32) * 0.02
        Wq_w = jax.random.normal(ks[3], (ROUTER_DIM, IN_F), dtype=jnp.float32) * 0.02
        keys = jax.random.normal(ks[4], (NUM_EXPERTS, ROUTER_DIM), dtype=jnp.float32) * 0.01
        return {'x': x, 'A_w': A_w, 'B_w': B_w, 'Wq_w': Wq_w, 'keys': keys}
    _L0_ffn_all = _L0_ffn_setup()
    _L0_ffn_in = {k: v for k, v in _L0_ffn_all.items() if k in ('A_w', 'B_w', 'Wq_w', 'keys')}
    del _L0_ffn_all
    return {'x': x, 'ctx_4096': ctx_4096, 'pos_BxS2': pos_BxS2, 'mask_BxSxS2_ik0': mask_BxSxS2_ik0, 'L0_attn_in_proj_w': _L0_attn_in['in_proj_w'], 'L0_attn_conv_w': _L0_attn_in['conv_w'], 'L0_attn_conv_b': _L0_attn_in['conv_b'], 'L0_attn_x_proj_w': _L0_attn_in['x_proj_w'], 'L0_attn_dt_proj_w': _L0_attn_in['dt_proj_w'], 'L0_attn_dt_bias': _L0_attn_in['dt_bias'], 'L0_attn_A_log': _L0_attn_in['A_log'], 'L0_attn_D_param': _L0_attn_in['D_param'], 'L0_attn_out_proj_w': _L0_attn_in['out_proj_w'], 'L0_attn_dt_ln_w': _L0_attn_in['dt_ln_w'], 'L0_attn_B_ln_w': _L0_attn_in['B_ln_w'], 'L0_attn_C_ln_w': _L0_attn_in['C_ln_w'], 'L0_xattn_Wq': _L0_xattn_in['Wq'], 'L0_xattn_Wk': _L0_xattn_in['Wk'], 'L0_xattn_Wv': _L0_xattn_in['Wv'], 'L0_xattn_Wo': _L0_xattn_in['Wo'], 'L0_ffn_A_w': _L0_ffn_in['A_w'], 'L0_ffn_B_w': _L0_ffn_in['B_w'], 'L0_ffn_Wq_w': _L0_ffn_in['Wq_w'], 'L0_ffn_keys': _L0_ffn_in['keys']}

def reference(x, ctx_4096, pos_BxS2, mask_BxSxS2_ik0, L0_attn_in_proj_w, L0_attn_conv_w, L0_attn_conv_b, L0_attn_x_proj_w, L0_attn_dt_proj_w, L0_attn_dt_bias, L0_attn_A_log, L0_attn_D_param, L0_attn_out_proj_w, L0_attn_dt_ln_w, L0_attn_B_ln_w, L0_attn_C_ln_w, L0_xattn_Wq, L0_xattn_Wk, L0_xattn_Wv, L0_xattn_Wo, L0_ffn_A_w, L0_ffn_B_w, L0_ffn_Wq_w, L0_ffn_keys):
    import jax
    import jax.numpy as jnp

    def _L0_attn_ref(hidden_states, in_proj_w, conv_w, conv_b, x_proj_w, dt_proj_w, dt_bias, A_log, D_param, out_proj_w, dt_ln_w, B_ln_w, C_ln_w):
        import jax, jax.numpy as jnp
        import numpy as np
        from jax import lax
        H = 512
        DIN = 1024
        N = 16
        K = 4
        R = 32
        B_SZ = 2
        L = 256
        EPS = 1e-06

        def rmsnorm(x, w):
            return x * lax.rsqrt(jnp.mean(x * x, axis=-1, keepdims=True) + EPS) * w

        def _selective_scan(x, dt, A, Bm, Cm):
            xT = jnp.transpose(x, (2, 0, 1))
            dtT = jnp.transpose(dt, (2, 0, 1))
            BT = jnp.transpose(Bm, (2, 0, 1))
            CT = jnp.transpose(Cm, (2, 0, 1))

            def step(h, inp):
                x_t, dt_t, B_t, C_t = inp
                dA = jnp.exp(dt_t[..., None] * A)
                dBx = dt_t[..., None] * B_t[:, None, :] * x_t[..., None]
                h = dA * h + dBx
                y = jnp.einsum('bdn,bn->bd', h, C_t)
                return (h, y)
            h0 = jnp.zeros((x.shape[0], x.shape[1], A.shape[1]), dtype=x.dtype)
            _, ys = lax.scan(step, h0, (xT, dtT, BT, CT))
            return jnp.transpose(ys, (1, 2, 0))
        proj = hidden_states @ in_proj_w
        x, z = jnp.split(proj, 2, axis=-1)
        x = jnp.transpose(x, (0, 2, 1))
        z = jnp.transpose(z, (0, 2, 1))
        Lq = x.shape[-1]
        xp = jnp.pad(x, ((0, 0), (0, 0), (K - 1, 0)))
        xc = conv_b[None, :, None]
        for k in range(K):
            xc = xc + conv_w[None, :, k:k + 1] * xp[:, :, k:k + Lq]
        xc = jax.nn.silu(xc)
        ssm_p = jnp.einsum('bdl,ed->ble', xc, x_proj_w)
        dt_r = rmsnorm(ssm_p[..., :R], dt_ln_w)
        Bm = rmsnorm(ssm_p[..., R:R + N], B_ln_w)
        Cm = rmsnorm(ssm_p[..., R + N:], C_ln_w)
        dt = jnp.einsum('blr,dr->bdl', dt_r, dt_proj_w)
        dt = jax.nn.softplus(dt + dt_bias[None, :, None])
        A = -jnp.exp(A_log)
        Bm = jnp.transpose(Bm, (0, 2, 1))
        Cm = jnp.transpose(Cm, (0, 2, 1))
        ys = _selective_scan(xc, dt, A, Bm, Cm)
        y = (ys + D_param[None, :, None] * xc) * jax.nn.silu(z)
        return jnp.einsum('bdl,hd->blh', y, out_proj_w)

    def _L0_xattn_ref(query, key, value, position_ids, src_mask, Wq, Wk, Wv, Wo):
        import jax, jax.numpy as jnp
        import numpy as np
        B, S, E = (2, 256, 512)
        H, KVH, D = (32, 8, 128)
        GROUPS = H // KVH
        MAX_POS = 512
        ROPE_THETA = 10000.0

        def _rope_tables(max_pos, dim, theta):
            inv_freq = 1.0 / theta ** (jnp.arange(0, dim, 2, dtype=jnp.float32) / dim)
            t = jnp.arange(max_pos, dtype=jnp.float32)
            freqs = jnp.einsum('i,j->ij', t, inv_freq)
            emb = jnp.concatenate([freqs, freqs], axis=-1)
            return (jnp.cos(emb), jnp.sin(emb))

        def _rotate_half(x):
            x1, x2 = (x[..., :x.shape[-1] // 2], x[..., x.shape[-1] // 2:])
            return jnp.concatenate([-x2, x1], axis=-1)
        nb, q_len, _ = query.shape
        q = (query @ Wq).reshape(nb, q_len, H, D).transpose(0, 2, 1, 3)
        k = (key @ Wk).reshape(nb, q_len, KVH, D).transpose(0, 2, 1, 3)
        v = (value @ Wv).reshape(nb, q_len, KVH, D).transpose(0, 2, 1, 3)
        cos_t, sin_t = _rope_tables(MAX_POS, D, ROPE_THETA)
        cos = cos_t[position_ids][:, None]
        sin = sin_t[position_ids][:, None]
        q = q * cos + _rotate_half(q) * sin
        k = k * cos + _rotate_half(k) * sin
        k = jnp.repeat(k, GROUPS, axis=1)
        v = jnp.repeat(v, GROUPS, axis=1)
        scores = jnp.einsum('bhqd,bhkd->bhqk', q, k) / jnp.sqrt(jnp.float32(D))
        mask = src_mask[:, None]
        scores = jnp.where(mask == 0, jnp.float32(-1000000000.0), scores)
        attn = jax.nn.softmax(scores, axis=-1)
        x = jnp.einsum('bhqk,bhkd->bhqd', attn, v)
        x = x.transpose(0, 2, 1, 3).reshape(nb, q_len, H * D)
        return x @ Wo

    def _L0_ffn_ref(x, A_w, B_w, Wq_w, keys):
        import jax, jax.numpy as jnp
        import numpy as np
        IN_F = 512
        OUT_F = 512
        RANK = 8
        NUM_EXPERTS = 64
        TOP_K = 16
        ROUTER_DIM = 16
        ALPHA = 32
        SCALING = ALPHA / TOP_K
        BOTTLENECK = NUM_EXPERTS * RANK
        q = jnp.einsum('bsd,rd->bsr', x, Wq_w)
        scores = jnp.einsum('bsr,er->bse', q, keys)
        top_vals, top_idx = jax.lax.top_k(scores, TOP_K)
        top_w = jax.nn.softmax(top_vals, axis=-1)
        gate = jnp.sum(jax.nn.one_hot(top_idx, NUM_EXPERTS, dtype=top_w.dtype) * top_w[..., None], axis=-2)
        z = jnp.einsum('bsd,nd->bsn', x, A_w)
        z = z.reshape(*z.shape[:-1], NUM_EXPERTS, RANK)
        z_gated = (z * gate[..., None]).reshape(*z.shape[:-2], BOTTLENECK)
        out = jnp.einsum('bsn,on->bso', z_gated, B_w) * SCALING
        return out
    x = x + _L0_attn_ref(_layernorm(x, axis=-1), L0_attn_in_proj_w, L0_attn_conv_w, L0_attn_conv_b, L0_attn_x_proj_w, L0_attn_dt_proj_w, L0_attn_dt_bias, L0_attn_A_log, L0_attn_D_param, L0_attn_out_proj_w, L0_attn_dt_ln_w, L0_attn_B_ln_w, L0_attn_C_ln_w)
    x = x + _L0_xattn_ref(_layernorm(x, axis=-1), ctx_4096, ctx_4096, pos_BxS2, mask_BxSxS2_ik0, L0_xattn_Wq, L0_xattn_Wk, L0_xattn_Wv, L0_xattn_Wo)
    x = x + _L0_ffn_ref(_layernorm(x, axis=-1), L0_ffn_A_w, L0_ffn_B_w, L0_ffn_Wq_w, L0_ffn_keys)
    return x

_drawn_inputs = setup_inputs


def setup_inputs(seed=0):
    import zlib

    import numpy as np

    out = dict(_drawn_inputs(seed))
    spreads = {'L0_attn_D_param': (1.0, 0.6),
     'L0_attn_dt_ln_w': (1.0, 0.6),
     'L0_attn_B_ln_w': (1.0, 0.6),
     'L0_attn_C_ln_w': (1.0, 0.6)}
    factors = {'L0_attn_in_proj_w': 6.254,
     'L0_attn_conv_w': 6.362,
     'L0_attn_conv_b': 8.0,
     'L0_attn_x_proj_w': 8.0,
     'L0_attn_dt_proj_w': 8.0,
     'L0_attn_dt_bias': 8.0,
     'L0_attn_A_log': 8.0,
     'L0_attn_out_proj_w': 6.308,
     'L0_ffn_A_w': 3.146,
     'L0_ffn_B_w': 3.109,
     'L0_ffn_Wq_w': 3.572,
     'L0_ffn_keys': 3.697}
    for name, (base, spread) in spreads.items():
        noise = np.random.default_rng([zlib.crc32(name.encode()), seed]).standard_normal(out[name].shape)
        drawn = base * np.exp(spread * noise) if base else spread * noise
        out[name] = jnp.asarray(drawn.astype(out[name].dtype))
    for name, factor in factors.items():
        out[name] = (out[name] * factor).astype(out[name].dtype)
    return out
```

```python
from contextlib import ExitStack

import numpy as np

import concourse.bass as bass
from concourse import mybir

F32 = mybir.dt.float32
I32 = mybir.dt.int32
U32 = mybir.dt.uint32
BF16 = mybir.dt.bfloat16
ALU = mybir.AluOpType
ACT = mybir.ActivationFunctionType
AX = mybir.AxisListType

P = 128
BATCH, SEQ, E = 32, 64, 512
NTOK = BATCH * SEQ
T = 512
NBLK = NTOK // T
TT = T // P
NB = T // SEQ
KE = E // P
DIN, NS, KC, R = 1024, 16, 4, 32
DT_TILES = DIN // P
SSM = R + 2 * NS
HEADS, KVH, D = 32, 8, 128
PAIRS = HEADS // 2
MAXPOS, THETA = 512, 10000.0
EXPERTS, RANK, TOPK, RD = 64, 8, 16, 16
SCALING = 32 / TOPK
LN_EPS, RMS_EPS = 1e-5, 1e-6
NCH = 4
CW = 2 * T
NEG = -3.0e38
LEAD = 8


class Stage:

    def __init__(self, nc, ctx, name, per):
        self.sem = ctx.enter_context(nc.semaphore(name))
        self.per = per

    def upto(self, block, index):
        return block * self.per + (index + 1 + LEAD)


class Chain:

    def __init__(self, eng, stage, block):
        self.eng, self.stage, self.block, self.n = eng, stage, block, 0

    def __call__(self, ins):
        ins.then_inc(self.stage.sem, 1)
        self.n += 1

    def wait(self):
        self.eng.wait_ge(self.stage.sem, self.stage.upto(self.block, self.n - 1))

    def end(self):
        assert self.n == self.stage.per, (self.n, self.stage.per)


def build(nc, a, out):
    ctx = ExitStack()
    with ctx:
        def sb(name, shape, dt=F32):
            return ctx.enter_context(nc.sbuf_tensor(name, shape, dt))

        def pb(name, shape):
            return ctx.enter_context(nc.psum_tensor(name, shape, F32))

        def sem(name):
            return ctx.enter_context(nc.semaphore(name))

        scr = nc.dram_tensor("bc_rows", (NBLK, 2, NS, T), F32, kind="Internal").ap()

        xm = sb("xm", [P, TT, E])
        xa = sb("xa", [P, TT, E])
        xnT = sb("xnT", [P, KE, T])
        qT = sb("qT", [P, KE, T])
        ctxT = sb("ctxT", [P, KE, T])
        xc = sb("xc", [P, DT_TILES, T])
        dt = sb("dt", [P, DT_TILES, T])
        u = sb("u", [P, DT_TILES, T])
        bc = sb("bc", [P, 2, 2, T])
        dA = sb("dA", [P, 2, CW])
        hs = sb("hs", [P, NCH, CW])
        wa = sb("wa", [P, 2, KE * 2 * P])
        wb = sb("wb", [P, 2, 2 * E])
        wk = sb("wk", [P, KE, D])
        wv = sb("wv", [P, KE, D])
        qp = sb("qp", [P, NB, 2 * SEQ])
        qr = sb("qr", [P, 2, T])
        kT = sb("kT", [P, T])
        kr = sb("kr", [P, T])
        vt = sb("vt", [P, TT, D])
        pr = sb("pr", [P, NB, SEQ])
        pz = sb("pz", [P, TT, 2, P])
        oT = sb("oT", [P, 2, T])
        cosT = sb("cosT", [P, T])
        sinT = sb("sinT", [P, T])
        mmul = sb("mmul", [P, NB, SEQ])
        madd = sb("madd", [P, NB, SEQ])
        ident = sb("ident", [P, P])
        zeros = sb("zeros", [P, 512], BF16)
        xpw = sb("xpw", [P, DT_TILES, SSM])
        dtw = sb("dtw", [R, DIN])
        rqw = sb("rqw", [P, KE, RD])
        rkw = sb("rkw", [RD, EXPERTS])
        lnw = sb("lnw", [P, SSM])
        cw = sb("cw", [P, DT_TILES, KC])
        chan = sb("chan", [P, 3, DT_TILES])
        aneg = sb("aneg", [P, DT_TILES, NS])
        posi = sb("posi", [P, TT], I32)
        posf = sb("posf", [P, 2, TT])
        posu = sb("posu", [P, TT], U32)
        stats = sb("stats", [P, TT, 6])
        mv = sb("mv", [P, TT, 2])
        ve = sb("ve", [P, 16])
        rs = sb("rs", [P, 16])
        mhalf = sb("mhalf", [P, 16])
        ss = sb("ss", [P, TT, 3])
        mx = sb("mx", [P, NB])
        sm = sb("sm", [P, NB])
        top = sb("top", [P, TT, 16])
        negm = sb("negm", [P, TT])
        gs = sb("gs", [P, TT])
        xn = dt[:, 0:TT, :]
        ssmT = kr[0:SSM, :]
        ssq = qr[:, 0, 0:TT * SSM].rearrange("p (t c) -> p t c", c=SSM)
        ssn = qr[:, 1, 0:TT * SSM].rearrange("p (t c) -> p t c", c=SSM)
        qp2 = qp[:, :, :].rearrange("p b c -> p (b c)").rearrange("p (h t) -> p h t", h=2)
        e_b, l_b, v_b = qp2, oT, qr
        x3T = u[:, 0:KE, :]
        zgT = u[:, KE:2 * KE, :]
        zg = dt[:, TT:2 * TT, :]
        rq = kr[0:RD, :]
        rsc = pr[:, :, :].rearrange("p b k -> p (b k)")[:, 0:TT * EXPERTS].rearrange("p (t e) -> p t e", e=EXPERTS)
        gate = pr[:, :, :].rearrange("p b k -> p (b k)")[:, TT * EXPERTS:2 * TT * EXPERTS].rearrange(
            "p (t e) -> p t e", e=EXPERTS)
        gex = kT[:, 0:TT * EXPERTS].rearrange("p (t e) -> p t e", e=EXPERTS)
        tab = oT[:, :, :].rearrange("p h t -> p (h t)").rearrange("p (t c) -> p t c", c=2 * D)
        mraw = qr[:, 0, :].bitcast(I32).rearrange("p (b k) -> p b k", k=SEQ)
        sz = qp2

        acc = pb("acc", [P, TT, 512])
        pq = pb("pq", [P, 2, 512])
        pk = pb("pk", [P, 2, 512])

        def bank(n):
            return pq[:, n, :] if n < 2 else pk[:, n - 2, :]

        def stage(name, per):
            return Stage(nc, ctx, name, per)

        s_const = sem("const_loaded")
        s_x = sem("x_loaded")
        s_ctx = sem("ctx_loaded")
        s_mask = sem("mask_loaded")
        s_pos = sem("pos_loaded")
        s_tab = sem("rotary_rows_loaded")
        s_bcw = sem("bc_rows_stored")
        s_bc = [sem(f"bc_loaded{p}") for p in range(2)]
        s_wa = [sem(f"wa_loaded{p}") for p in range(2)]
        s_wb = [sem(f"wb_loaded{p}") for p in range(2)]
        s_wk = sem("wk_loaded")
        s_wv = sem("wv_loaded")
        s_out = sem("out_stored")
        s_ident = sem("ident_made")
        s_init = sem("buffers_cleared")
        s_aneg = sem("decay_rates_made")
        ln1 = stage("ln1_variance", 1)
        ln1r = stage("ln1_rstd", 1)
        ln1n = stage("ln1_done", TT)
        ln1t = stage("ln1_transposed", KE)
        xnr = stage("xnT_ready", KE)
        inx = stage("in_proj_x", DT_TILES)
        cv0 = stage("conv_tap_last", DT_TILES)
        cv = stage("conv_done", DT_TILES)
        xcr = stage("xc_ready", DT_TILES)
        ssd = stage("ssm_done", 1)
        ssqd = stage("ssm_squared", 1)
        ssv = stage("ssm_mean_square", 1)
        ssr = stage("ssm_rms", 1)
        ssnd = stage("ssm_normalised", 1)
        sst = stage("ssm_transposed", 1)
        sstr = stage("ssmT_ready", 1)
        dtd = stage("dt_proj", DT_TILES)
        spa = stage("softplus_act", DT_TILES)
        spe = stage("softplus_exp", DT_TILES)
        spd = stage("softplus_dve", DT_TILES)
        ur = stage("u_ready", DT_TILES)
        ch_f = stage("dve_first_phase", 2 * TT + 6 + (KC - 2 + 5) * DT_TILES)
        ca_f = stage("act_first_phase", 2 * DT_TILES)
        dar = stage("decay_ready", NS * NCH)
        inr = stage("scan_input_ready", NS * NCH)
        scd = stage("scan_done", NS * NCH)
        hcd = stage("state_times_c", NS * NCH)
        yad = stage("y_added", NS * NCH)
        pxd = stage("mask_ready", 1)
        pid = stage("pos_index_ready", 1)
        rot = stage("rotary_transposed", 1)
        rop = stage("rotary_ready", 1)
        ac0 = stage("acc_cleared", 1)
        qd = stage("q_done", PAIRS)
        kd = stage("k_done", KVH)
        vd = stage("v_done", KVH)
        qrd = stage("q_swapped", PAIRS)
        krd = stage("k_swapped", KVH)
        qt1 = stage("q_times_cos", PAIRS)
        qt2 = stage("q_times_sin", PAIRS)
        kt1 = stage("k_times_cos", KVH)
        kt2 = stage("k_times_sin", KVH)
        qrdy = stage("q_ready", PAIRS)
        krdy = stage("k_ready", KVH)
        vrdy = stage("v_ready", KVH)
        sd = stage("scores_done", PAIRS)
        srd = stage("scores_read", PAIRS)
        smk = stage("scores_masked", PAIRS)
        smx = stage("scores_max", PAIRS)
        ssb = stage("scores_shifted", PAIRS)
        exd = stage("exp_done", PAIRS)
        sum_ = stage("exp_summed", PAIRS)
        rcp = stage("sum_inverted", PAIRS)
        prdy = stage("probs_ready", PAIRS)
        ptd = stage("probs_transposed", PAIRS)
        ptr = stage("probsT_ready", PAIRS)
        pvd = stage("pv_done", PAIRS)
        ordy = stage("o_ready", PAIRS)
        wod = stage("wo_done", PAIRS)
        x2r = stage("x2_ready", TT)
        ln3 = stage("ln3_variance", 1)
        ln3r = stage("ln3_rstd", 1)
        ln3n = stage("ln3_done", TT)
        ln3t = stage("ln3_transposed", KE)
        x3r = stage("x3T_ready", KE)
        rqd = stage("router_q", 1)
        rqr = stage("router_q_ready", 1)
        rsd = stage("router_scores", 1)
        rmd = stage("router_max", 1)
        rex = stage("router_exp", 1)
        awd = stage("a_proj", TT)
        zgd = stage("z_gated", TT)
        zgt = stage("z_transposed", KE)
        zgr = stage("zT_ready", KE)
        bwd = stage("b_proj", TT)
        outr = stage("out_ready", 1)
        ch_a = stage("dve_mixture", 4 + 8 * TT)
        inz = stage("in_proj_z", DT_TILES)
        szr = stage("silu_z", DT_TILES)
        yr = stage("y_gated", DT_TILES)
        opd = stage("out_proj", TT)
        x1r = stage("x1_ready", TT)
        ln2 = stage("ln2_variance", 1)
        ln2r = stage("ln2_rstd", 1)
        ln2n = stage("ln2_done", TT)
        ln2t = stage("ln2_transposed", KE)
        qTr = stage("qT_ready", KE)
        ch_m = stage("dve_x1_norm", 2 * TT)
        wad = sem("wa_used")
        wbd = sem("wb_used")
        WA_MAMBA, WA_ATTN = 2 * DT_TILES // 2, PAIRS + KE // 2
        WB_MAMBA, WB_ATTN = DT_TILES // 2, PAIRS + KE // 2

        def wa_base(i):
            return WA_MAMBA + (i - 1) * (WA_MAMBA + WA_ATTN) if not isinstance(i, int) or i else 0

        def wb_base(i):
            return WB_MAMBA + (i - 1) * (WB_MAMBA + WB_ATTN) if not isinstance(i, int) or i else 0

        def wa_half(i):
            return wa_base(i) // 2 if isinstance(i, int) else (
                WA_MAMBA // 2 + (i - 1) * ((WA_MAMBA + WA_ATTN) // 2))

        def wb_half(i):
            return wb_base(i) // 2 if isinstance(i, int) else (
                WB_MAMBA // 2 + (i - 1) * ((WB_MAMBA + WB_ATTN) // 2))

        def wa_first(mamba, attn):
            at_q = WA_MAMBA // 2 if mamba else 0
            at_a = at_q + (PAIRS if attn else 0)
            at_z = at_a + (KE // 2 if attn else 0)
            return at_q, at_a, at_z

        def wb_first(mamba, attn):
            return (PAIRS, PAIRS + KE // 2) if attn else (0, 0)

        block = ctx.enter_context(nc.Block())

        s_hold = sem("held_on_its_own")

        def hold(eng):
            eng.sem_inc(s_hold, 1)

        def lead(eng, *stages):
            for s in stages:
                eng.sem_inc(s.sem if isinstance(s, Stage) else s, LEAD)

        def iterations(eng, one):
            one(0, True, False)
            with eng.Fori(1, NBLK) as i:
                one(i, True, True)
            one(NBLK, False, True)

        def steps(eng, one):
            with eng.Fori(0, NS // 2 - 1) as jj:
                one(jj, 0, False)
                one(jj, 1, False)
            one(NS // 2 - 1, 0, True)
            one(NS // 2 - 1, 1, True)

        @block.sync
        def _(eng):
            consts = [(xpw, a["xpw"]), (dtw, a["dtw"]), (rqw, a["rqw"]), (rkw, a["rkw"]), (lnw, a["lnw"]),
                      (cw, a["cw"]), (chan, a["chan"]), (aneg, a["alog"])]

            def load_wa(i, at, src):
                eng.wait_ge(wad, wa_base(i) + at + (LEAD - 1))
                eng.dma_start(wa[:, at % 2, :], src).then_inc(s_wa[at % 2], 16)

            def load_wa_j(i, at, jj, p, src):
                eng.wait_ge(wad, wa_base(i) + jj * 2 + (at + p + LEAD - 1))
                eng.dma_start(wa[:, p, :], src).then_inc(s_wa[p], 16)

            def load_wb(i, at, src):
                eng.wait_ge(wbd, wb_base(i) + at + (LEAD - 1))
                eng.dma_start(wb[:, at % 2, :], src).then_inc(s_wb[at % 2], 16)

            def load_wb_j(i, at, jj, p, src):
                eng.wait_ge(wbd, wb_base(i) + jj * 2 + (at + p + LEAD - 1))
                eng.dma_start(wb[:, p, :], src).then_inc(s_wb[p], 16)

            def one(i, mamba, attn):
                at_q, at_a, at_z = wa_first(mamba, attn)
                at_b, at_o = wb_first(mamba, attn)
                blk = i - 1
                if mamba:
                    if not isinstance(i, int):
                        eng.wait_ge(x1r.sem, x1r.upto(blk, TT - 1))
                    eng.dma_start(xm[:, :, :], a["x"][i]).then_inc(s_x, 16)
                if attn:
                    eng.wait_ge(vd.sem, vd.upto(blk, -1))
                    eng.dma_start(ctxT[:, :, :], a["ctx"][blk]).then_inc(s_ctx, 16)
                    eng.dma_start(posi[:, :], a["pos"][blk]).then_inc(s_pos, 16)
                    eng.dma_start(wk[:, :, :], a["wk"][0]).then_inc(s_wk, 16)
                    eng.dma_start(wv[:, :, :], a["wv"][0]).then_inc(s_wv, 16)
                if mamba:
                    for n in range(DT_TILES // 2):
                        load_wa(i, n, a["wx"][n])
                        if isinstance(i, int) and n == 0:
                            for dst, src in consts:
                                eng.dma_start(dst[...], src).then_inc(s_const, 16)
                if attn:
                    for n in range(2):
                        load_wa(i, at_q + n, a["wq"][n])
                        load_wb(i, n, a["wo"][n])
                if mamba:
                    eng.wait_ge(sstr.sem, sstr.upto(i, 0))
                    eng.dma_start(scr[i].rearrange("c n t -> (c n) t"), ssmT[R:SSM, :]).then_inc(s_bcw, 16)
                    eng.wait_ge(s_bcw, i * 16 + 16)
                    for n in range(2):
                        eng.wait_ge(hcd.sem, hcd.upto(i, -1))
                        eng.dma_start(bc[:, n, :, :], scr[i, :, n, :].partition_broadcast(P)).then_inc(s_bc[n], 16)
                if attn:
                    if mamba:
                        eng.wait_ge(spd.sem, spd.upto(i, DT_TILES - 1))
                    else:
                        eng.wait_ge(outr.sem, outr.upto(blk, -1))
                    for h in range(2):
                        eng.dma_start(mraw[h * SEQ:(h + 1) * SEQ, :, :], a["mask"][blk]).then_inc(s_mask, 16)

                def step(jj, p, tail):
                    if attn:
                        if not tail:
                            load_wa_j(i, at_q + 2, jj, p, a["wq"][jj * 2 + (2 + p)])
                            if p == 0:
                                eng.wait_ge(kd.sem, kd.upto(blk, jj))
                                eng.dma_start(wk[:, :, :], a["wk"][jj + 1]).then_inc(s_wk, 16)
                            else:
                                eng.wait_ge(vd.sem, vd.upto(blk, jj))
                                eng.dma_start(wv[:, :, :], a["wv"][jj + 1]).then_inc(s_wv, 16)
                    if mamba and not tail:
                        eng.wait_ge(hcd.sem, hcd.upto(i, NCH * (p + 1) - 1) + jj * (2 * NCH))
                        eng.dma_start(bc[:, p, :, :], scr[i, :, jj * 2 + (2 + p), :].partition_broadcast(P)).then_inc(
                            s_bc[p], 16)
                    if attn and not tail:
                        load_wb_j(i, 2, jj, p, a["wo"][jj * 2 + (2 + p)])

                steps(eng, step)
                if attn:
                    for n in range(KE // 2):
                        load_wa(i, at_a + n, a["aw"][n])
                        load_wb(i, at_b + n, a["bw"][n])
                if mamba:
                    for n in range(DT_TILES // 2):
                        load_wa(i, at_z + n, a["wz"][n])
                    for n in range(DT_TILES // 2):
                        load_wb(i, at_o + n, a["ow"][n])
                if attn:
                    eng.wait_ge(outr.sem, outr.upto(blk, 0))
                    eng.dma_start(out[blk], xn).then_inc(s_out, 16)

            iterations(eng, one)
            eng.wait_ge(s_out, 16 * NBLK)

        @block.gpsimd
        def _(eng):
            lead(eng, ln1r, ssr, ln2r, ln3r, inr)
            G = nc.gpsimd
            G.memset(ident[:, :], 0.0).then_inc(s_ident, 1)
            eng.wait_ge(s_ident, 1)
            G.affine_select(out=ident[:, :], in_=ident[:, :], compare_op=ALU.not_equal, fill=1.0, base=0,
                            pattern=[[-1, P]], channel_multiplier=1).then_inc(s_ident, 1)
            G.memset(mhalf[:, :], -0.5).then_inc(s_init, 1)
            G.memset(dA[:, :, :], 0.0).then_inc(s_init, 1)
            G.memset(pz[:, :, :, :], 0.0).then_inc(s_init, 1)
            G.memset(zeros[:, :].bitcast(F32), 0.0).then_inc(s_init, 1)
            eng.wait_ge(s_init, 4)

            def rstd(blk, variance, done, n):
                eng.wait_ge(variance.sem, variance.upto(blk, 0))
                G.tensor_tensor(rs[:, 0:n], ve[:, 0:n], mhalf[:, 0:n], ALU.pow).then_inc(done.sem, 1)

            def one(i, mamba, attn):
                if mamba:
                    rstd(i, ln1, ln1r, TT)
                    rstd(i, ssv, ssr, 3 * TT)
                if attn:
                    eng.wait_ge(pid.sem, pid.upto(i - 1, 0))
                    hold(eng)
                    for t in range(TT):
                        eng.indirect_dma_start(
                            out=tab[:, t, :], out_offset=None, in_=a["rotary"],
                            in_offset=bass.IndirectOffsetOnAxis(ap=posu[:, t:t + 1], axis=0)).then_inc(s_tab, 16)

                def step(jj, p, tail):
                    if not mamba:
                        return
                    for c in range(NCH):
                        if c == 0:
                            eng.wait_ge(s_bc[p], i * (8 * NS) + jj * 16 + 16)
                        if c == 0 and p == 0:
                            eng.wait_ge(ur.sem, ur.upto(i, DT_TILES - 1))
                        eng.wait_ge(yad.sem, yad.upto(i, NCH * (p - 1) + c) + jj * (2 * NCH))
                        G.tensor_tensor(
                            hs[:, c, :].rearrange("p (d t) -> p d t", t=T), u[:, 2 * c:2 * c + 2, :],
                            bc[:, p, 0:1, :].to_broadcast([P, 2, T]), ALU.mult).then_inc(inr.sem, 1)

                if mamba:
                    steps(eng, step)
                if attn:
                    rstd(i - 1, ln3, ln3r, TT)
                if mamba:
                    rstd(i, ln2, ln2r, TT)

            iterations(eng, one)

        @block.scalar
        def _(eng):
            lead(eng, xnr, cv0, xcr, ssqd, sstr, spa, spe, ca_f, dar, rop, qrd, krd, vrdy, exd, ptr, ordy,
                 x3r, rqr, rex, zgr, szr, qTr)
            S = nc.scalar
            eng.wait_ge(s_const, 16 * 8)
            S.activation(aneg[:, :, :], aneg[:, :, :], ACT.Exp).then_inc(s_aneg, 1)

            def one(i, mamba, attn):
                blk = i - 1

                def evacuate(to, banks, done, ready, b):
                    for k in range(KE):
                        eng.wait_ge(done.sem, done.upto(b, k))
                        S.activation(to[:, k, :], banks(k), ACT.Copy).then_inc(ready.sem, 1)

                if mamba:
                    evacuate(xnT, lambda k: acc[:, k, :], ln1t, xnr, i)
                    for s in range(DT_TILES):
                        eng.wait_ge(inx.sem, inx.upto(i, s))
                        if s == 0:
                            eng.wait_ge(s_const, 16 * 8)
                        S.activation(xc[:, s, :], bank(s % 4), ACT.Identity, bias=chan[:, 0, s:s + 1],
                                     scale=cw[:, s, KC - 1:KC]).then_inc(cv0.sem, 1)
                        if s >= 1:
                            eng.wait_ge(cv.sem, cv.upto(i, s - 1))
                            S.activation(xc[:, s - 1, :], xc[:, s - 1, :], ACT.Silu).then_inc(xcr.sem, 1)
                    eng.wait_ge(cv.sem, cv.upto(i, DT_TILES - 1))
                    S.activation(xc[:, DT_TILES - 1, :], xc[:, DT_TILES - 1, :], ACT.Silu).then_inc(xcr.sem, 1)
                    eng.wait_ge(ssd.sem, ssd.upto(i, 0))
                    S.activation(ssq, acc[:, 0, 0:TT * SSM].rearrange("p (t c) -> p t c", c=SSM),
                                 ACT.Square).then_inc(ssqd.sem, 1)
                    eng.wait_ge(sst.sem, sst.upto(i, 0))
                    S.activation(ssmT, acc[0:SSM, 1, :], ACT.Copy).then_inc(sstr.sem, 1)
                    ca = Chain(eng, ca_f, i)
                    for s in range(DT_TILES):
                        q = s % 2
                        eng.wait_ge(dtd.sem, dtd.upto(i, s))
                        if s >= 2:
                            eng.wait_ge(spd.sem, spd.upto(i, s - 2))
                        elif s == 0:
                            eng.wait_ge(ssnd.sem, ssnd.upto(i, 0))
                        ca(S.activation(e_b[:, q, :], bank(s % 4), ACT.Abs, bias=chan[:, 1, s:s + 1]))
                        ca(S.activation(dt[:, s, :], bank(s % 4), ACT.Relu, bias=chan[:, 1, s:s + 1]))
                        ca.wait()
                        S.activation(e_b[:, q, :], e_b[:, q, :], ACT.Exp, scale=-1.0).then_inc(spe.sem, 1)
                        eng.wait_ge(spe.sem, spe.upto(i, s))
                        S.activation(l_b[:, q, :], e_b[:, q, :], ACT.Ln, bias=1.0).then_inc(spa.sem, 1)
                    ca.end()
                if attn:
                    eng.wait_ge(rot.sem, rot.upto(blk, 0))
                    S.activation(cosT[:, :], pq[:, 0, :], ACT.Copy)
                    S.activation(sinT[:, :], pq[:, 1, :], ACT.Copy).then_inc(rop.sem, 1)

                def swap_q(jj, o):
                    eng.wait_ge(qd.sem, qd.upto(blk, o) + jj * 2)
                    eng.wait_ge(qrdy.sem, qrdy.upto(blk, o - 1) + jj * 2)
                    S.activation(qr[0:64, :, :], pq[64:128, :, :], ACT.Copy)
                    S.activation(qr[64:128, :, :], pq[0:64, :, :], ACT.Copy).then_inc(qrd.sem, 1)

                def swap_k(g):
                    eng.wait_ge(kd.sem, kd.upto(blk, 0) + g)
                    eng.wait_ge(krdy.sem, krdy.upto(blk, -1) + g)
                    S.activation(kr[0:64, :], pk[64:128, 0, :], ACT.Copy)
                    S.activation(kr[64:128, :], pk[0:64, 0, :], ACT.Copy).then_inc(krd.sem, 1)

                def evac_v(g):
                    eng.wait_ge(vd.sem, vd.upto(blk, 0) + g)
                    eng.wait_ge(pvd.sem, pvd.upto(blk, -1) + g * 2)
                    S.activation(vt[:, :, :], pk[:, 1, :].rearrange("p (t d) -> p t d", d=D),
                                 ACT.Copy).then_inc(vrdy.sem, 1)

                def exps(jj, o):
                    eng.wait_ge(ssb.sem, ssb.upto(blk, o) + jj * 2)
                    S.activation(pr[:, :, :], pr[:, :, :], ACT.Exp).then_inc(exd.sem, 1)

                def evac_pt(jj, p):
                    eng.wait_ge(ptd.sem, ptd.upto(blk, p) + jj * 2)
                    eng.wait_ge(pvd.sem, pvd.upto(blk, p - 1) + jj * 2)
                    for b in range(2):
                        ins = S.activation(pz[b * 64:(b + 1) * 64, :, b, :],
                                           pq[b * 64:(b + 1) * 64, 1, :].rearrange("p (t r) -> p t r", r=P),
                                           ACT.Copy)
                    ins.then_inc(ptr.sem, 1)

                def evac_o(jj, p):
                    eng.wait_ge(pvd.sem, pvd.upto(blk, p) + jj * 2)
                    eng.wait_ge(wod.sem, wod.upto(blk, p - 1) + jj * 2)
                    o_ps = pk[:, :, :].rearrange("p c (x h q) -> p (c x) h q", h=2, q=SEQ)
                    for h in range(2):
                        ins = S.activation(oT[:, h, :].rearrange("p (x q) -> p x q", q=SEQ), o_ps[:, :, h, :],
                                           ACT.Copy)
                    ins.then_inc(ordy.sem, 1)

                def decay(jj, p, c):
                    if c == 0 and p == 0:
                        eng.wait_ge(ur.sem, ur.upto(i, DT_TILES - 1))
                    eng.wait_ge(scd.sem, scd.upto(i, NCH * p + c - 2) + jj * (2 * NCH))
                    for d in range(2):
                        s = 2 * c + d
                        to = dA[:, c % 2, d * T:(d + 1) * T].rearrange("p (b t) -> p b t", t=SEQ)
                        ins = S.activation(to[:, :, 1:SEQ],
                                           dt[:, s, :].rearrange("p (b t) -> p b t", t=SEQ)[:, :, 1:SEQ],
                                           ACT.Exp, scale=aneg[:, s, bass.ds(jj * 2 + p, 1)])
                    ins.then_inc(dar.sem, 1)

                def step(jj, p, tail):
                    last = tail and p == 1
                    if mamba:
                        decay(jj, p, 0)
                    if attn:
                        evac_pt(jj, p)
                    if mamba:
                        decay(jj, p, 1)
                    if attn:
                        evac_o(jj, p)
                        if not last:
                            exps(jj, p + 1)
                    if mamba:
                        decay(jj, p, 2)
                    if attn and not tail:
                        swap_q(jj, p + 2)
                        if p == 0:
                            swap_k(jj + 1)
                        else:
                            evac_v(jj + 1)
                    if mamba:
                        decay(jj, p, 3)

                if attn:
                    if mamba:
                        eng.wait_ge(s_bcw, i * 16 + 16)
                    swap_k(0)
                    evac_v(0)
                    eng.wait_ge(pxd.sem, pxd.upto(blk, 0))
                    swap_q(0, 0)
                    exps(0, 0)
                    swap_q(0, 1)
                steps(eng, step)
                if attn:
                    evacuate(x3T, bank, ln3t, x3r, blk)
                    eng.wait_ge(rqd.sem, rqd.upto(blk, 0))
                    S.activation(rq, pq[0:RD, 0, :], ACT.Copy).then_inc(rqr.sem, 1)
                    eng.wait_ge(rmd.sem, rmd.upto(blk, 0))
                    for t in range(TT):
                        ins = S.activation(gex[:, t, :], pq[:, 1, t * EXPERTS:(t + 1) * EXPERTS], ACT.Exp,
                                           bias=negm[:, t:t + 1])
                    ins.then_inc(rex.sem, 1)
                    evacuate(zgT, bank, zgt, zgr, blk)
                if mamba:
                    for s in range(DT_TILES):
                        eng.wait_ge(inz.sem, inz.upto(i, s))
                        if s >= 2:
                            eng.wait_ge(yr.sem, yr.upto(i, s - 2))
                        S.activation(sz[:, s % 2, :], bank(s % 4), ACT.Silu).then_inc(szr.sem, 1)
                    evacuate(qT, lambda k: acc[:, k, :], ln2t, qTr, i)

            iterations(eng, one)

        @block.vector
        def _(eng):
            lead(eng, ln1, ln1n, cv, ssv, ssnd, spd, ur, ch_f, scd, hcd, yad, pxd, pid, qt1, qt2, kt1, kt2, qrdy,
                 krdy, srd, smk, smx, ssb, sum_, rcp, prdy, x2r, ln3, ln3n, rmd, zgd, outr, ch_a, yr, x1r,
                 ln2, ln2n, ch_m)
            V = nc.vector
            eng.wait_ge(s_init, 4)
            eng.wait_ge(s_aneg, 1)
            V.tensor_scalar(aneg[:, :, :], aneg[:, :, :], -1.0, None, ALU.mult).then_inc(s_aneg, 1)

            def norm(ch, x, to, b, variance, rstd, done):
                for t in range(TT):
                    ch(V.bn_stats(stats[:, t, :], x[:, t, :]))
                for t in range(TT):
                    ch.wait()
                    hold(eng)
                    ch(V.bn_aggr(mv[:, t, :], stats[:, t, :]))
                ch.wait()
                V.tensor_scalar(ve[:, 0:TT], mv[:, :, 1], LN_EPS, None, ALU.add).then_inc(variance.sem, 1)
                eng.wait_ge(rstd.sem, rstd.upto(b, 0))
                for t in range(TT):
                    V.tensor_scalar(to[:, t, :], x[:, t, :], mv[:, t, 0:1], rs[:, t:t + 1], ALU.subtract,
                                    ALU.mult).then_inc(done.sem, 1)

            def first_phase(i):
                ch = Chain(eng, ch_f, i)
                eng.wait_ge(s_x, i * 16 + 16)
                eng.wait_ge(ln2t.sem, ln2t.upto(i, -1))
                norm(ch, xm, u[:, 0:TT, :], i, ln1, ln1r, ln1n)
                for s in range(DT_TILES):
                    eng.wait_ge(cv0.sem, cv0.upto(i, s))
                    x3 = bank(s % 4).rearrange("p (b t) -> p b t", t=SEQ)
                    y3 = xc[:, s, :].rearrange("p (b t) -> p b t", t=SEQ)
                    for d in range(1, KC):
                        ins = V.scalar_tensor_tensor(
                            out=y3[:, :, d:SEQ], in0=x3[:, :, 0:SEQ - d], scalar=cw[:, s, KC - 1 - d:KC - d],
                            in1=y3[:, :, d:SEQ], op0=ALU.mult, op1=ALU.add)
                        if d < KC - 1:
                            ch(ins)
                            ch.wait()
                    ins.then_inc(cv.sem, 1)
                eng.wait_ge(ssqd.sem, ssqd.upto(i, 0))
                ch(V.tensor_reduce(ss[:, :, 0], ssq[:, :, 0:R], AX.X, ALU.add))
                ch(V.tensor_reduce(ss[:, :, 1:3], ssq[:, :, R:SSM].rearrange("p t (c n) -> p t c n", n=NS), AX.X,
                                   ALU.add))
                ch.wait()
                ve3 = ve[:, 0:3 * TT].rearrange("p (t c) -> p t c", c=3)
                ch(V.tensor_scalar(ve3[:, :, 0], ss[:, :, 0], 1.0 / R, RMS_EPS, ALU.mult, ALU.add))
                V.tensor_scalar(ve3[:, :, 1:3], ss[:, :, 1:3], 1.0 / NS, RMS_EPS, ALU.mult,
                                ALU.add).then_inc(ssv.sem, 1)
                ch.wait()
                eng.wait_ge(ssr.sem, ssr.upto(i, 0))
                rs3 = rs[:, 0:3 * TT].rearrange("p (t c) -> p t c", c=3)
                ps3 = acc[:, 0, 0:TT * SSM].rearrange("p (t c) -> p t c", c=SSM)
                ch(V.tensor_tensor(ssn[:, :, 0:R], ps3[:, :, 0:R], rs3[:, :, 0:1].to_broadcast([P, TT, R]),
                                   ALU.mult))
                for c in range(2):
                    at = R + c * NS
                    ch(V.tensor_tensor(ssn[:, :, at:at + NS], ps3[:, :, at:at + NS],
                                       rs3[:, :, 1 + c:2 + c].to_broadcast([P, TT, NS]), ALU.mult))
                ch.wait()
                V.tensor_tensor(ssn, ssn, lnw[:, :].unsqueeze(1).to_broadcast([P, TT, SSM]),
                                ALU.mult).then_inc(ssnd.sem, 1)
                for s in range(DT_TILES):
                    q = s % 2
                    e, l, v = e_b[:, q, :], l_b[:, q, :], v_b[:, q, :]
                    if s == 0:
                        eng.wait_ge(sst.sem, sst.upto(i, 0))
                    eng.wait_ge(spe.sem, spe.upto(i, s))
                    ch(V.tensor_scalar(v, e, 1.0, 1.0, ALU.add, ALU.subtract))
                    ch.wait()
                    eng.wait_ge(spa.sem, spa.upto(i, s))
                    ch(V.tensor_tensor(e, e, v, ALU.subtract))
                    ch(V.scalar_tensor_tensor(out=l, in0=v, scalar=0.0, in1=l, op0=ALU.is_gt, op1=ALU.mult))
                    ch.wait()
                    ch(V.tensor_tensor(l, l, e, ALU.add))
                    ch.wait()
                    V.tensor_tensor(dt[:, s, :], dt[:, s, :], l, ALU.add).then_inc(spd.sem, 1)
                    eng.wait_ge(spd.sem, spd.upto(i, s))
                    ch(V.tensor_tensor(u[:, s, :], dt[:, s, :], xc[:, s, :], ALU.mult))
                    ch.wait()
                    V.tensor_scalar(xc[:, s, :], xc[:, s, :], chan[:, 2, s:s + 1], None,
                                    ALU.mult).then_inc(ur.sem, 1)
                ch.end()

            def scan(i, jj, p, c):
                at = jj * (2 * NCH)
                h = hs[:, c, :]
                eng.wait_ge(inr.sem, inr.upto(i, NCH * p + c) + at)
                eng.wait_ge(dar.sem, dar.upto(i, NCH * p + c) + at)
                V.tensor_tensor_scan(out=h, data0=dA[:, c % 2, :], data1=h, initial=0.0, op0=ALU.mult,
                                     op1=ALU.add).then_inc(scd.sem, 1)
                eng.wait_ge(scd.sem, scd.upto(i, NCH * p + c) + at)
                h3 = h.rearrange("p (d t) -> p d t", t=T)
                V.tensor_tensor(h3, h3, bc[:, p, 1:2, :].to_broadcast([P, 2, T]), ALU.mult).then_inc(hcd.sem, 1)
                eng.wait_ge(hcd.sem, hcd.upto(i, NCH * p + c) + at)
                V.tensor_tensor(xc[:, 2 * c:2 * c + 2, :], xc[:, 2 * c:2 * c + 2, :], h3,
                                ALU.add).then_inc(yad.sem, 1)

            def attention_of(blk):
                def rope(x_ps, swapped, to, cos, sin, t1, t2, ready, at):
                    V.tensor_tensor(to, x_ps, cos, ALU.mult).then_inc(t1.sem, 1)
                    V.tensor_tensor(swapped, swapped, sin, ALU.mult).then_inc(t2.sem, 1)
                    eng.wait_ge(t1.sem, at(t1))
                    eng.wait_ge(t2.sem, at(t2))
                    V.tensor_tensor(to, to, swapped, ALU.add).then_inc(ready.sem, 1)

                def rope_q(jj, o):
                    eng.wait_ge(qrd.sem, qrd.upto(blk, o) + jj * 2)
                    eng.wait_ge(sd.sem, sd.upto(blk, o - 1) + jj * 2)

                    def seqs(x):
                        return x.rearrange("p h (b q) -> p h b q", q=SEQ)

                    two = [P, 2, T]
                    rope(seqs(pq[:, :, :]), seqs(qr[:, :, :]), qp[:, :, :].rearrange("p b (h q) -> p h b q", h=2),
                         seqs(cosT[:, :].unsqueeze(1).to_broadcast(two)),
                         seqs(sinT[:, :].unsqueeze(1).to_broadcast(two)), qt1, qt2, qrdy,
                         lambda s: s.upto(blk, o) + jj * 2)

                def rope_k(g):
                    eng.wait_ge(krd.sem, krd.upto(blk, 0) + g)
                    eng.wait_ge(sd.sem, sd.upto(blk, -1) + g * 2)
                    rope(pk[:, 0, :], kr[:, :], kT[:, :], cosT[:, :], sinT[:, :], kt1, kt2, krdy,
                         lambda s: s.upto(blk, 0) + g)

                def softmax_in(jj, o):
                    def at(s):
                        return s.upto(blk, o) + jj * 2
                    eng.wait_ge(sd.sem, at(sd))
                    eng.wait_ge(ptd.sem, ptd.upto(blk, o - 1) + jj * 2)
                    V.tensor_tensor(pr[:, :, :], pq[:, 0, :].rearrange("p (b k) -> p b k", k=SEQ), mmul[:, :, :],
                                    ALU.mult).then_inc(srd.sem, 1)
                    eng.wait_ge(srd.sem, at(srd))
                    V.tensor_tensor(pr[:, :, :], pr[:, :, :], madd[:, :, :], ALU.add).then_inc(smk.sem, 1)
                    eng.wait_ge(smk.sem, at(smk))
                    V.tensor_reduce(mx[:, :], pr[:, :, :], AX.X, ALU.max).then_inc(smx.sem, 1)
                    eng.wait_ge(smx.sem, at(smx))
                    V.tensor_tensor(pr[:, :, :], pr[:, :, :], mx[:, :].unsqueeze(2).to_broadcast([P, NB, SEQ]),
                                    ALU.subtract).then_inc(ssb.sem, 1)

                def softmax_out(jj, o):
                    def at(s):
                        return s.upto(blk, o) + jj * 2
                    eng.wait_ge(exd.sem, at(exd))
                    V.tensor_reduce(sm[:, :], pr[:, :, :], AX.X, ALU.add).then_inc(sum_.sem, 1)
                    eng.wait_ge(sum_.sem, at(sum_))
                    V.reciprocal(sm[:, :], sm[:, :]).then_inc(rcp.sem, 1)
                    eng.wait_ge(rcp.sem, at(rcp))
                    V.tensor_tensor(pr[:, :, :], pr[:, :, :], sm[:, :].unsqueeze(2).to_broadcast([P, NB, SEQ]),
                                    ALU.mult).then_inc(prdy.sem, 1)

                return rope_q, rope_k, softmax_in, softmax_out

            def one(i, mamba, attn):
                blk = i - 1
                rope_q, rope_k, softmax_in, softmax_out = attention_of(blk)
                if attn:
                    ca = Chain(eng, ch_a, blk)
                    eng.wait_ge(s_pos, blk * 16 + 16)
                    ca(V.tensor_scalar(posf[:, 0, :], posi[:, :], 0.0, float(MAXPOS), ALU.is_lt, ALU.mult))
                    ca.wait()
                    ca(V.tensor_tensor(posf[:, 1, :], posi[:, :], posf[:, 0, :], ALU.add))
                    ca.wait()
                    if mamba:
                        V.tensor_scalar(posu[:, :], posf[:, 1, :], 0.0, float(MAXPOS - 1), ALU.max, ALU.min)
                    else:
                        V.tensor_scalar(posu[:, :], posf[:, 1, :], 0.0, float(MAXPOS - 1), ALU.max, ALU.min)
                if mamba:
                    first_phase(i)
                if attn:
                    V.tensor_copy(posf[:, 0, :], mv[:, :, 0]).then_inc(pid.sem, 1)
                    eng.wait_ge(s_mask, blk * 32 + 32)
                    V.tensor_scalar(mmul[:, :, :], mraw, 0.0, float(D) ** -0.5, ALU.not_equal, ALU.mult)
                    V.tensor_scalar(madd[:, :, :], mraw, 0.0, -1.0e9, ALU.is_equal, ALU.mult).then_inc(pxd.sem, 1)
                    eng.wait_ge(pxd.sem, pxd.upto(blk, 0))
                    eng.wait_ge(rop.sem, rop.upto(blk, 0))
                    rope_k(0)
                    rope_q(0, 0)
                    softmax_in(0, 0)
                    softmax_out(0, 0)
                    rope_q(0, 1)

                def step(jj, p, tail):
                    last = tail and p == 1
                    if mamba:
                        scan(i, jj, p, 0)
                    if attn and not last:
                        softmax_in(jj, p + 1)
                    if mamba:
                        scan(i, jj, p, 1)
                    if attn and not last:
                        softmax_out(jj, p + 1)
                    if mamba:
                        scan(i, jj, p, 2)
                    if attn and not tail:
                        rope_q(jj, p + 2)
                        if p == 0:
                            rope_k(jj + 1)
                    if mamba:
                        scan(i, jj, p, 3)

                steps(eng, step)
                if attn:
                    for t in range(TT):
                        if t == 0:
                            eng.wait_ge(wod.sem, wod.upto(blk, PAIRS - 1))
                        V.tensor_tensor(xa[:, t, :], xa[:, t, :], acc[:, t, :], ALU.add).then_inc(x2r.sem, 1)
                    eng.wait_ge(x2r.sem, x2r.upto(blk, TT - 1))
                    norm(ca, xa, xn, blk, ln3, ln3r, ln3n)
                    eng.wait_ge(rsd.sem, rsd.upto(blk, 0))
                    hold(eng)
                    for t in range(TT):
                        sc = pq[:, 1, t * EXPERTS:(t + 1) * EXPERTS]
                        ca(V.max(top[:, t, 0:8], sc))
                        ca.wait()
                        hold(eng)
                        ca(V.match_replace(rsc[:, t, :], top[:, t, 0:8], sc, NEG))
                        ca.wait()
                        hold(eng)
                        ca(V.max(top[:, t, 8:16], rsc[:, t, :]))
                        ca.wait()
                        hold(eng)
                        ca(V.match_replace(rsc[:, t, :], top[:, t, 8:16], rsc[:, t, :], NEG))
                    ca.wait()
                    V.tensor_scalar(negm[:, :], top[:, :, 0], -1.0, None, ALU.mult).then_inc(rmd.sem, 1)
                    eng.wait_ge(rex.sem, rex.upto(blk, 0))
                    for t in range(TT):
                        ca(V.scalar_tensor_tensor(out=gate[:, t, :], in0=rsc[:, t, :], scalar=NEG,
                                                  in1=gex[:, t, :], op0=ALU.is_equal, op1=ALU.mult))
                    ca.wait()
                    ca(V.tensor_reduce(gs[:, :], gate, AX.X, ALU.add))
                    ca.wait()
                    ca(V.reciprocal(gs[:, :], gs[:, :]))
                    ca.wait()
                    for t in range(TT):
                        ca(V.tensor_scalar(gate[:, t, :], gate[:, t, :], gs[:, t:t + 1], SCALING, ALU.mult,
                                           ALU.mult))
                    ca.wait()
                    for t in range(TT):
                        eng.wait_ge(awd.sem, awd.upto(blk, t))
                        V.tensor_tensor(zg[:, t, :].rearrange("p (e r) -> p e r", r=RANK),
                                        acc[:, t, :].rearrange("p (e r) -> p e r", r=RANK),
                                        gate[:, t, :].unsqueeze(2).to_broadcast([P, EXPERTS, RANK]),
                                        ALU.mult).then_inc(zgd.sem, 1)
                    for t in range(TT):
                        eng.wait_ge(bwd.sem, bwd.upto(blk, t))
                        ins = V.tensor_tensor(xn[:, t, :], xa[:, t, :], acc[:, t, :], ALU.add)
                    ins.then_inc(outr.sem, 1)
                    ca.end()
                if mamba:
                    cm = Chain(eng, ch_m, i)
                    for s in range(DT_TILES):
                        eng.wait_ge(szr.sem, szr.upto(i, s))
                        V.tensor_tensor(xc[:, s, :], xc[:, s, :], sz[:, s % 2, :], ALU.mult).then_inc(yr.sem, 1)
                    for t in range(TT):
                        eng.wait_ge(opd.sem, opd.upto(i, t))
                        V.tensor_tensor(xa[:, t, :], xm[:, t, :], acc[:, t, :], ALU.add).then_inc(x1r.sem, 1)
                    eng.wait_ge(x1r.sem, x1r.upto(i, TT - 1))
                    norm(cm, xa, u[:, 0:TT, :], i, ln2, ln2r, ln2n)
                    cm.end()

            iterations(eng, one)

        @block.tensor
        def _(eng):
            lead(eng, ln1t, inx, ssd, sst, dtd, rot, ac0, qd, kd, vd, sd, ptd, pvd, wod, ln3t, rqd, rsd, awd, zgt,
                 bwd, inz, opd, ln2t, wad, wbd)
            M = nc.tensor
            eng.wait_ge(s_ident, 2)
            eng.wait_ge(s_init, 4)
            eng.wait_ge(s_const, 16 * 8)

            def one(i, mamba, attn):
                blk = i - 1
                at_q, at_a, at_z = wa_first(mamba, attn)
                at_b, at_o = wb_first(mamba, attn)

                def turn(x, banks, normed, done, b):
                    for k in range(KE):
                        for t in range(TT):
                            if k == 0:
                                eng.wait_ge(normed.sem, normed.upto(b, t))
                            ins = M.transpose(banks(k)[:, t * P:(t + 1) * P], x[:, t, k * P:(k + 1) * P],
                                              ident[:, :])
                        ins.then_inc(done.sem, 1)

                def use_wa(at):
                    eng.wait_ge(s_wa[at % 2], (wa_half(i) + (at // 2 + 1)) * 16)

                def use_wb(at):
                    eng.wait_ge(s_wb[at % 2], (wb_half(i) + (at // 2 + 1)) * 16)

                def wa4(p):
                    return wa[:, p, :].rearrange("p (k c) -> p k c", k=KE)

                def wb2(p):
                    return wb[:, p, :].rearrange("p (h c) -> p h c", h=2)

                if mamba:
                    eng.wait_ge(qTr.sem, qTr.upto(i, -1))
                    turn(u[:, 0:TT, :], lambda k: acc[:, k, :], ln1n, ln1t, i)
                    for s in range(DT_TILES):
                        if s == 0:
                            eng.wait_ge(xnr.sem, xnr.upto(i, KE - 1))
                        if s % 2 == 0:
                            use_wa(s // 2)
                        if s >= 4:
                            eng.wait_ge(cv.sem, cv.upto(i, s - 4))
                        for k in range(KE):
                            ins = M.matmul(bank(s % 4), wa4((s // 2) % 2)[:, k, (s % 2) * P:(s % 2 + 1) * P],
                                           xnT[:, k, :], start=(k == 0), stop=(k == KE - 1))
                        ins.then_inc(inx.sem, 1)
                        if s % 2 == 1:
                            eng.wait_ge(inx.sem, inx.upto(i, s))
                            eng.sem_inc(wad, 1)
                    eng.wait_ge(xcr.sem, xcr.upto(i, DT_TILES - 1))
                    for t in range(TT):
                        for s in range(DT_TILES):
                            ins = M.matmul(acc[:, 0, t * SSM:(t + 1) * SSM], xc[:, s, t * P:(t + 1) * P],
                                           xpw[:, s, :], start=(s == 0), stop=(s == DT_TILES - 1))
                    ins.then_inc(ssd.sem, 1)
                    eng.wait_ge(ssnd.sem, ssnd.upto(i, 0))
                    hold(eng)
                    for t in range(TT):
                        ins = M.transpose(acc[0:SSM, 1, t * P:(t + 1) * P], ssn[:, t, :], ident[:, :])
                    ins.then_inc(sst.sem, 1)
                    eng.wait_ge(sstr.sem, sstr.upto(i, 0))
                    for s in range(DT_TILES):
                        if s >= 4:
                            eng.wait_ge(spa.sem, spa.upto(i, s - 4))
                        M.matmul(bank(s % 4), dtw[:, s * P:(s + 1) * P], ssmT[0:R, :], start=True,
                                 stop=True).then_inc(dtd.sem, 1)

                def project_q(jj, o):
                    p = o % 2
                    eng.wait_ge(s_wa[p], (wa_half(i) + ((at_q + o) // 2 + 1) + jj) * 16)
                    for h in range(2):
                        for k in range(KE):
                            ins = M.matmul(pq[:, h, :], wa4(p)[:, k, h * P:(h + 1) * P], qT[:, k, :],
                                           start=(k == 0), stop=(k == KE - 1))
                    ins.then_inc(qd.sem, 1)

                def free_wa(jj, o):
                    eng.wait_ge(qd.sem, qd.upto(blk, o) + jj * 2)
                    eng.sem_inc(wad, 1)

                def project_k(g):
                    eng.wait_ge(s_wk, blk * (16 * KVH) + g * 16 + 16)
                    for k in range(KE):
                        ins = M.matmul(pk[:, 0, :], wk[:, k, :], ctxT[:, k, :], start=(k == 0),
                                       stop=(k == KE - 1))
                    ins.then_inc(kd.sem, 1)

                def project_v(g):
                    eng.wait_ge(s_wv, blk * (16 * KVH) + g * 16 + 16)
                    for t in range(TT):
                        for k in range(KE):
                            ins = M.matmul(pk[:, 1, t * D:(t + 1) * D], ctxT[:, k, t * P:(t + 1) * P],
                                           wv[:, k, :], start=(k == 0), stop=(k == KE - 1))
                    ins.then_inc(vd.sem, 1)

                def scores(jj, o):
                    eng.wait_ge(qrdy.sem, qrdy.upto(blk, o) + jj * 2)
                    eng.wait_ge(krdy.sem, krdy.upto(blk, o // 2) + jj)
                    for b in range(NB):
                        ins = M.matmul(pq[:, 0, b * SEQ:(b + 1) * SEQ], qp[:, b, :],
                                       kT[:, b * SEQ:(b + 1) * SEQ], start=True, stop=True)
                    ins.then_inc(sd.sem, 1)

                def turn_probs(jj, p, last):
                    eng.wait_ge(prdy.sem, prdy.upto(blk, p) + jj * 2)
                    if not last:
                        eng.wait_ge(qrdy.sem, qrdy.upto(blk, p + 1) + jj * 2)
                    flat = pr[:, :, :].rearrange("p b k -> p (b k)")
                    for t in range(TT):
                        ins = M.transpose(pq[:, 1, t * P:(t + 1) * P], flat[:, t * P:(t + 1) * P], ident[:, :])
                    ins.then_inc(ptd.sem, 1)

                def values(jj, p):
                    eng.wait_ge(ptr.sem, ptr.upto(blk, p) + jj * 2)
                    eng.wait_ge(vrdy.sem, vrdy.upto(blk, 0) + jj)
                    for t in range(TT):
                        ins = M.matmul(pk[:, t // 2, (t % 2) * 2 * P:(t % 2 + 1) * 2 * P], vt[:, t, :],
                                       pz[:, t, :, :], start=True, stop=True)
                    ins.then_inc(pvd.sem, 1)

                def project_o(jj, p, stop):
                    eng.wait_ge(ordy.sem, ordy.upto(blk, p) + jj * 2)
                    eng.wait_ge(s_wb[p], (wb_half(i) + (jj + 1)) * 16)
                    for t in range(TT):
                        for h in range(2):
                            ins = M.matmul(acc[:, t, :], oT[:, h, t * P:(t + 1) * P], wb2(p)[:, h, :],
                                           start=False, stop=(stop and h == 1))
                    ins.then_inc(wod.sem, 1)
                    eng.wait_ge(wod.sem, wod.upto(blk, p) + jj * 2)
                    eng.sem_inc(wbd, 1)

                def step(jj, p, tail):
                    last = tail and p == 1
                    turn_probs(jj, p, last)
                    if not last:
                        scores(jj, p + 1)
                    values(jj, p)
                    if not tail:
                        eng.wait_ge(srd.sem, srd.upto(blk, p + 1) + jj * 2)
                        project_q(jj, p + 2)
                        eng.wait_ge(ordy.sem, ordy.upto(blk, p) + jj * 2)
                        free_wa(jj, p + 2)
                        if p == 0:
                            project_k(jj + 1)
                        else:
                            project_v(jj + 1)
                    project_o(jj, p, last)

                if attn:
                    eng.wait_ge(s_tab, blk * (16 * TT) + 16 * TT)
                    for c in range(2):
                        for t in range(TT):
                            ins = M.transpose(pq[:, c, t * P:(t + 1) * P], tab[:, t, c * D:(c + 1) * D],
                                              ident[:, :])
                    ins.then_inc(rot.sem, 1)
                    eng.wait_ge(qTr.sem, qTr.upto(blk, KE - 1))
                    for t in range(TT):
                        M.matmul(acc[:, t, :], zeros[:, 0:P], zeros[:, :], start=True, stop=False)
                    eng.wait_ge(s_ctx, blk * 16 + 16)
                    project_k(0)
                    project_v(0)
                    eng.wait_ge(rop.sem, rop.upto(blk, 0))
                    project_q(0, 0)
                    free_wa(0, 0)
                    scores(0, 0)
                    eng.wait_ge(srd.sem, srd.upto(blk, 0))
                    project_q(0, 1)
                    free_wa(0, 1)
                    steps(eng, step)
                    turn(xn, bank, ln3n, ln3t, blk)
                    eng.wait_ge(x3r.sem, x3r.upto(blk, KE - 1))
                    for k in range(KE):
                        ins = M.matmul(pq[0:RD, 0, :], rqw[:, k, :], x3T[:, k, :], start=(k == 0),
                                       stop=(k == KE - 1))
                    ins.then_inc(rqd.sem, 1)
                    for k in range(KE):
                        if k % 2 == 0:
                            use_wa(at_a + k // 2)
                        for t in range(TT):
                            ins = M.matmul(acc[:, t, :], x3T[:, k, t * P:(t + 1) * P],
                                           wb2_of_wa(k // 2)[:, k % 2, :], start=(k == 0), stop=(k == KE - 1))
                            if k == KE - 1:
                                ins.then_inc(awd.sem, 1)
                        if k == 1:
                            eng.drain().then_inc(wad, 1)
                        if k == 0:
                            eng.wait_ge(rqr.sem, rqr.upto(blk, 0))
                            for t in range(TT):
                                ins = M.matmul(pq[:, 1, t * EXPERTS:(t + 1) * EXPERTS], rq[:, t * P:(t + 1) * P],
                                               rkw[:, :], start=True, stop=True)
                            ins.then_inc(rsd.sem, 1)
                    eng.wait_ge(awd.sem, awd.upto(blk, TT - 1))
                    eng.sem_inc(wad, 1)
                    eng.wait_ge(rex.sem, rex.upto(blk, 0))
                    turn(zg, bank, zgd, zgt, blk)
                    for k in range(KE):
                        eng.wait_ge(zgr.sem, zgr.upto(blk, k))
                        if k % 2 == 0:
                            use_wb(at_b + k // 2)
                        for t in range(TT):
                            ins = M.matmul(acc[:, t, :], zgT[:, k, t * P:(t + 1) * P], wb2(k // 2)[:, k % 2, :],
                                           start=(k == 0), stop=(k == KE - 1))
                            if k == KE - 1:
                                ins.then_inc(bwd.sem, 1)
                        if k % 2 == 1:
                            eng.drain().then_inc(wbd, 1)
                if mamba:
                    for s in range(DT_TILES):
                        if s % 2 == 0:
                            use_wa(at_z + s // 2)
                        if s >= 4:
                            eng.wait_ge(szr.sem, szr.upto(i, s - 4))
                        for k in range(KE):
                            ins = M.matmul(bank(s % 4), wa4((s // 2) % 2)[:, k, (s % 2) * P:(s % 2 + 1) * P],
                                           xnT[:, k, :], start=(k == 0), stop=(k == KE - 1))
                        ins.then_inc(inz.sem, 1)
                        if s % 2 == 1:
                            eng.wait_ge(inz.sem, inz.upto(i, s))
                            eng.sem_inc(wad, 1)
                    if attn:
                        eng.wait_ge(outr.sem, outr.upto(blk, 0))
                    for s in range(DT_TILES):
                        eng.wait_ge(yr.sem, yr.upto(i, s))
                        if s % 2 == 0:
                            use_wb(at_o + s // 2)
                        for t in range(TT):
                            ins = M.matmul(acc[:, t, :], xc[:, s, t * P:(t + 1) * P], wb2((s // 2) % 2)[:, s % 2, :],
                                           start=(s == 0), stop=(s == DT_TILES - 1))
                            if s == DT_TILES - 1:
                                ins.then_inc(opd.sem, 1)
                        if s % 2 == 1:
                            eng.drain().then_inc(wbd, 1)
                    eng.wait_ge(x1r.sem, x1r.upto(i, TT - 1))
                    turn(u[:, 0:TT, :], lambda k: acc[:, k, :], ln2n, ln2t, i)

            def wb2_of_wa(p):
                return wa[:, p, :].rearrange("p (h c) -> p h c", h=2)

            iterations(eng, one)


_KC = np.ascontiguousarray


def _tables():
    inv = (np.float32(1.0) / np.float32(THETA) ** (np.arange(0, D, 2, dtype=np.float32) / np.float32(D))).astype(
        np.float32)
    f = np.arange(MAXPOS, dtype=np.float32)[:, None] * inv[None, :]
    c, s = np.cos(f), np.sin(f)
    return np.concatenate([c, c, -s, s], axis=1).astype(np.float32)


def kernel(**inputs):
    import concourse.bacc as _bacc
    from concourse.bass_utils import run_bass_kernel_spmd as _run

    w = {k: np.asarray(v) for k, v in inputs.items()}

    def cols(m, width):
        return _KC(m.reshape(KE, P, -1, width).transpose(2, 1, 0, 3))

    def rows2(m):
        return _KC(m.reshape(-1, 2, P, E).transpose(0, 2, 1, 3))

    inw = w["L0_attn_in_proj_w"]
    arrays = {
        "x": _KC(w["x"].reshape(NBLK, TT, P, E).transpose(0, 2, 1, 3)),
        "ctx": _KC(w["ctx_4096"].reshape(NBLK, T, KE, P).transpose(0, 3, 2, 1)),
        "pos": _KC(w["pos_BxS2"].reshape(NBLK, TT, P).transpose(0, 2, 1)),
        "mask": _KC(w["mask_BxSxS2_ik0"].reshape(NBLK, NB, SEQ, SEQ).transpose(0, 2, 1, 3)),
        "wx": cols(inw[:, :DIN], 2 * P), "wz": cols(inw[:, DIN:], 2 * P),
        "wq": cols(w["L0_xattn_Wq"], 2 * P), "wk": cols(w["L0_xattn_Wk"], D), "wv": cols(w["L0_xattn_Wv"], D),
        "wo": rows2(w["L0_xattn_Wo"]), "ow": rows2(w["L0_attn_out_proj_w"].T),
        "aw": rows2(w["L0_ffn_A_w"].T), "bw": rows2(w["L0_ffn_B_w"].T),
        "xpw": _KC(w["L0_attn_x_proj_w"].T.reshape(DT_TILES, P, SSM).transpose(1, 0, 2)),
        "dtw": _KC(w["L0_attn_dt_proj_w"].T),
        "rqw": _KC(w["L0_ffn_Wq_w"].T.reshape(KE, P, RD).transpose(1, 0, 2)),
        "rkw": _KC(w["L0_ffn_keys"].T),
        "lnw": _KC(np.broadcast_to(np.concatenate(
            [w["L0_attn_dt_ln_w"], w["L0_attn_B_ln_w"], w["L0_attn_C_ln_w"]])[None, :], (P, SSM))),
        "cw": _KC(w["L0_attn_conv_w"].reshape(DT_TILES, P, KC).transpose(1, 0, 2)),
        "chan": _KC(np.stack([w["L0_attn_conv_b"], w["L0_attn_dt_bias"], w["L0_attn_D_param"]]).reshape(
            3, DT_TILES, P).transpose(2, 0, 1)),
        "alog": _KC(w["L0_attn_A_log"].reshape(DT_TILES, P, NS).transpose(1, 0, 2)),
        "rotary": _tables(),
    }
    nc = _bacc.Bacc("TRN2", target_bir_lowering=False, num_devices=1)
    aps = {}
    for name, arr in arrays.items():
        aps[name] = nc.dram_tensor(f"in_{name}", arr.shape, mybir.dt.from_np(arr.dtype), kind="ExternalInput").ap()
    for name in ("wx", "wz", "wq", "wo", "ow", "aw", "bw"):
        aps[name] = aps[name].rearrange("n p k c -> n p (k c)")
    out = nc.dram_tensor("out", (NBLK, TT, P, E), F32, kind="ExternalOutput").ap()
    build(nc, aps, out.rearrange("b t p e -> b p t e"))
    r = _run(nc, [{f"in_{k}": v for k, v in arrays.items()}], core_ids=[0])
    return r.results[0]["out"].reshape(BATCH, SEQ, E)
```

```python
from contextlib import ExitStack

import numpy as np

import concourse.bass as bass
from concourse import mybir

F32 = mybir.dt.float32
I32 = mybir.dt.int32
U32 = mybir.dt.uint32
BF16 = mybir.dt.bfloat16
ALU = mybir.AluOpType
ACT = mybir.ActivationFunctionType
AX = mybir.AxisListType

P = 128
BATCH, SEQ, E = 32, 64, 512
NTOK = BATCH * SEQ
T = 512
NBLK = NTOK // T
TT = T // P
NB = T // SEQ
KE = E // P
DIN, NS, KC, R = 1024, 16, 4, 32
DT_TILES = DIN // P
SSM = R + 2 * NS
HEADS, KVH, D = 32, 8, 128
PAIRS = HEADS // 2
MAXPOS, THETA = 512, 10000.0
EXPERTS, RANK, TOPK, RD = 64, 8, 16, 16
SCALING = 32 / TOPK
LN_EPS, RMS_EPS = 1e-5, 1e-6
NCH = 4
CW = 2 * T
NEG = -3.0e38
MASKED = -1.0e9
LEAD = 8


class Stage:

    def __init__(self, nc, ctx, name, per):
        self.sem = ctx.enter_context(nc.semaphore(name))
        self.per = per

    def upto(self, block, index):
        return block * self.per + (index + 1 + LEAD)


class Chain:

    def __init__(self, eng, stage, block):
        self.eng, self.stage, self.block, self.n = eng, stage, block, 0

    def __call__(self, ins):
        ins.then_inc(self.stage.sem, 1)
        self.n += 1

    def wait(self):
        self.eng.wait_ge(self.stage.sem, self.stage.upto(self.block, self.n - 1))

    def end(self):
        assert self.n == self.stage.per, (self.n, self.stage.per)


def build(nc, a, out):
    ctx = ExitStack()
    with ctx:
        def sb(name, shape, dt=F32):
            return ctx.enter_context(nc.sbuf_tensor(name, shape, dt))

        def pb(name, shape):
            return ctx.enter_context(nc.psum_tensor(name, shape, F32))

        def sem(name):
            return ctx.enter_context(nc.semaphore(name))

        scr = nc.dram_tensor("bc_rows", (NBLK, 2, NS, T), F32, kind="Internal").ap()

        xm = sb("xm", [P, TT, E])
        xr = sb("xr", [P, TT, E])
        xa = sb("xa", [P, TT, E])
        xnT = sb("xnT", [P, KE, T])
        qT = sb("qT", [P, KE, T])
        ctxT = sb("ctxT", [P, KE, T])
        xc = sb("xc", [P, DT_TILES, T])
        dt = sb("dt", [P, DT_TILES, T])
        u = sb("u", [P, DT_TILES, T])
        bc = sb("bc", [P, 2, 2, T])
        dA = sb("dA", [P, 2, CW])
        hs = sb("hs", [P, NCH, CW])
        wa = sb("wa", [P, 2, KE * 2 * P])
        wb = sb("wb", [P, 2, 2 * E])
        wk = sb("wk", [P, KE, D])
        wv = sb("wv", [P, KE, D])
        qp = sb("qp", [P, NB, 2 * SEQ])
        qr = sb("qr", [P, 2, T])
        kT = sb("kT", [P, T])
        kr = sb("kr", [P, T])
        vt = sb("vt", [P, TT, D])
        pr = sb("pr", [P, NB, SEQ])
        pz = sb("pz", [P, TT, 2, P])
        oT = sb("oT", [P, 2, T])
        cosT = sb("cosT", [P, T])
        sinT = sb("sinT", [P, T])
        mask = sb("mask", [P, NB, SEQ], I32)
        sc = sb("sc", [P, NB, SEQ])
        ssmT = sb("ssmT", [SSM, T])
        ssq = sb("ssq", [P, TT, SSM])
        ssn = sb("ssn", [P, TT, SSM])
        ident = sb("ident", [P, P])
        zeros = sb("zeros", [P, 512], BF16)
        xpw = sb("xpw", [P, DT_TILES, SSM])
        dtw = sb("dtw", [R, DIN])
        rqw = sb("rqw", [P, KE, RD])
        rkw = sb("rkw", [RD, EXPERTS])
        lnw = sb("lnw", [P, SSM])
        cw = sb("cw", [P, DT_TILES, KC])
        chan = sb("chan", [P, 3, DT_TILES])
        aneg = sb("aneg", [P, DT_TILES, NS])
        posi = sb("posi", [P, TT], I32)
        posf = sb("posf", [P, 2, TT])
        posu = sb("posu", [P, TT], U32)
        stats = sb("stats", [P, TT, 6])
        mv = sb("mv", [P, TT, 2])
        ve = sb("ve", [P, 16])
        rs = sb("rs", [P, 16])
        mhalf = sb("mhalf", [P, 16])
        ss = sb("ss", [P, TT, 3])
        mx = sb("mx", [P, NB])
        sm = sb("sm", [P, NB])
        top = sb("top", [P, TT, 16])
        negm = sb("negm", [P, TT])
        gs = sb("gs", [P, TT])
        xn = dt[:, 0:TT, :]
        h2 = hs[:, :, :].rearrange("p c w -> p (c w)").rearrange("p (t e) -> p t e", e=E)
        xn1, xn2 = h2[:, 0:TT, :], h2[:, TT:2 * TT, :]
        qp2 = qp[:, :, :].rearrange("p b c -> p (b c)").rearrange("p (h t) -> p h t", h=2)
        x3T = u[:, 0:KE, :]
        zgT = u[:, KE:2 * KE, :]
        zg = dt[:, TT:2 * TT, :]
        rq = kr[0:RD, :]
        rsc = pr[:, :, :].rearrange("p b k -> p (b k)")[:, 0:TT * EXPERTS].rearrange("p (t e) -> p t e", e=EXPERTS)
        gate = pr[:, :, :].rearrange("p b k -> p (b k)")[:, TT * EXPERTS:2 * TT * EXPERTS].rearrange(
            "p (t e) -> p t e", e=EXPERTS)
        gex = kT[:, 0:TT * EXPERTS].rearrange("p (t e) -> p t e", e=EXPERTS)
        tab = oT[:, :, :].rearrange("p h t -> p (h t)").rearrange("p (t c) -> p t c", c=2 * D)
        sz = qp2

        acc = pb("acc", [P, TT, 512])
        pq = pb("pq", [P, 2, 512])
        pk = pb("pk", [P, 2, 512])

        def bank(n):
            return pq[:, n, :] if n < 2 else pk[:, n - 2, :]

        def stage(name, per):
            return Stage(nc, ctx, name, per)

        s_const = sem("const_loaded")
        s_x = sem("x_loaded")
        s_xr = sem("xr_loaded")
        s_xa = sem("xa_copied")
        s_ctx = sem("ctx_loaded")
        s_mask = sem("mask_loaded")
        s_pos = sem("pos_loaded")
        s_tab = sem("rotary_rows_loaded")
        s_bcw = sem("bc_rows_stored")
        s_bc = [sem(f"bc_loaded{p}") for p in range(2)]
        s_wa = [sem(f"wa_loaded{p}") for p in range(2)]
        s_wb = [sem(f"wb_loaded{p}") for p in range(2)]
        s_wk = sem("wk_loaded")
        s_wv = sem("wv_loaded")
        s_out = sem("out_stored")
        s_ident = sem("ident_made")
        s_init = sem("buffers_cleared")
        s_aneg = sem("decay_rates_made")
        ln1 = stage("ln1_variance", 1)
        ln1r = stage("ln1_rstd", 1)
        ln1n = stage("ln1_done", TT)
        ln1t = stage("ln1_transposed", KE)
        xnr = stage("xnT_ready", KE)
        inx = stage("in_proj_x", DT_TILES)
        cv0 = stage("conv_tap_last", DT_TILES)
        cv = stage("conv_done", DT_TILES)
        xcr = stage("xc_ready", DT_TILES)
        ssd = stage("ssm_done", 1)
        ssqd = stage("ssm_squared", 1)
        ssv = stage("ssm_mean_square", 1)
        ssr = stage("ssm_rms", 1)
        ssnd = stage("ssm_normalised", 1)
        sst = stage("ssm_transposed", 1)
        sstr = stage("ssmT_ready", 1)
        dtd = stage("dt_proj", DT_TILES)
        dtv = stage("dt_read", DT_TILES)
        spe = stage("softplus_exp", NCH)
        spl = stage("softplus_ln", NCH)
        spd = stage("softplus_done", NCH)
        ur = stage("u_ready", NCH)
        ch_n = stage("dve_ln1", 2 * TT)
        ch_c = stage("dve_conv", (KC - 2) * DT_TILES)
        ch_f = stage("dve_ssm_softplus", 6 + 5 * NCH)
        dar = stage("decay_ready", NS * NCH)
        inr = stage("scan_input_ready", NS * NCH)
        scd = stage("scan_done", NS * NCH)
        hcd = stage("state_times_c", NS * NCH)
        yad = stage("y_added", NS * NCH)
        pid = stage("pos_index_ready", 1)
        rot = stage("rotary_transposed", 1)
        rop = stage("rotary_ready", 1)
        ac0 = stage("acc_cleared", 1)
        qd = stage("q_done", PAIRS)
        kd = stage("k_done", KVH)
        vd = stage("v_done", KVH)
        qrd = stage("q_swapped", PAIRS)
        krd = stage("k_swapped", KVH)
        qt1 = stage("q_times_cos", PAIRS)
        qt2 = stage("q_times_sin", PAIRS)
        kt1 = stage("k_times_cos", KVH)
        kt2 = stage("k_times_sin", KVH)
        qrdy = stage("q_ready", PAIRS)
        krdy = stage("k_ready", KVH)
        vrdy = stage("v_ready", KVH)
        sd = stage("scores_done", PAIRS)
        srd = stage("scores_read", PAIRS)
        scf = stage("scores_prefilled", PAIRS)
        smx = stage("scores_max", PAIRS)
        exd = stage("exp_done", PAIRS)
        sum_ = stage("exp_summed", PAIRS)
        rcp = stage("sum_inverted", PAIRS)
        prdy = stage("probs_ready", PAIRS)
        ptd = stage("probs_transposed", PAIRS)
        ptr = stage("probsT_ready", PAIRS)
        pvd = stage("pv_done", PAIRS)
        ordy = stage("o_ready", PAIRS)
        wod = stage("wo_done", PAIRS)
        x2r = stage("x2_ready", TT)
        ln3 = stage("ln3_variance", 1)
        ln3r = stage("ln3_rstd", 1)
        ln3n = stage("ln3_done", TT)
        ln3t = stage("ln3_transposed", KE)
        x3r = stage("x3T_ready", KE)
        rqd = stage("router_q", 1)
        rqr = stage("router_q_ready", 1)
        rsd = stage("router_scores", 1)
        rmd = stage("router_max", 1)
        rex = stage("router_exp", 1)
        awd = stage("a_proj", TT)
        zgd = stage("z_gated", TT)
        zgt = stage("z_transposed", KE)
        zgr = stage("zT_ready", KE)
        bwd = stage("b_proj", TT)
        outr = stage("out_ready", 1)
        ch_p = stage("dve_positions", 2)
        ch_a = stage("dve_mixture", 2 + 8 * TT)
        inz = stage("in_proj_z", DT_TILES)
        szr = stage("silu_z", DT_TILES)
        yr = stage("y_gated", DT_TILES)
        opd = stage("out_proj", TT)
        x1r = stage("x1_ready", TT)
        ln2 = stage("ln2_variance", 1)
        ln2r = stage("ln2_rstd", 1)
        ln2n = stage("ln2_done", TT)
        ln2t = stage("ln2_transposed", KE)
        qTr = stage("qT_ready", KE)
        ch_m = stage("dve_x1_norm", 2 * TT)
        wad = sem("wa_used")
        wbd = sem("wb_used")
        W_DT, W_KE = DT_TILES // 2, KE // 2

        def wa_base(i):
            if isinstance(i, int) and i == 0:
                return W_DT
            full = PAIRS + 2 * W_DT + W_KE
            return (i - 1) * full + (3 * W_DT - (W_DT if isinstance(i, int) and i == NBLK else 0))

        def wb_base(i):
            return 0 if isinstance(i, int) and i == 0 else (i - 1) * (PAIRS + W_DT + W_KE) + W_DT

        def wa_half(i):
            if isinstance(i, int):
                return wa_base(i) // 2
            return (i - 1) * ((PAIRS + 2 * W_DT + W_KE) // 2) + 3 * W_DT // 2

        def wb_half(i):
            return wb_base(i) // 2 if isinstance(i, int) else (i - 1) * ((PAIRS + W_DT + W_KE) // 2) + W_DT // 2

        def wa_places(mamba, attn):
            at_z = PAIRS if attn else 0
            at_a = at_z + (W_DT if mamba else 0)
            return at_z, at_a, at_a + (W_KE if attn else 0)

        def wb_places(mamba, attn):
            at_o = PAIRS if attn else 0
            return at_o, at_o + (W_DT if mamba else 0)

        block = ctx.enter_context(nc.Block())

        s_hold = sem("held_on_its_own")

        def hold(eng):
            eng.sem_inc(s_hold, 1)

        def lead(eng, *stages):
            for s in stages:
                eng.sem_inc(s.sem if isinstance(s, Stage) else s, LEAD)

        def iterations(eng, one):
            one(0, True, False, True)
            with eng.Fori(1, NBLK - 1) as i:
                one(i, True, True, True)
            one(NBLK - 1, True, True, False)
            one(NBLK, False, True, False)

        def steps(eng, one):
            with eng.Fori(0, NS // 2 - 1) as jj:
                one(jj, 0, False)
                one(jj, 1, False)
            one(NS // 2 - 1, 0, True)
            one(NS // 2 - 1, 1, True)

        @block.sync
        def _(eng):
            consts = [(xpw, a["xpw"]), (dtw, a["dtw"]), (rqw, a["rqw"]), (rkw, a["rkw"]), (lnw, a["lnw"]),
                      (cw, a["cw"]), (chan, a["chan"]), (aneg, a["alog"])]

            def load_wa(i, at, src):
                eng.wait_ge(wad, wa_base(i) + at + (LEAD - 1))
                eng.dma_start(wa[:, at % 2, :], src).then_inc(s_wa[at % 2], 16)

            def load_wa_j(i, at, jj, p, src):
                eng.wait_ge(wad, wa_base(i) + jj * 2 + (at + p + LEAD - 1))
                eng.dma_start(wa[:, p, :], src).then_inc(s_wa[p], 16)

            def load_wb(i, at, src):
                eng.wait_ge(wbd, wb_base(i) + at + (LEAD - 1))
                eng.dma_start(wb[:, at % 2, :], src).then_inc(s_wb[at % 2], 16)

            def load_wb_j(i, jj, o, src):
                eng.wait_ge(wbd, wb_base(i) + jj * 2 + (o + LEAD - 1))
                eng.dma_start(wb[:, o % 2, :], src).then_inc(s_wb[o % 2], 16)

            lead(eng, s_out)
            eng.dma_start(xm[:, :, :], a["x"][0]).then_inc(s_x, 16)
            for n in range(W_DT):
                if n >= 2:
                    eng.wait_ge(wad, LEAD + n - 1)
                eng.dma_start(wa[:, n % 2, :], a["wx"][n]).then_inc(s_wa[n % 2], 16)
                if n == 0:
                    for dst, src in consts:
                        eng.dma_start(dst[...], src).then_inc(s_const, 16)

            def one(i, mamba, attn, nxt):
                at_z, at_a, at_x = wa_places(mamba, attn)
                at_o, at_b = wb_places(mamba, attn)
                blk = i - 1
                if attn:
                    eng.wait_ge(vd.sem, vd.upto(blk, -1))
                    eng.dma_start(ctxT[:, :, :], a["ctx"][blk]).then_inc(s_ctx, 16)
                    eng.dma_start(wk[:, :, :], a["wk"][0]).then_inc(s_wk, 16)
                    eng.dma_start(wv[:, :, :], a["wv"][0]).then_inc(s_wv, 16)
                    eng.dma_start(posi[:, :], a["pos"][blk]).then_inc(s_pos, 16)
                    eng.wait_ge(srd.sem, srd.upto(blk, -1))
                    for h in range(2):
                        eng.dma_start(mask[h * SEQ:(h + 1) * SEQ, :, :], a["mask"][blk]).then_inc(s_mask, 16)
                    for n in range(2):
                        load_wa(i, n, a["wq"][n])
                    load_wb(i, 0, a["wo"][0])
                if mamba:
                    eng.wait_ge(sstr.sem, sstr.upto(i, 0))
                    eng.dma_start(scr[i].rearrange("c n t -> (c n) t"), ssmT[R:SSM, :]).then_inc(s_bcw, 16)
                    eng.wait_ge(s_bcw, i * 16 + 16)
                    for n in range(2):
                        eng.wait_ge(hcd.sem, hcd.upto(i, -1))
                        eng.dma_start(bc[:, n, :, :], scr[i, :, n, :].partition_broadcast(P)).then_inc(s_bc[n], 16)
                if mamba:
                    if attn:
                        eng.wait_ge(ln2n.sem, ln2n.upto(blk, TT - 1))
                        hold(eng)
                        if not isinstance(i, int) or i > 1:
                            eng.wait_ge(outr.sem, outr.upto(blk, -1))
                        eng.dma_start(xa[:, :, :], xr[:, :, :]).then_inc(s_xa, 16)
                        eng.wait_ge(s_xa, blk * 16 + 16)
                    eng.dma_start(xr[:, :, :], a["x"][i]).then_inc(s_xr, 16)
                elif attn:
                    eng.wait_ge(ln2n.sem, ln2n.upto(blk, TT - 1))
                    eng.wait_ge(outr.sem, outr.upto(blk, -1))
                    eng.dma_start(xa[:, :, :], xr[:, :, :]).then_inc(s_xa, 16)
                if nxt:
                    eng.wait_ge(ln1n.sem, ln1n.upto(i, TT - 1))
                    eng.dma_start(xm[:, :, :], a["x"][i + 1]).then_inc(s_x, 16)

                def step(jj, p, tail):
                    if attn:
                        if not tail:
                            load_wa_j(i, 2, jj, p, a["wq"][jj * 2 + (2 + p)])
                            if p == 0:
                                eng.wait_ge(kd.sem, kd.upto(blk, jj))
                                eng.dma_start(wk[:, :, :], a["wk"][jj + 1]).then_inc(s_wk, 16)
                            else:
                                eng.wait_ge(vd.sem, vd.upto(blk, jj))
                                eng.dma_start(wv[:, :, :], a["wv"][jj + 1]).then_inc(s_wv, 16)
                    if attn and not (tail and p == 1):
                        load_wb_j(i, jj, p + 1, a["wo"][jj * 2 + (1 + p)])
                    if mamba and not tail:
                        eng.wait_ge(hcd.sem, hcd.upto(i, NCH * (p + 1) - 1) + jj * (2 * NCH))
                        eng.dma_start(bc[:, p, :, :], scr[i, :, jj * 2 + (2 + p), :].partition_broadcast(P)).then_inc(
                            s_bc[p], 16)

                steps(eng, step)
                if mamba:
                    for n in range(2):
                        load_wa(i, at_z + n, a["wz"][n])
                    for n in range(2):
                        load_wb(i, at_o + n, a["ow"][n])
                    for n in range(2, W_DT):
                        load_wa(i, at_z + n, a["wz"][n])
                if attn:
                    for n in range(W_KE):
                        load_wa(i, at_a + n, a["aw"][n])
                if mamba:
                    for n in range(2, W_DT):
                        load_wb(i, at_o + n, a["ow"][n])
                if attn:
                    for n in range(W_KE):
                        load_wb(i, at_b + n, a["bw"][n])
                if nxt:
                    for n in range(W_DT):
                        load_wa(i, at_x + n, a["wx"][n])
                if attn:
                    eng.wait_ge(outr.sem, outr.upto(blk, 0))
                    eng.dma_start(out[blk], xn).then_inc(s_out, 16)

            iterations(eng, one)
            eng.wait_ge(s_out, 16 * NBLK + LEAD)

        @block.gpsimd
        def _(eng):
            lead(eng, ln1r, ssr, ln2r, ln3r, inr)
            G = nc.gpsimd
            G.memset(ident[:, :], 0.0).then_inc(s_ident, 1)
            eng.wait_ge(s_ident, 1)
            G.affine_select(out=ident[:, :], in_=ident[:, :], compare_op=ALU.not_equal, fill=1.0, base=0,
                            pattern=[[-1, P]], channel_multiplier=1).then_inc(s_ident, 1)
            G.memset(mhalf[:, :], -0.5).then_inc(s_init, 1)
            G.memset(dA[:, :, :], 0.0).then_inc(s_init, 1)
            G.memset(pz[:, :, :, :], 0.0).then_inc(s_init, 1)
            G.memset(zeros[:, :].bitcast(F32), 0.0).then_inc(s_init, 1)
            eng.wait_ge(s_init, 4)

            def rstd(blk, variance, done, n):
                eng.wait_ge(variance.sem, variance.upto(blk, 0))
                G.tensor_tensor(rs[:, 0:n], ve[:, 0:n], mhalf[:, 0:n], ALU.pow).then_inc(done.sem, 1)

            rstd(0, ln1, ln1r, TT)

            def one(i, mamba, attn, nxt):
                if attn:
                    eng.wait_ge(pid.sem, pid.upto(i - 1, 0))
                    hold(eng)
                    for t in range(TT):
                        eng.indirect_dma_start(
                            out=tab[:, t, :], out_offset=None, in_=a["rotary"],
                            in_offset=bass.IndirectOffsetOnAxis(ap=posu[:, t:t + 1], axis=0)).then_inc(s_tab, 16)
                if mamba:
                    rstd(i, ssv, ssr, 3 * TT)

                def step(jj, p, tail):
                    if not mamba:
                        return
                    for c in range(NCH):
                        if c == 0:
                            eng.wait_ge(s_bc[p], i * (8 * NS) + jj * 16 + 16)
                        if c == 0 and p == 0:
                            eng.wait_ge(ur.sem, ur.upto(i, NCH - 1))
                        eng.wait_ge(yad.sem, yad.upto(i, NCH * (p - 1) + c) + jj * (2 * NCH))
                        G.tensor_tensor(
                            hs[:, c, :].rearrange("p (d t) -> p d t", t=T), u[:, 2 * c:2 * c + 2, :],
                            bc[:, p, 0:1, :].to_broadcast([P, 2, T]), ALU.mult).then_inc(inr.sem, 1)

                if mamba:
                    steps(eng, step)
                if attn:
                    rstd(i - 1, ln3, ln3r, TT)
                if nxt:
                    rstd(i + 1, ln1, ln1r, TT)
                if mamba:
                    rstd(i, ln2, ln2r, TT)

            iterations(eng, one)

        @block.scalar
        def _(eng):
            lead(eng, xnr, cv0, xcr, ssqd, sstr, dtv, spe, spl, dar, rop, qrd, krd, vrdy, scf, exd, ptr, ordy,
                 x3r, rqr, rex, zgr, szr, qTr)
            S = nc.scalar
            eng.wait_ge(s_const, 16 * 8)
            S.activation(aneg[:, :, :], aneg[:, :, :], ACT.Exp).then_inc(s_aneg, 1)

            def evacuate(to, banks, done, ready, b):
                for k in range(KE):
                    eng.wait_ge(done.sem, done.upto(b, k))
                    S.activation(to[:, k, :], banks(k), ACT.Copy).then_inc(ready.sem, 1)

            def convolve(b):
                for s in range(DT_TILES + 1):
                    if s < DT_TILES:
                        eng.wait_ge(inx.sem, inx.upto(b, s))
                        S.activation(xc[:, s, :], acc[:, s % 4, :], ACT.Identity, bias=chan[:, 0, s:s + 1],
                                     scale=cw[:, s, KC - 1:KC]).then_inc(cv0.sem, 1)
                    if s >= 1:
                        eng.wait_ge(cv.sem, cv.upto(b, s - 1))
                        S.activation(xc[:, s - 1, :], xc[:, s - 1, :], ACT.Silu).then_inc(xcr.sem, 1)

            evacuate(xnT, bank, ln1t, xnr, 0)
            convolve(0)

            def one(i, mamba, attn, nxt):
                blk = i - 1

                def swap_q(jj, o):
                    eng.wait_ge(qd.sem, qd.upto(blk, o) + jj * 2)
                    eng.wait_ge(qrdy.sem, qrdy.upto(blk, o - 1) + jj * 2)
                    S.activation(qr[0:64, :, :], pq[64:128, :, :], ACT.Copy)
                    S.activation(qr[64:128, :, :], pq[0:64, :, :], ACT.Copy).then_inc(qrd.sem, 1)

                def swap_k(g):
                    eng.wait_ge(kd.sem, kd.upto(blk, 0) + g)
                    eng.wait_ge(krdy.sem, krdy.upto(blk, -1) + g)
                    S.activation(kr[0:64, :], pk[64:128, 0, :], ACT.Copy, scale=float(D) ** -0.5)
                    S.activation(kr[64:128, :], pk[0:64, 0, :], ACT.Copy,
                                 scale=float(D) ** -0.5).then_inc(krd.sem, 1)

                def evac_v(g):
                    eng.wait_ge(vd.sem, vd.upto(blk, 0) + g)
                    eng.wait_ge(pvd.sem, pvd.upto(blk, -1) + g * 2)
                    S.activation(vt[:, :, :], pk[:, 1, :].rearrange("p (t d) -> p t d", d=D),
                                 ACT.Copy).then_inc(vrdy.sem, 1)

                def prefill(jj, o):
                    eng.wait_ge(exd.sem, exd.upto(blk, o - 1) + jj * 2)
                    S.activation(sc[:, :, :], zeros[:, :].rearrange("p (b k) -> p b k", k=SEQ), ACT.Copy,
                                 bias=MASKED).then_inc(scf.sem, 1)

                def exps(jj, o):
                    eng.wait_ge(smx.sem, smx.upto(blk, o) + jj * 2)
                    for b in range(NB):
                        ins = S.activation(pr[:, b, :], sc[:, b, :], ACT.Exp, bias=mx[:, b:b + 1])
                    ins.then_inc(exd.sem, 1)

                def evac_pt(jj, p):
                    eng.wait_ge(ptd.sem, ptd.upto(blk, p) + jj * 2)
                    eng.wait_ge(pvd.sem, pvd.upto(blk, p - 1) + jj * 2)
                    for b in range(2):
                        ins = S.activation(pz[b * 64:(b + 1) * 64, :, b, :],
                                           pk[b * 64:(b + 1) * 64, p, :].rearrange("p (t r) -> p t r", r=P),
                                           ACT.Copy)
                    ins.then_inc(ptr.sem, 1)

                def evac_o(jj, p):
                    eng.wait_ge(pvd.sem, pvd.upto(blk, p) + jj * 2)
                    eng.wait_ge(wod.sem, wod.upto(blk, p - 1) + jj * 2)
                    o_ps = pk[:, :, :].rearrange("p c (x h q) -> p (c x) h q", h=2, q=SEQ)
                    for h in range(2):
                        ins = S.activation(oT[:, h, :].rearrange("p (x q) -> p x q", q=SEQ), o_ps[:, :, h, :],
                                           ACT.Copy)
                    ins.then_inc(ordy.sem, 1)

                def decay(jj, p, c):
                    if c == 0 and p == 0:
                        eng.wait_ge(ur.sem, ur.upto(i, NCH - 1))
                    eng.wait_ge(scd.sem, scd.upto(i, NCH * p + c - 2) + jj * (2 * NCH))
                    for d in range(2):
                        s = 2 * c + d
                        to = dA[:, c % 2, d * T:(d + 1) * T].rearrange("p (b t) -> p b t", t=SEQ)
                        ins = S.activation(to[:, :, 1:SEQ],
                                           dt[:, s, :].rearrange("p (b t) -> p b t", t=SEQ)[:, :, 1:SEQ],
                                           ACT.Exp, scale=aneg[:, s, bass.ds(jj * 2 + p, 1)])
                    ins.then_inc(dar.sem, 1)

                def step(jj, p, tail):
                    last = tail and p == 1
                    if mamba:
                        decay(jj, p, 0)
                    if attn:
                        evac_pt(jj, p)
                    if mamba:
                        decay(jj, p, 1)
                    if attn and not last:
                        exps(jj, p + 1)
                    if mamba:
                        decay(jj, p, 2)
                    if attn:
                        evac_o(jj, p)
                    if attn and not tail:
                        swap_q(jj, p + 2)
                        if p == 0:
                            swap_k(jj + 1)
                        else:
                            evac_v(jj + 1)
                        prefill(jj, p + 2)
                    if mamba:
                        decay(jj, p, 3)

                if attn:
                    prefill(0, 0)
                if mamba:
                    eng.wait_ge(ssd.sem, ssd.upto(i, 0))
                    S.activation(ssq[:, :, :], acc[:, 0, 0:TT * SSM].rearrange("p (t c) -> p t c", c=SSM),
                                 ACT.Square).then_inc(ssqd.sem, 1)
                if attn:
                    eng.wait_ge(rot.sem, rot.upto(blk, 0))
                    S.activation(cosT[:, :], pq[:, 0, :], ACT.Copy)
                    S.activation(sinT[:, :], pq[:, 1, :], ACT.Copy).then_inc(rop.sem, 1)
                    swap_k(0)
                    evac_v(0)
                    swap_q(0, 0)
                if mamba:
                    eng.wait_ge(sst.sem, sst.upto(i, 0))
                    S.activation(ssmT[:, :], acc[0:SSM, 1, :], ACT.Copy).then_inc(sstr.sem, 1)
                    for s in range(DT_TILES):
                        eng.wait_ge(dtd.sem, dtd.upto(i, s))
                        S.activation(u[:, s, :], acc[:, s % 4, :], ACT.Abs, bias=chan[:, 1, s:s + 1])
                        if s == 0 and attn and (not isinstance(i, int) or i > 1):
                            eng.wait_ge(s_out, blk * 16 + LEAD)
                        S.activation(dt[:, s, :], acc[:, s % 4, :], ACT.Relu,
                                     bias=chan[:, 1, s:s + 1]).then_inc(dtv.sem, 1)
                if attn:
                    exps(0, 0)
                    swap_q(0, 1)
                    prefill(0, 1)
                if mamba:
                    eng.wait_ge(dtv.sem, dtv.upto(i, DT_TILES - 1))
                    for c in range(NCH):
                        S.activation(u[:, 2 * c:2 * c + 2, :], u[:, 2 * c:2 * c + 2, :], ACT.Exp,
                                     scale=-1.0).then_inc(spe.sem, 1)
                    for c in range(NCH):
                        eng.wait_ge(spe.sem, spe.upto(i, c))
                        if c >= 2:
                            eng.wait_ge(spd.sem, spd.upto(i, c - 2))
                        S.activation(hs[:, c % 2, :], u[:, 2 * c:2 * c + 2, :].rearrange("p d t -> p (d t)"),
                                     ACT.Ln, bias=1.0).then_inc(spl.sem, 1)
                steps(eng, step)
                if mamba:
                    for s in range(DT_TILES):
                        eng.wait_ge(inz.sem, inz.upto(i, s))
                        if s >= 2:
                            eng.wait_ge(yr.sem, yr.upto(i, s - 2))
                        S.activation(sz[:, s % 2, :], bank(s % 4), ACT.Silu).then_inc(szr.sem, 1)
                if attn:
                    evacuate(x3T, lambda k: acc[:, k, :], ln3t, x3r, blk)
                if nxt:
                    evacuate(xnT, bank, ln1t, xnr, i + 1)
                if attn:
                    eng.wait_ge(rqd.sem, rqd.upto(blk, 0))
                    S.activation(rq, pq[0:RD, 0, :], ACT.Copy).then_inc(rqr.sem, 1)
                    eng.wait_ge(rmd.sem, rmd.upto(blk, 0))
                    for t in range(TT):
                        ins = S.activation(gex[:, t, :], pq[:, 1, t * EXPERTS:(t + 1) * EXPERTS], ACT.Exp,
                                           bias=negm[:, t:t + 1])
                    ins.then_inc(rex.sem, 1)
                if nxt:
                    convolve(i + 1)
                if attn:
                    evacuate(zgT, bank, zgt, zgr, blk)
                if mamba:
                    evacuate(qT, lambda k: acc[:, k, :], ln2t, qTr, i)

            iterations(eng, one)

        @block.vector
        def _(eng):
            lead(eng, ln1, ln1n, cv, ssv, ssnd, spd, ur, ch_n, ch_c, ch_f, scd, hcd, yad, pid, qt1, qt2, kt1, kt2, qrdy,
                 krdy, srd, smx, sum_, rcp, prdy, x2r, ln3, ln3n, rmd, zgd, outr, ch_p, ch_a, yr, x1r,
                 ln2, ln2n, ch_m)
            V = nc.vector
            eng.wait_ge(s_init, 4)
            eng.wait_ge(s_aneg, 1)
            V.tensor_scalar(aneg[:, :, :], aneg[:, :, :], -1.0, None, ALU.mult).then_inc(s_aneg, 1)

            def norm(ch, x, to, b, variance, rstd, done):
                for t in range(TT):
                    ch(V.bn_stats(stats[:, t, :], x[:, t, :]))
                for t in range(TT):
                    ch.wait()
                    hold(eng)
                    ch(V.bn_aggr(mv[:, t, :], stats[:, t, :]))
                ch.wait()
                V.tensor_scalar(ve[:, 0:TT], mv[:, :, 1], LN_EPS, None, ALU.add).then_inc(variance.sem, 1)
                eng.wait_ge(rstd.sem, rstd.upto(b, 0))
                for t in range(TT):
                    V.tensor_scalar(to[:, t, :], x[:, t, :], mv[:, t, 0:1], rs[:, t:t + 1], ALU.subtract,
                                    ALU.mult).then_inc(done.sem, 1)

            def norm_in(b):
                ch = Chain(eng, ch_n, b)
                eng.wait_ge(s_x, b * 16 + 16)
                eng.wait_ge(ln1t.sem, ln1t.upto(b, -1))
                norm(ch, xm, xn1, b, ln1, ln1r, ln1n)
                ch.end()

            def convolve(b):
                ch = Chain(eng, ch_c, b)
                for s in range(DT_TILES):
                    eng.wait_ge(cv0.sem, cv0.upto(b, s))
                    x3 = acc[:, s % 4, :].rearrange("p (b t) -> p b t", t=SEQ)
                    y3 = xc[:, s, :].rearrange("p (b t) -> p b t", t=SEQ)
                    for d in range(1, KC):
                        ins = V.scalar_tensor_tensor(
                            out=y3[:, :, d:SEQ], in0=x3[:, :, 0:SEQ - d], scalar=cw[:, s, KC - 1 - d:KC - d],
                            in1=y3[:, :, d:SEQ], op0=ALU.mult, op1=ALU.add)
                        if d < KC - 1:
                            ch(ins)
                            ch.wait()
                    ins.then_inc(cv.sem, 1)
                ch.end()

            def ssm_rows(i, ch):
                eng.wait_ge(ssqd.sem, ssqd.upto(i, 0))
                ch(V.tensor_reduce(ss[:, :, 0], ssq[:, :, 0:R], AX.X, ALU.add))
                ch(V.tensor_reduce(ss[:, :, 1:3], ssq[:, :, R:SSM].rearrange("p t (c n) -> p t c n", n=NS), AX.X,
                                   ALU.add))
                ch.wait()
                ve3 = ve[:, 0:3 * TT].rearrange("p (t c) -> p t c", c=3)
                ch(V.tensor_scalar(ve3[:, :, 0], ss[:, :, 0], 1.0 / R, RMS_EPS, ALU.mult, ALU.add))
                V.tensor_scalar(ve3[:, :, 1:3], ss[:, :, 1:3], 1.0 / NS, RMS_EPS, ALU.mult,
                                ALU.add).then_inc(ssv.sem, 1)
                ch.wait()
                eng.wait_ge(ssr.sem, ssr.upto(i, 0))
                rs3 = rs[:, 0:3 * TT].rearrange("p (t c) -> p t c", c=3)
                ps3 = acc[:, 0, 0:TT * SSM].rearrange("p (t c) -> p t c", c=SSM)
                ch(V.tensor_tensor(ssn[:, :, 0:R], ps3[:, :, 0:R], rs3[:, :, 0:1].to_broadcast([P, TT, R]),
                                   ALU.mult))
                for c in range(2):
                    at = R + c * NS
                    ch(V.tensor_tensor(ssn[:, :, at:at + NS], ps3[:, :, at:at + NS],
                                       rs3[:, :, 1 + c:2 + c].to_broadcast([P, TT, NS]), ALU.mult))
                ch.wait()
                V.tensor_tensor(ssn[:, :, :], ssn[:, :, :], lnw[:, :].unsqueeze(1).to_broadcast([P, TT, SSM]),
                                ALU.mult).then_inc(ssnd.sem, 1)

            def softplus(i, ch):
                for c in range(NCH):
                    two = slice(2 * c, 2 * c + 2)
                    e, l, v = u[:, two, :], hs[:, c % 2, :].rearrange("p (d t) -> p d t", t=T), \
                        hs[:, 2 + c % 2, :].rearrange("p (d t) -> p d t", t=T)
                    eng.wait_ge(spe.sem, spe.upto(i, c))
                    ch(V.tensor_scalar(v, e, 1.0, 1.0, ALU.add, ALU.subtract))
                    eng.wait_ge(spl.sem, spl.upto(i, c))
                    ch(V.scalar_tensor_tensor(out=l, in0=e, scalar=2.0 ** -24, in1=l, op0=ALU.is_gt,
                                              op1=ALU.mult))
                    ch.wait()
                    ch(V.tensor_tensor(e, e, v, ALU.subtract))
                    ch.wait()
                    ch(V.tensor_tensor(l, l, e, ALU.add))
                    ch.wait()
                    V.tensor_tensor(dt[:, two, :], dt[:, two, :], l, ALU.add).then_inc(spd.sem, 1)
                    eng.wait_ge(spd.sem, spd.upto(i, c))
                    ch(V.tensor_tensor(u[:, two, :], dt[:, two, :], xc[:, two, :], ALU.mult))
                    ch.wait()
                    V.tensor_scalar(xc[:, 2 * c, :], xc[:, 2 * c, :], chan[:, 2, 2 * c:2 * c + 1], None, ALU.mult)
                    V.tensor_scalar(xc[:, 2 * c + 1, :], xc[:, 2 * c + 1, :], chan[:, 2, 2 * c + 1:2 * c + 2], None,
                                    ALU.mult).then_inc(ur.sem, 1)

            def scan(i, jj, p, c):
                at = jj * (2 * NCH)
                h = hs[:, c, :]
                eng.wait_ge(inr.sem, inr.upto(i, NCH * p + c) + at)
                eng.wait_ge(dar.sem, dar.upto(i, NCH * p + c) + at)
                V.tensor_tensor_scan(out=h, data0=dA[:, c % 2, :], data1=h, initial=0.0, op0=ALU.mult,
                                     op1=ALU.add).then_inc(scd.sem, 1)
                eng.wait_ge(scd.sem, scd.upto(i, NCH * p + c) + at)
                h3 = h.rearrange("p (d t) -> p d t", t=T)
                V.tensor_tensor(h3, h3, bc[:, p, 1:2, :].to_broadcast([P, 2, T]), ALU.mult).then_inc(hcd.sem, 1)
                eng.wait_ge(hcd.sem, hcd.upto(i, NCH * p + c) + at)
                V.tensor_tensor(xc[:, 2 * c:2 * c + 2, :], xc[:, 2 * c:2 * c + 2, :], h3,
                                ALU.add).then_inc(yad.sem, 1)

            def attention_of(blk):
                def rope(x_ps, scale, swapped, to, cos, sin, t1, t2, ready, at):
                    if scale is None:
                        V.tensor_tensor(to, x_ps, cos, ALU.mult).then_inc(t1.sem, 1)
                    else:
                        V.scalar_tensor_tensor(out=to, in0=x_ps, scalar=scale, in1=cos, op0=ALU.mult,
                                               op1=ALU.mult).then_inc(t1.sem, 1)
                    V.tensor_tensor(swapped, swapped, sin, ALU.mult).then_inc(t2.sem, 1)
                    eng.wait_ge(t1.sem, at(t1))
                    eng.wait_ge(t2.sem, at(t2))
                    V.tensor_tensor(to, to, swapped, ALU.add).then_inc(ready.sem, 1)

                def rope_q(jj, o):
                    eng.wait_ge(qrd.sem, qrd.upto(blk, o) + jj * 2)
                    eng.wait_ge(sd.sem, sd.upto(blk, o - 1) + jj * 2)

                    def seqs(x):
                        return x.rearrange("p h (b q) -> p h b q", q=SEQ)

                    two = [P, 2, T]
                    rope(seqs(pq[:, :, :]), None, seqs(qr[:, :, :]), qp[:, :, :].rearrange("p b (h q) -> p h b q", h=2),
                         seqs(cosT[:, :].unsqueeze(1).to_broadcast(two)),
                         seqs(sinT[:, :].unsqueeze(1).to_broadcast(two)), qt1, qt2, qrdy,
                         lambda s: s.upto(blk, o) + jj * 2)

                def rope_k(g):
                    eng.wait_ge(krd.sem, krd.upto(blk, 0) + g)
                    eng.wait_ge(sd.sem, sd.upto(blk, -1) + g * 2)
                    rope(pk[:, 0, :], float(D) ** -0.5, kr[:, :], kT[:, :], cosT[:, :], sinT[:, :], kt1, kt2, krdy,
                         lambda s: s.upto(blk, 0) + g)

                def softmax_in(jj, o):
                    def at(s):
                        return s.upto(blk, o) + jj * 2
                    eng.wait_ge(sd.sem, at(sd))
                    eng.wait_ge(scf.sem, at(scf))
                    hold(eng)
                    V.copy_predicated(sc[:, :, :], mask[:, :, :],
                                      pq[:, 0, :].rearrange("p (b k) -> p b k", k=SEQ)).then_inc(srd.sem, 1)
                    eng.wait_ge(srd.sem, at(srd))
                    V.tensor_reduce(mx[:, :], sc[:, :, :], AX.X, ALU.max, negate=True).then_inc(smx.sem, 1)

                def softmax_out(jj, o):
                    def at(s):
                        return s.upto(blk, o) + jj * 2
                    eng.wait_ge(exd.sem, at(exd))
                    V.tensor_reduce(sm[:, :], pr[:, :, :], AX.X, ALU.add).then_inc(sum_.sem, 1)
                    eng.wait_ge(sum_.sem, at(sum_))
                    V.reciprocal(sm[:, :], sm[:, :]).then_inc(rcp.sem, 1)
                    eng.wait_ge(rcp.sem, at(rcp))
                    V.tensor_tensor(pr[:, :, :], pr[:, :, :], sm[:, :].unsqueeze(2).to_broadcast([P, NB, SEQ]),
                                    ALU.mult).then_inc(prdy.sem, 1)

                return rope_q, rope_k, softmax_in, softmax_out

            norm_in(0)
            convolve(0)

            def one(i, mamba, attn, nxt):
                blk = i - 1
                rope_q, rope_k, softmax_in, softmax_out = attention_of(blk)
                if attn:
                    cp = Chain(eng, ch_p, blk)
                    eng.wait_ge(s_pos, blk * 16 + 16)
                    cp(V.tensor_scalar(posf[:, 0, :], posi[:, :], 0.0, float(MAXPOS), ALU.is_lt, ALU.mult))
                    cp.wait()
                    cp(V.tensor_tensor(posf[:, 1, :], posi[:, :], posf[:, 0, :], ALU.add))
                    cp.wait()
                    V.tensor_scalar(posu[:, :], posf[:, 1, :], 0.0, float(MAXPOS - 1), ALU.max,
                                    ALU.min).then_inc(pid.sem, 1)
                    cp.end()
                if mamba:
                    ch = Chain(eng, ch_f, i)
                    ssm_rows(i, ch)
                if attn:
                    eng.wait_ge(s_mask, blk * 32 + 32)
                    eng.wait_ge(rop.sem, rop.upto(blk, 0))
                    rope_k(0)
                    rope_q(0, 0)
                    softmax_in(0, 0)
                    softmax_out(0, 0)
                    rope_q(0, 1)
                if mamba:
                    softplus(i, ch)
                    ch.end()

                def step(jj, p, tail):
                    last = tail and p == 1
                    if mamba:
                        scan(i, jj, p, 0)
                    if attn and not last:
                        softmax_in(jj, p + 1)
                    if mamba:
                        scan(i, jj, p, 1)
                    if attn and not last:
                        softmax_out(jj, p + 1)
                    if mamba:
                        scan(i, jj, p, 2)
                    if attn and not tail:
                        rope_q(jj, p + 2)
                        if p == 0:
                            rope_k(jj + 1)
                    if mamba:
                        scan(i, jj, p, 3)

                steps(eng, step)
                if attn:
                    ca = Chain(eng, ch_a, blk)
                    eng.wait_ge(wod.sem, wod.upto(blk, PAIRS - 1))
                    eng.wait_ge(s_xa, blk * 16 + 16)
                    for t in range(TT):
                        V.tensor_tensor(xa[:, t, :], xa[:, t, :], acc[:, t, :], ALU.add).then_inc(x2r.sem, 1)
                    eng.wait_ge(x2r.sem, x2r.upto(blk, TT - 1))
                    norm(ca, xa, xn, blk, ln3, ln3r, ln3n)
                if nxt:
                    norm_in(i + 1)
                if mamba:
                    for s in range(DT_TILES):
                        eng.wait_ge(szr.sem, szr.upto(i, s))
                        V.tensor_tensor(xc[:, s, :], xc[:, s, :], sz[:, s % 2, :], ALU.mult).then_inc(yr.sem, 1)
                if attn:
                    eng.wait_ge(rsd.sem, rsd.upto(blk, 0))
                    hold(eng)
                    for t in range(TT):
                        raw = pq[:, 1, t * EXPERTS:(t + 1) * EXPERTS]
                        ca(V.max(top[:, t, 0:8], raw))
                        ca.wait()
                        hold(eng)
                        ca(V.match_replace(rsc[:, t, :], top[:, t, 0:8], raw, NEG))
                        ca.wait()
                        hold(eng)
                        ca(V.max(top[:, t, 8:16], rsc[:, t, :]))
                        ca.wait()
                        hold(eng)
                        ca(V.match_replace(rsc[:, t, :], top[:, t, 8:16], rsc[:, t, :], NEG))
                    ca.wait()
                    V.tensor_scalar(negm[:, :], top[:, :, 0], -1.0, None, ALU.mult).then_inc(rmd.sem, 1)
                    eng.wait_ge(rex.sem, rex.upto(blk, 0))
                    for t in range(TT):
                        ca(V.scalar_tensor_tensor(out=gate[:, t, :], in0=rsc[:, t, :], scalar=NEG,
                                                  in1=gex[:, t, :], op0=ALU.is_equal, op1=ALU.mult))
                    ca.wait()
                    ca(V.tensor_reduce(gs[:, :], gate, AX.X, ALU.add))
                    ca.wait()
                    ca(V.reciprocal(gs[:, :], gs[:, :]))
                    ca.wait()
                    for t in range(TT):
                        ca(V.tensor_scalar(gate[:, t, :], gate[:, t, :], gs[:, t:t + 1], SCALING, ALU.mult,
                                           ALU.mult))
                    ca.wait()
                if mamba:
                    cm = Chain(eng, ch_m, i)
                    eng.wait_ge(s_xr, i * 16 + 16)
                    for t in range(TT):
                        eng.wait_ge(opd.sem, opd.upto(i, t))
                        V.tensor_tensor(xr[:, t, :], xr[:, t, :], acc[:, t, :], ALU.add).then_inc(x1r.sem, 1)
                    eng.wait_ge(x1r.sem, x1r.upto(i, TT - 1))
                    norm(cm, xr, xn2, i, ln2, ln2r, ln2n)
                    cm.end()
                if attn:
                    for t in range(TT):
                        eng.wait_ge(awd.sem, awd.upto(blk, t))
                        V.tensor_tensor(zg[:, t, :].rearrange("p (e r) -> p e r", r=RANK),
                                        bank(t).rearrange("p (e r) -> p e r", r=RANK),
                                        gate[:, t, :].unsqueeze(2).to_broadcast([P, EXPERTS, RANK]),
                                        ALU.mult).then_inc(zgd.sem, 1)
                if nxt:
                    convolve(i + 1)
                if attn:
                    for t in range(TT):
                        eng.wait_ge(bwd.sem, bwd.upto(blk, t))
                        ins = V.tensor_tensor(xn[:, t, :], xa[:, t, :], bank(t), ALU.add)
                    ins.then_inc(outr.sem, 1)
                    ca.end()

            iterations(eng, one)

        @block.tensor
        def _(eng):
            lead(eng, ln1t, inx, ssd, sst, dtd, rot, ac0, qd, kd, vd, sd, ptd, pvd, wod, ln3t, rqd, rsd, awd, zgt,
                 bwd, inz, opd, ln2t, wad, wbd)
            M = nc.tensor
            eng.wait_ge(s_ident, 2)
            eng.wait_ge(s_init, 4)
            eng.wait_ge(s_const, 16 * 8)

            def accs(k):
                return acc[:, k, :]

            def turn(x, banks, normed, done, b):
                for k in range(KE):
                    for t in range(TT):
                        if k == 0:
                            eng.wait_ge(normed.sem, normed.upto(b, t))
                        ins = M.transpose(banks(k)[:, t * P:(t + 1) * P], x[:, t, k * P:(k + 1) * P], ident[:, :])
                    ins.then_inc(done.sem, 1)

            def wa4(p):
                return wa[:, p, :].rearrange("p (k c) -> p k c", k=KE)

            def project_in(b, loaded, banks, free, done):
                for s in range(DT_TILES):
                    if s % 2 == 0:
                        loaded(s // 2)
                    free(s)
                    for k in range(KE):
                        ins = M.matmul(banks(s % 4), wa4((s // 2) % 2)[:, k, (s % 2) * P:(s % 2 + 1) * P],
                                       xnT[:, k, :], start=(k == 0), stop=(k == KE - 1))
                    ins.then_inc(done.sem, 1)
                    if s % 2 == 1:
                        eng.wait_ge(done.sem, done.upto(b, s))
                        eng.sem_inc(wad, 1)

            def free_conv(b):
                def free(s):
                    if s >= 4:
                        eng.wait_ge(cv.sem, cv.upto(b, s - 4))
                return free

            turn(xn1, bank, ln1n, ln1t, 0)
            eng.wait_ge(xnr.sem, xnr.upto(0, KE - 1))
            project_in(0, lambda n: eng.wait_ge(s_wa[n % 2], 16 * (n // 2 + 1)), accs, free_conv(0), inx)

            def one(i, mamba, attn, nxt):
                blk = i - 1
                at_z, at_a, at_x = wa_places(mamba, attn)
                at_o, at_b = wb_places(mamba, attn)

                def use_wa(at):
                    eng.wait_ge(s_wa[at % 2], (wa_half(i) + (at // 2 + 1)) * 16)

                def use_wb(at):
                    eng.wait_ge(s_wb[at % 2], (wb_half(i) + (at // 2 + 1)) * 16)

                def wb2(p):
                    return wb[:, p, :].rearrange("p (h c) -> p h c", h=2)

                def project_q(jj, o):
                    p = o % 2
                    eng.wait_ge(s_wa[p], (wa_half(i) + (o // 2 + 1) + jj) * 16)
                    for h in range(2):
                        for k in range(KE):
                            ins = M.matmul(pq[:, h, :], wa4(p)[:, k, h * P:(h + 1) * P], qT[:, k, :],
                                           start=(k == 0), stop=(k == KE - 1))
                    ins.then_inc(qd.sem, 1)

                def free_wa(jj, o):
                    eng.wait_ge(qd.sem, qd.upto(blk, o) + jj * 2)
                    eng.sem_inc(wad, 1)

                def project_k(g):
                    eng.wait_ge(s_wk, blk * (16 * KVH) + g * 16 + 16)
                    for k in range(KE):
                        ins = M.matmul(pk[:, 0, :], wk[:, k, :], ctxT[:, k, :], start=(k == 0),
                                       stop=(k == KE - 1))
                    ins.then_inc(kd.sem, 1)

                def project_v(g):
                    eng.wait_ge(s_wv, blk * (16 * KVH) + g * 16 + 16)
                    for t in range(TT):
                        for k in range(KE):
                            ins = M.matmul(pk[:, 1, t * D:(t + 1) * D], ctxT[:, k, t * P:(t + 1) * P],
                                           wv[:, k, :], start=(k == 0), stop=(k == KE - 1))
                    ins.then_inc(vd.sem, 1)

                def scores(jj, o):
                    eng.wait_ge(qrdy.sem, qrdy.upto(blk, o) + jj * 2)
                    eng.wait_ge(krdy.sem, krdy.upto(blk, o // 2) + jj)
                    for b in range(NB):
                        ins = M.matmul(pq[:, 0, b * SEQ:(b + 1) * SEQ], qp[:, b, :],
                                       kT[:, b * SEQ:(b + 1) * SEQ], start=True, stop=True)
                    ins.then_inc(sd.sem, 1)

                def turn_probs(jj, p, last):
                    eng.wait_ge(prdy.sem, prdy.upto(blk, p) + jj * 2)
                    if last:
                        eng.wait_ge(ordy.sem, ordy.upto(blk, p - 1) + jj * 2)
                    flat = pr[:, :, :].rearrange("p b k -> p (b k)")
                    for t in range(TT):
                        ins = M.transpose(pk[:, p, t * P:(t + 1) * P], flat[:, t * P:(t + 1) * P], ident[:, :])
                    ins.then_inc(ptd.sem, 1)

                def values(jj, p):
                    eng.wait_ge(ptr.sem, ptr.upto(blk, p) + jj * 2)
                    eng.wait_ge(vrdy.sem, vrdy.upto(blk, 0) + jj)
                    for t in range(TT):
                        ins = M.matmul(pk[:, t // 2, (t % 2) * 2 * P:(t % 2 + 1) * 2 * P], vt[:, t, :],
                                       pz[:, t, :, :], start=True, stop=True)
                    ins.then_inc(pvd.sem, 1)

                def project_o(jj, o, half, stop):
                    if half == 0:
                        eng.wait_ge(ordy.sem, ordy.upto(blk, o) + jj * 2)
                        eng.wait_ge(s_wb[o % 2], (wb_half(i) + (o // 2 + 1) + jj) * 16)
                    for t in (2 * half, 2 * half + 1):
                        for h in range(2):
                            ins = M.matmul(acc[:, t, :], oT[:, h, t * P:(t + 1) * P], wb2(o % 2)[:, h, :],
                                           start=False, stop=(stop and h == 1))
                    if half == 1:
                        ins.then_inc(wod.sem, 1)

                def free_wb(jj, o):
                    eng.wait_ge(wod.sem, wod.upto(blk, o) + jj * 2)
                    eng.sem_inc(wbd, 1)

                def step(jj, p, tail, first=False):
                    last = tail and p == 1
                    turn_probs(jj, p, last)
                    if not first:
                        project_o(jj, p - 1, 0, False)
                    if not last:
                        scores(jj, p + 1)
                    if not first:
                        project_o(jj, p - 1, 1, False)
                    values(jj, p)
                    if not first:
                        free_wb(jj, p - 1)
                    if not tail:
                        eng.wait_ge(srd.sem, srd.upto(blk, p + 1) + jj * 2)
                        project_q(jj, p + 2)
                        eng.wait_ge(ordy.sem, ordy.upto(blk, p) + jj * 2)
                        if p == 0:
                            project_k(jj + 1)
                        else:
                            project_v(jj + 1)
                        free_wa(jj, p + 2)
                    if last:
                        project_o(jj, p, 0, True)
                        project_o(jj, p, 1, True)
                        free_wb(jj, p)

                if mamba:
                    eng.wait_ge(qTr.sem, qTr.upto(i, -1))
                    eng.wait_ge(xcr.sem, xcr.upto(i, DT_TILES - 1))
                    for t in range(TT):
                        for s in range(DT_TILES):
                            ins = M.matmul(acc[:, 0, t * SSM:(t + 1) * SSM], xc[:, s, t * P:(t + 1) * P],
                                           xpw[:, s, :], start=(s == 0), stop=(s == DT_TILES - 1))
                    ins.then_inc(ssd.sem, 1)
                if attn:
                    eng.wait_ge(outr.sem, outr.upto(blk, -1))
                    eng.wait_ge(s_tab, blk * (16 * TT) + 16 * TT)
                    hold(eng)
                    for c in range(2):
                        for t in range(TT):
                            ins = M.transpose(pq[:, c, t * P:(t + 1) * P], tab[:, t, c * D:(c + 1) * D],
                                              ident[:, :])
                    ins.then_inc(rot.sem, 1)
                    eng.wait_ge(s_ctx, blk * 16 + 16)
                    project_k(0)
                    project_v(0)
                    eng.wait_ge(rop.sem, rop.upto(blk, 0))
                    eng.wait_ge(qTr.sem, qTr.upto(blk, KE - 1))
                    project_q(0, 0)
                    free_wa(0, 0)
                if mamba:
                    eng.wait_ge(ssnd.sem, ssnd.upto(i, 0))
                    hold(eng)
                    for t in range(TT):
                        ins = M.transpose(acc[0:SSM, 1, t * P:(t + 1) * P], ssn[:, t, :], ident[:, :])
                    ins.then_inc(sst.sem, 1)
                    eng.wait_ge(sstr.sem, sstr.upto(i, 0))
                    for s in range(DT_TILES):
                        if s >= 4:
                            eng.wait_ge(dtv.sem, dtv.upto(i, s - 4))
                        M.matmul(acc[:, s % 4, :], dtw[:, s * P:(s + 1) * P], ssmT[0:R, :], start=True,
                                 stop=True).then_inc(dtd.sem, 1)
                if attn:
                    scores(0, 0)
                    eng.wait_ge(srd.sem, srd.upto(blk, 0))
                    project_q(0, 1)
                    free_wa(0, 1)
                    if mamba:
                        eng.wait_ge(dtv.sem, dtv.upto(i, DT_TILES - 1))
                    for t in range(TT):
                        M.matmul(acc[:, t, :], zeros[:, 0:P], zeros[:, :], start=True, stop=False)
                    step(0, 0, False, first=True)
                    step(0, 1, False)
                    with eng.Fori(1, NS // 2 - 1) as jj:
                        step(jj, 0, False)
                        step(jj, 1, False)
                    step(NS // 2 - 1, 0, True)
                    step(NS // 2 - 1, 1, True)
                if mamba:
                    if attn:
                        eng.wait_ge(ordy.sem, ordy.upto(blk, PAIRS - 1))

                    def free_z(s):
                        if s >= 4:
                            eng.wait_ge(szr.sem, szr.upto(i, s - 4))

                    project_in(i, lambda n: use_wa(at_z + n), bank, free_z, inz)
                if attn:
                    turn(xn, accs, ln3n, ln3t, blk)
                if nxt:
                    if mamba:
                        eng.wait_ge(szr.sem, szr.upto(i, DT_TILES - 1))
                    turn(xn1, bank, ln1n, ln1t, i + 1)
                if attn:
                    if nxt:
                        eng.wait_ge(xnr.sem, xnr.upto(i + 1, KE - 1))
                    elif mamba:
                        eng.wait_ge(szr.sem, szr.upto(i, DT_TILES - 1))
                    eng.wait_ge(x3r.sem, x3r.upto(blk, KE - 1))
                    for k in range(KE):
                        ins = M.matmul(pq[0:RD, 0, :], rqw[:, k, :], x3T[:, k, :], start=(k == 0),
                                       stop=(k == KE - 1))
                    ins.then_inc(rqd.sem, 1)
                    eng.wait_ge(rqr.sem, rqr.upto(blk, 0))
                    for t in range(TT):
                        ins = M.matmul(pq[:, 1, t * EXPERTS:(t + 1) * EXPERTS], rq[:, t * P:(t + 1) * P],
                                       rkw[:, :], start=True, stop=True)
                    ins.then_inc(rsd.sem, 1)
                if mamba:
                    for s in range(DT_TILES):
                        eng.wait_ge(yr.sem, yr.upto(i, s))
                        if s % 2 == 0:
                            use_wb(at_o + s // 2)
                        for t in range(TT):
                            ins = M.matmul(acc[:, t, :], xc[:, s, t * P:(t + 1) * P], wb2((s // 2) % 2)[:, s % 2, :],
                                           start=(s == 0), stop=(s == DT_TILES - 1))
                            if s == DT_TILES - 1:
                                ins.then_inc(opd.sem, 1)
                        if s % 2 == 1:
                            eng.drain().then_inc(wbd, 1)
                if attn:
                    eng.wait_ge(rex.sem, rex.upto(blk, 0))
                    for k in range(KE):
                        if k % 2 == 0:
                            use_wa(at_a + k // 2)
                        for t in range(TT):
                            ins = M.matmul(bank(t), x3T[:, k, t * P:(t + 1) * P],
                                           wb2_of_wa(k // 2)[:, k % 2, :], start=(k == 0), stop=(k == KE - 1))
                            if k == KE - 1:
                                ins.then_inc(awd.sem, 1)
                        if k % 2 == 1:
                            eng.drain().then_inc(wad, 1)
                if nxt:
                    eng.wait_ge(x1r.sem, x1r.upto(i, TT - 1))
                    eng.wait_ge(xnr.sem, xnr.upto(i + 1, KE - 1))
                    project_in(i + 1, lambda n: use_wa(at_x + n), accs, free_conv(i + 1), inx)
                if attn:
                    turn(zg, bank, zgd, zgt, blk)
                    for k in range(KE):
                        eng.wait_ge(zgr.sem, zgr.upto(blk, KE - 1)) if k == 0 else None
                        if k % 2 == 0:
                            use_wb(at_b + k // 2)
                        for t in range(TT):
                            ins = M.matmul(bank(t), zgT[:, k, t * P:(t + 1) * P], wb2(k // 2)[:, k % 2, :],
                                           start=(k == 0), stop=(k == KE - 1))
                            if k == KE - 1:
                                ins.then_inc(bwd.sem, 1)
                        if k % 2 == 1:
                            eng.drain().then_inc(wbd, 1)
                if mamba:
                    if nxt:
                        eng.wait_ge(cv.sem, cv.upto(i + 1, DT_TILES - 1))
                    else:
                        eng.wait_ge(x1r.sem, x1r.upto(i, TT - 1))
                    turn(xn2, accs, ln2n, ln2t, i)

            def wb2_of_wa(p):
                return wa[:, p, :].rearrange("p (h c) -> p h c", h=2)

            iterations(eng, one)


_KC = np.ascontiguousarray


def _tables():
    inv = (np.float32(1.0) / np.float32(THETA) ** (np.arange(0, D, 2, dtype=np.float32) / np.float32(D))).astype(
        np.float32)
    f = np.arange(MAXPOS, dtype=np.float32)[:, None] * inv[None, :]
    c, s = np.cos(f), np.sin(f)
    return np.concatenate([c, c, -s, s], axis=1).astype(np.float32)


def kernel(**inputs):
    import concourse.bacc as _bacc
    from concourse.bass_utils import run_bass_kernel_spmd as _run

    w = {k: np.asarray(v) for k, v in inputs.items()}

    def cols(m, width):
        return _KC(m.reshape(KE, P, -1, width).transpose(2, 1, 0, 3))

    def rows2(m):
        return _KC(m.reshape(-1, 2, P, E).transpose(0, 2, 1, 3))

    inw = w["L0_attn_in_proj_w"]
    arrays = {
        "x": _KC(w["x"].reshape(NBLK, TT, P, E).transpose(0, 2, 1, 3)),
        "ctx": _KC(w["ctx_4096"].reshape(NBLK, T, KE, P).transpose(0, 3, 2, 1)),
        "pos": _KC(w["pos_BxS2"].reshape(NBLK, TT, P).transpose(0, 2, 1)),
        "mask": _KC(w["mask_BxSxS2_ik0"].reshape(NBLK, NB, SEQ, SEQ).transpose(0, 2, 1, 3)),
        "wx": cols(inw[:, :DIN], 2 * P), "wz": cols(inw[:, DIN:], 2 * P),
        "wq": cols(w["L0_xattn_Wq"], 2 * P), "wk": cols(w["L0_xattn_Wk"], D), "wv": cols(w["L0_xattn_Wv"], D),
        "wo": rows2(w["L0_xattn_Wo"]), "ow": rows2(w["L0_attn_out_proj_w"].T),
        "aw": rows2(w["L0_ffn_A_w"].T), "bw": rows2(w["L0_ffn_B_w"].T),
        "xpw": _KC(w["L0_attn_x_proj_w"].T.reshape(DT_TILES, P, SSM).transpose(1, 0, 2)),
        "dtw": _KC(w["L0_attn_dt_proj_w"].T),
        "rqw": _KC(w["L0_ffn_Wq_w"].T.reshape(KE, P, RD).transpose(1, 0, 2)),
        "rkw": _KC(w["L0_ffn_keys"].T),
        "lnw": _KC(np.broadcast_to(np.concatenate(
            [w["L0_attn_dt_ln_w"], w["L0_attn_B_ln_w"], w["L0_attn_C_ln_w"]])[None, :], (P, SSM))),
        "cw": _KC(w["L0_attn_conv_w"].reshape(DT_TILES, P, KC).transpose(1, 0, 2)),
        "chan": _KC(np.stack([w["L0_attn_conv_b"], w["L0_attn_dt_bias"], w["L0_attn_D_param"]]).reshape(
            3, DT_TILES, P).transpose(2, 0, 1)),
        "alog": _KC(w["L0_attn_A_log"].reshape(DT_TILES, P, NS).transpose(1, 0, 2)),
        "rotary": _tables(),
    }
    nc = _bacc.Bacc("TRN2", target_bir_lowering=False, num_devices=1)
    aps = {}
    for name, arr in arrays.items():
        aps[name] = nc.dram_tensor(f"in_{name}", arr.shape, mybir.dt.from_np(arr.dtype), kind="ExternalInput").ap()
    for name in ("wx", "wz", "wq", "wo", "ow", "aw", "bw"):
        aps[name] = aps[name].rearrange("n p k c -> n p (k c)")
    out = nc.dram_tensor("out", (NBLK, TT, P, E), F32, kind="ExternalOutput").ap()
    build(nc, aps, out.rearrange("b t p e -> b p t e"))
    r = _run(nc, [{f"in_{k}": v for k, v in arrays.items()}], core_ids=[0])
    return r.results[0]["out"].reshape(BATCH, SEQ, E)
```

```python
from contextlib import ExitStack

import numpy as np

import concourse.bass as bass
from concourse import mybir

F32 = mybir.dt.float32
I32 = mybir.dt.int32
U32 = mybir.dt.uint32
BF16 = mybir.dt.bfloat16
F32R = mybir.dt.float32r
ALU = mybir.AluOpType
ACT = mybir.ActivationFunctionType
AX = mybir.AxisListType

P = 128
BATCH, SEQ, E = 32, 64, 512
NTOK = BATCH * SEQ
T = 512
NBLK = NTOK // T
TT = T // P
NB = T // SEQ
KE = E // P
DIN, NS, KC, R = 1024, 16, 4, 32
DT_TILES = DIN // P
SSM = R + 2 * NS
HEADS, KVH, D = 32, 8, 128
PAIRS = HEADS // 2
MAXPOS, THETA = 512, 10000.0
EXPERTS, RANK, TOPK, RD = 64, 8, 16, 16
SCALING = 32 / TOPK
LN_EPS, RMS_EPS = 1e-5, 1e-6
NCH = 4
CW = 2 * T
NEG = -3.0e38
MASKED = -1.0e9
PASSES = [(0, 0), (0, 1), (1, 0)]
LEAD = 8


class Stage:

    def __init__(self, nc, ctx, name, per):
        self.sem = ctx.enter_context(nc.semaphore(name))
        self.per = per

    def upto(self, block, index):
        return block * self.per + (index + 1 + LEAD)


class Chain:

    def __init__(self, eng, stage, block):
        self.eng, self.stage, self.block, self.n = eng, stage, block, 0

    def __call__(self, ins):
        ins.then_inc(self.stage.sem, 1)
        self.n += 1

    def wait(self):
        self.eng.wait_ge(self.stage.sem, self.stage.upto(self.block, self.n - 1))

    def end(self):
        assert self.n == self.stage.per, (self.n, self.stage.per)


def build(nc, a, out):
    ctx = ExitStack()
    with ctx:
        start = {}

        def sb(name, shape, dt=F32):
            start[name] = -(-nc.sbuf_base // 32) * 32
            return ctx.enter_context(nc.sbuf_tensor(name, shape, dt))

        def pb(name, shape):
            return ctx.enter_context(nc.psum_tensor(name, shape, F32))

        def sem(name):
            return ctx.enter_context(nc.semaphore(name))

        scr = nc.dram_tensor("bc_rows", (NBLK, 2, NS, T), F32, kind="Internal").ap()

        xm = sb("xm", [P, TT, E])
        xr = sb("xr", [P, TT, E])
        xa = sb("xa", [P, TT, E])
        xnT = sb("xnT", [P, KE, T])
        qT = sb("qT", [P, KE, T])
        ctxT = sb("ctxT", [P, KE, T])
        xc = sb("xc", [P, DT_TILES, T])
        dt = sb("dt", [P, DT_TILES, T])
        u = sb("u", [P, DT_TILES, T])
        sz = sb("sz", [P, KE, T])
        bc = sb("bc", [P, 2, 2, T])
        dA = sb("dA", [P, 2, CW])
        hs = sb("hs", [P, NCH, CW])
        wa = sb("wa", [P, 2, KE * 2 * P])
        wb = sb("wb", [P, 2, 2 * E])
        wk = sb("wk", [P, KE, D])
        wv = sb("wv", [P, KE, D])
        qp = sb("qp", [P, NB, 2 * SEQ])
        qr = sb("qr", [P, 2, T])
        kT = sb("kT", [P, T])
        kr = sb("kr", [P, T])
        vt = sb("vt", [P, TT, D])
        pr = sb("pr", [P, NB, SEQ])
        pz = sb("pz", [P, TT, 2, P])
        oT = sb("oT", [P, 2, T])
        cosT = sb("cosT", [P, T])
        sinT = sb("sinT", [P, T])
        mask = sb("mask", [P, NB, SEQ], I32)
        sc = sb("sc", [P, NB, SEQ])
        ssmT = sb("ssmT", [SSM, T])
        ssq = sb("ssq", [P, TT, SSM])
        ssn = sb("ssn", [P, TT, SSM])
        ident = sb("ident", [P, P])
        zeros = sb("zeros", [P, 512], BF16)
        xpw = sb("xpw", [P, DT_TILES, SSM])
        dtw = sb("dtw", [R, DIN])
        rqw = sb("rqw", [P, KE, RD])
        rkw = sb("rkw", [RD, EXPERTS])
        lnw = sb("lnw", [P, SSM])
        cw = sb("cw", [P, DT_TILES, KC])
        chan = sb("chan", [P, 3, DT_TILES])
        aneg = sb("aneg", [P, DT_TILES, NS])
        posi = sb("posi", [P, TT], I32)
        posf = sb("posf", [P, 2, TT])
        posu = sb("posu", [P, TT], U32)
        stats = sb("stats", [P, TT, 6])
        mv = sb("mv", [P, TT, 2])
        ve = sb("ve", [P, 16])
        rs = sb("rs", [P, 16])
        mhalf = sb("mhalf", [P, 16])
        ss = sb("ss", [P, TT, 3])
        mx = sb("mx", [P, NB])
        sm = sb("sm", [P, NB])
        top = sb("top", [P, TT, 16])
        negm = sb("negm", [P, TT])
        gs = sb("gs", [P, TT])
        xn = dt[:, 0:TT, :]
        h2 = hs[:, :, :].rearrange("p c w -> p (c w)").rearrange("p (t e) -> p t e", e=E)
        xn1, xn2 = h2[:, 0:TT, :], h2[:, TT:2 * TT, :]
        x3T = u[:, 0:KE, :]
        zgT = u[:, KE:2 * KE, :]
        zg = dt[:, TT:2 * TT, :]
        rq = kr[0:RD, :]
        rsc = pr[:, :, :].rearrange("p b k -> p (b k)")[:, 0:TT * EXPERTS].rearrange("p (t e) -> p t e", e=EXPERTS)
        gate = pr[:, :, :].rearrange("p b k -> p (b k)")[:, TT * EXPERTS:2 * TT * EXPERTS].rearrange(
            "p (t e) -> p t e", e=EXPERTS)
        gex = kT[:, 0:TT * EXPERTS].rearrange("p (t e) -> p t e", e=EXPERTS)
        tab = oT[:, :, :].rearrange("p h t -> p (h t)").rearrange("p (t c) -> p t c", c=2 * D)

        def over(name, shape, buffer, word):
            return nc.alloc_sbuf_tensor_at(name, shape, F32R, offset=start[buffer] + 4 * word)

        qT2 = over("qT_hi", [P, KE, T], "xnT", 0), over("qT_lo", [P, KE, T], "sz", 0)
        ctxT2 = over("ctxT_hi", [P, KE, T], "xm", 0), over("ctxT_lo", [P, KE, T], "xc", 0)
        oT2 = over("oT_hi", [P, 2, T], "u", 0), over("oT_lo", [P, 2, T], "dA", CW)
        wk2 = over("wk_hi", [P, KE, D], "dA", 0), over("wk_lo", [P, KE, D], "dA", KE * D)
        wq2 = [(over(f"wq_hi{p}", [P, CW], "hs", 2 * p * CW), over(f"wq_lo{p}", [P, CW], "hs", (2 * p + 1) * CW))
               for p in range(2)]
        wo2 = [(over(f"wo_hi{p}", [P, CW], "bc", p * CW), over(f"wo_lo{p}", [P, CW], "xc", (KE + 2 * p) * T))
               for p in range(2)]

        acc = pb("acc", [P, TT, 512])
        pq = pb("pq", [P, 2, 512])
        pk = pb("pk", [P, 2, 512])

        def bank(n):
            return pq[:, n, :] if n < 2 else pk[:, n - 2, :]

        def silu_z(s):
            return sz[:, s, :] if s < 4 else xnT[:, s - 4, :]

        def y_bank(s):
            return acc[:, s, :] if s < TT else bank(s - TT)

        def stage(name, per):
            return Stage(nc, ctx, name, per)

        s_const = sem("const_loaded")
        s_x = sem("x_loaded")
        s_xr = sem("xr_loaded")
        s_xa = sem("xa_copied")
        s_ctx = sem("ctx_loaded")
        s_mask = sem("mask_loaded")
        s_pos = sem("pos_loaded")
        s_tab = sem("rotary_rows_loaded")
        s_bcw = sem("bc_rows_stored")
        s_bc = [sem(f"bc_loaded{p}") for p in range(2)]
        s_wa = [sem(f"wa_loaded{p}") for p in range(2)]
        s_wb = [sem(f"wb_loaded{p}") for p in range(2)]
        s_wk = sem("wk_loaded")
        s_wv = sem("wv_loaded")
        s_out = sem("out_stored")
        s_ident = sem("ident_made")
        s_init = sem("buffers_cleared")
        s_aneg = sem("decay_rates_made")
        s_ysum = sem("first_y_summed")
        ln1 = stage("ln1_variance", 1)
        ln1r = stage("ln1_rstd", 1)
        ln1n = stage("ln1_done", TT)
        ln1t = stage("ln1_transposed", KE)
        xnr = stage("xnT_ready", KE)
        inx = stage("in_proj_x", DT_TILES)
        cv0 = stage("conv_tap_last", DT_TILES)
        cv = stage("conv_done", DT_TILES)
        xcr = stage("xc_ready", DT_TILES)
        ssd = stage("ssm_done", 1)
        ssqd = stage("ssm_squared", 1)
        ssv = stage("ssm_mean_square", 1)
        ssr = stage("ssm_rms", 1)
        ssnd = stage("ssm_normalised", 1)
        sst = stage("ssm_transposed", 1)
        sstr = stage("ssmT_ready", 1)
        dtd = stage("dt_proj", DT_TILES)
        dtv = stage("dt_read", DT_TILES)
        spe = stage("softplus_exp", NCH)
        spl = stage("softplus_ln", NCH)
        spd = stage("softplus_done", NCH)
        ur = stage("u_ready", NCH)
        y0r = stage("y_started", NCH)
        ch_n = stage("dve_ln1", 2 * TT)
        ch_c = stage("dve_conv", (KC - 2) * DT_TILES)
        ch_f = stage("dve_ssm_softplus", 6 + 4 * NCH)
        dar = stage("decay_ready", NS * NCH)
        inr = stage("scan_input_ready", NS * NCH)
        scd = stage("scan_done", NS * NCH)
        hcd = stage("state_times_c", NS * NCH)
        yad = stage("y_added", NS * NCH)
        pid = stage("pos_index_ready", 1)
        rot = stage("rotary_transposed", 1)
        rop = stage("rotary_ready", 1)
        ac0 = stage("acc_cleared", 1)
        qd = stage("q_done", PAIRS)
        kd = stage("k_done", KVH)
        vd = stage("v_done", KVH)
        qrd = stage("q_swapped", PAIRS)
        krd = stage("k_swapped", KVH)
        qt1 = stage("q_times_cos", PAIRS)
        qt2 = stage("q_times_sin", PAIRS)
        kt1 = stage("k_times_cos", KVH)
        kt2 = stage("k_times_sin", KVH)
        qrdy = stage("q_ready", PAIRS)
        krdy = stage("k_ready", KVH)
        vrdy = stage("v_ready", KVH)
        sd = stage("scores_done", PAIRS)
        srd = stage("scores_read", PAIRS)
        scf = stage("scores_prefilled", PAIRS)
        smx = stage("scores_max", PAIRS)
        exd = stage("exp_done", PAIRS)
        rcp = stage("sum_inverted", PAIRS)
        prdy = stage("probs_ready", PAIRS)
        ptd = stage("probs_transposed", PAIRS)
        ptr = stage("probsT_ready", PAIRS)
        pvd = stage("pv_done", PAIRS)
        ordy = stage("o_ready", PAIRS)
        wod = stage("wo_done", PAIRS)
        s_acth = sem("activations_hi")
        s_actl = sem("activations_lo")
        wqh = stage("wq_hi", PAIRS)
        wqs = stage("wq_split", PAIRS)
        woh = stage("wo_hi", PAIRS)
        wos = stage("wo_split", PAIRS)
        wkh = stage("wk_hi", KVH)
        wks = stage("wk_split", KVH)
        olo = stage("o_lo_ready", PAIRS)
        x2r = stage("x2_ready", TT)
        ln3 = stage("ln3_variance", 1)
        ln3r = stage("ln3_rstd", 1)
        ln3n = stage("ln3_done", TT)
        ln3t = stage("ln3_transposed", KE)
        x3r = stage("x3T_ready", KE)
        rqd = stage("router_q", 1)
        rqr = stage("router_q_ready", 1)
        rsd = stage("router_scores", 1)
        rmd = stage("router_max", 1)
        rex = stage("router_exp", 1)
        awd = stage("a_proj", TT)
        zgd = stage("z_gated", TT)
        zgt = stage("z_transposed", KE)
        zgr = stage("zT_ready", KE)
        bwd = stage("b_proj", TT)
        outr = stage("out_ready", 1)
        ch_p = stage("dve_positions", 2)
        ch_a = stage("dve_mixture", 2 + 8 * TT)
        inz = stage("in_proj_z", DT_TILES)
        szr = stage("silu_z", DT_TILES)
        yr = stage("y_gated", DT_TILES)
        opd = stage("out_proj", TT)
        x1r = stage("x1_ready", TT)
        ln2 = stage("ln2_variance", 1)
        ln2r = stage("ln2_rstd", 1)
        ln2n = stage("ln2_done", TT)
        ln2t = stage("ln2_transposed", KE)
        qTr = stage("qT_ready", KE)
        ch_m = stage("dve_x1_norm", 2 * TT)
        wad = sem("wa_used")
        wbd = sem("wb_used")
        W_DT, W_KE = DT_TILES // 2, KE // 2

        def wa_base(i):
            if isinstance(i, int) and i == 0:
                return W_DT
            full = PAIRS + 2 * W_DT + W_KE
            return (i - 1) * full + (3 * W_DT - (W_DT if isinstance(i, int) and i == NBLK else 0))

        def wb_base(i):
            return 0 if isinstance(i, int) and i == 0 else (i - 1) * (PAIRS + W_DT + W_KE) + W_DT

        def wa_half(i):
            if isinstance(i, int):
                return wa_base(i) // 2
            return (i - 1) * ((PAIRS + 2 * W_DT + W_KE) // 2) + 3 * W_DT // 2

        def wb_half(i):
            return wb_base(i) // 2 if isinstance(i, int) else (i - 1) * ((PAIRS + W_DT + W_KE) // 2) + W_DT // 2

        def wa_places(mamba, attn, nxt):
            at_x = (PAIRS if attn else 0) + (W_DT if mamba else 0)
            return (2 if attn else 0), at_x, at_x + (W_DT if nxt else 0)

        def wb_places(mamba, attn):
            at_o = PAIRS if attn else 0
            return at_o, at_o + (W_DT if mamba else 0)

        block = ctx.enter_context(nc.Block())

        s_hold = sem("held_on_its_own")

        def hold(eng):
            eng.sem_inc(s_hold, 1)

        def lead(eng, *stages):
            for s in stages:
                eng.sem_inc(s.sem if isinstance(s, Stage) else s, LEAD)

        def iterations(eng, one):
            one(0, True, False, True)
            with eng.Fori(1, NBLK - 1) as i:
                one(i, True, True, True)
            one(NBLK - 1, True, True, False)
            one(NBLK, False, True, False)

        def steps(eng, one):
            with eng.Fori(0, NS // 2 - 1) as jj:
                one(jj, 0, False)
                one(jj, 1, False)
            one(NS // 2 - 1, 0, True)
            one(NS // 2 - 1, 1, True)

        @block.sync
        def _(eng):
            consts = [(xpw, a["xpw"]), (dtw, a["dtw"]), (rqw, a["rqw"]), (rkw, a["rkw"]), (lnw, a["lnw"]),
                      (cw, a["cw"]), (chan, a["chan"]), (aneg, a["alog"])]

            def load_wa(i, at, src):
                eng.wait_ge(wad, wa_base(i) + at + (LEAD - 1))
                eng.dma_start(wa[:, at % 2, :], src).then_inc(s_wa[at % 2], 16)

            def load_wa_j(i, at, jj, p, src):
                eng.wait_ge(wad, wa_base(i) + jj * 2 + (at + p + LEAD - 1))
                eng.dma_start(wa[:, p, :], src).then_inc(s_wa[p], 16)

            def load_wb(i, at, src):
                eng.wait_ge(wbd, wb_base(i) + at + (LEAD - 1))
                eng.dma_start(wb[:, at % 2, :], src).then_inc(s_wb[at % 2], 16)

            def load_wb_j(i, jj, o, src):
                eng.wait_ge(wbd, wb_base(i) + jj * 2 + (o + LEAD - 1))
                eng.dma_start(wb[:, o % 2, :], src).then_inc(s_wb[o % 2], 16)

            lead(eng, s_out)
            eng.dma_start(xm[:, :, :], a["x"][0]).then_inc(s_x, 16)
            for n in range(W_DT):
                if n >= 2:
                    eng.wait_ge(wad, LEAD + n - 1)
                eng.dma_start(wa[:, n % 2, :], a["wx"][n]).then_inc(s_wa[n % 2], 16)
                if n == 0:
                    for dst, src in consts:
                        eng.dma_start(dst[...], src).then_inc(s_const, 16)

            def one(i, mamba, attn, nxt):
                at_z, at_x, at_a = wa_places(mamba, attn, nxt)
                at_o, at_b = wb_places(mamba, attn)
                blk = i - 1
                if attn:
                    for n in range(2):
                        load_wa(i, n, a["wq"][n])
                    load_wb(i, 0, a["wo"][0])
                if mamba:
                    eng.wait_ge(sstr.sem, sstr.upto(i, 0))
                    eng.dma_start(scr[i].rearrange("c n t -> (c n) t"), ssmT[R:SSM, :]).then_inc(s_bcw, 16)
                    eng.wait_ge(s_bcw, i * 16 + 16)
                    for n in range(2):
                        eng.wait_ge(hcd.sem, hcd.upto(i, -1))
                        eng.dma_start(bc[:, n, :, :], scr[i, :, n, :].partition_broadcast(P)).then_inc(s_bc[n], 16)
                    for n in range(2):
                        load_wa(i, at_z + n, a["wz"][n])
                    if attn:
                        eng.wait_ge(ln2n.sem, ln2n.upto(blk, TT - 1))
                        hold(eng)
                        if not isinstance(i, int) or i > 1:
                            eng.wait_ge(outr.sem, outr.upto(blk, -1))
                        eng.dma_start(xa[:, :, :], xr[:, :, :]).then_inc(s_xa, 16)
                        eng.wait_ge(s_xa, blk * 16 + 16)
                    eng.dma_start(xr[:, :, :], a["x"][i]).then_inc(s_xr, 16)
                elif attn:
                    eng.wait_ge(ln2n.sem, ln2n.upto(blk, TT - 1))
                    eng.wait_ge(outr.sem, outr.upto(blk, -1))
                    eng.dma_start(xa[:, :, :], xr[:, :, :]).then_inc(s_xa, 16)
                if nxt:
                    eng.wait_ge(ln1n.sem, ln1n.upto(i, TT - 1))
                    eng.dma_start(xm[:, :, :], a["x"][i + 1]).then_inc(s_x, 16)
                if mamba:
                    for n in range(2, W_DT):
                        load_wa(i, at_z + n, a["wz"][n])
                z_uses = W_DT if mamba else 0

                def step(jj, p, tail):
                    if attn:
                        if not tail:
                            load_wa_j(i, z_uses + 2, jj, p, a["wq"][jj * 2 + (2 + p)])
                            if p == 0:
                                eng.wait_ge(kd.sem, kd.upto(blk, jj))
                                eng.dma_start(wk[:, :, :], a["wk"][jj + 1]).then_inc(s_wk, 16)
                            else:
                                eng.wait_ge(vd.sem, vd.upto(blk, jj))
                                eng.dma_start(wv[:, :, :], a["wv"][jj + 1]).then_inc(s_wv, 16)
                    if attn and not (tail and p == 1):
                        load_wb_j(i, jj, p + 1, a["wo"][jj * 2 + (1 + p)])
                    if mamba and not tail:
                        eng.wait_ge(hcd.sem, hcd.upto(i, NCH * (p + 1) - 1) + jj * (2 * NCH))
                        eng.dma_start(bc[:, p, :, :], scr[i, :, jj * 2 + (2 + p), :].partition_broadcast(P)).then_inc(
                            s_bc[p], 16)

                steps(eng, step)
                if mamba:
                    eng.wait_ge(pid.sem, pid.upto(i, -1))
                    hold(eng)
                    eng.dma_start(posi[:, :], a["pos"][i]).then_inc(s_pos, 16)
                    for n in range(2):
                        load_wb(i, at_o + n, a["ow"][n])
                if nxt:
                    for n in range(2):
                        load_wa(i, at_x + n, a["wx"][n])
                if mamba:
                    eng.wait_ge(kd.sem, kd.upto(i, -1))
                    hold(eng)
                    eng.wait_ge(vd.sem, vd.upto(i, -1))
                    hold(eng)
                    eng.dma_start(ctxT[:, :, :], a["ctx"][i]).then_inc(s_ctx, 16)
                    eng.dma_start(wk[:, :, :], a["wk"][0]).then_inc(s_wk, 16)
                    eng.dma_start(wv[:, :, :], a["wv"][0]).then_inc(s_wv, 16)
                    eng.wait_ge(srd.sem, srd.upto(i, -1))
                    hold(eng)
                    for h in range(2):
                        eng.dma_start(mask[h * SEQ:(h + 1) * SEQ, :, :], a["mask"][i]).then_inc(s_mask, 16)
                    for n in range(2, W_DT):
                        load_wb(i, at_o + n, a["ow"][n])
                if nxt:
                    for n in range(2, W_DT):
                        load_wa(i, at_x + n, a["wx"][n])
                if attn:
                    for n in range(W_KE):
                        load_wa(i, at_a + n, a["aw"][n])
                    for n in range(W_KE):
                        load_wb(i, at_b + n, a["bw"][n])
                if attn:
                    eng.wait_ge(outr.sem, outr.upto(blk, 0))
                    eng.dma_start(out[blk], xn).then_inc(s_out, 16)

            iterations(eng, one)
            eng.wait_ge(s_out, 16 * NBLK + LEAD)

        @block.gpsimd
        def _(eng):
            lead(eng, ln1r, ssr, ln2r, ln3r, inr, wqh, wqs, woh, wos, wkh, wks)
            G = nc.gpsimd
            G.memset(ident[:, :], 0.0).then_inc(s_ident, 1)
            eng.wait_ge(s_ident, 1)
            G.affine_select(out=ident[:, :], in_=ident[:, :], compare_op=ALU.not_equal, fill=1.0, base=0,
                            pattern=[[-1, P]], channel_multiplier=1).then_inc(s_ident, 1)
            G.memset(mhalf[:, :], -0.5).then_inc(s_init, 1)
            G.memset(dA[:, :, :], 0.0).then_inc(s_init, 1)
            G.memset(pz[:, :, :, :], 0.0).then_inc(s_init, 1)
            G.memset(zeros[:, :].bitcast(F32), 0.0).then_inc(s_init, 1)
            eng.wait_ge(s_init, 4)

            def rstd(blk, variance, done, n):
                eng.wait_ge(variance.sem, variance.upto(blk, 0))
                G.tensor_tensor(rs[:, 0:n], ve[:, 0:n], mhalf[:, 0:n], ALU.pow).then_inc(done.sem, 1)

            rstd(0, ln1, ln1r, TT)

            def one(i, mamba, attn, nxt):
                if mamba:
                    rstd(i, ssv, ssr, 3 * TT)

                def split(raw, two, hi, both, value):
                    G.tensor_scalar(two[0], raw, 1.0, None, ALU.mult).then_inc(hi.sem, 1)
                    eng.wait_ge(hi.sem, value(hi))
                    G.tensor_tensor(two[1], raw, two[0].bitcast(F32), ALU.subtract).then_inc(both.sem, 1)

                def split_wq(jj, o):
                    p = o % 2
                    eng.wait_ge(s_wa[p], (wa_half(i) + (o // 2 + 1) + jj) * 16)
                    eng.wait_ge(qd.sem, qd.upto(i - 1, o - 2) + jj * 2)
                    hold(eng)
                    split(wa[:, p, :], [x[:, :] for x in wq2[p]], wqh, wqs, lambda s: s.upto(0, o) + jj * 2)
                    eng.wait_ge(wqs.sem, wqs.upto(0, o) + jj * 2)
                    eng.sem_inc(wad, 1)

                def split_wo(jj, o):
                    p = o % 2
                    eng.wait_ge(s_wb[p], (wb_half(i) + (o // 2 + 1) + jj) * 16)
                    eng.wait_ge(wod.sem, wod.upto(i - 1, o - 2) + jj * 2)
                    hold(eng)
                    split(wb[:, p, :], [x[:, :] for x in wo2[p]], woh, wos, lambda s: s.upto(0, o) + jj * 2)
                    eng.wait_ge(wos.sem, wos.upto(0, o) + jj * 2)
                    eng.sem_inc(wbd, 1)

                def split_wk(g):
                    eng.wait_ge(s_wk, (i - 1) * (16 * KVH) + g * 16 + 16)
                    eng.wait_ge(kd.sem, kd.upto(i - 1, -1) + g)
                    hold(eng)
                    split(wk[:, :, :], [x[:, :, :] for x in wk2], wkh, wks, lambda s: s.upto(0, 0) + g)

                def split_step(jj, p, tail):
                    if not tail:
                        split_wq(jj, p + 2)
                        if p == 0:
                            split_wk(jj + 1)
                    if not (tail and p == 1):
                        split_wo(jj, p + 1)

                def step(jj, p, tail):
                    for c in range(NCH):
                        if c == 0:
                            eng.wait_ge(s_bc[p], i * (8 * NS) + jj * 16 + 16)
                        if p == 0:
                            eng.wait_ge(ur.sem, ur.upto(i, c))
                        eng.wait_ge(yad.sem, yad.upto(i, NCH * (p - 1) + c) + jj * (2 * NCH))
                        G.tensor_tensor(
                            hs[:, c, :].rearrange("p (d t) -> p d t", t=T), u[:, 2 * c:2 * c + 2, :],
                            bc[:, p, 0:1, :].to_broadcast([P, 2, T]), ALU.mult).then_inc(inr.sem, 1)

                if mamba:
                    steps(eng, step)
                else:
                    eng.wait_ge(yad.sem, yad.upto(i - 1, NS * NCH - 1))
                    split_wk(0)
                    split_wq(0, 0)
                    eng.wait_ge(ln2t.sem, ln2t.upto(i - 1, KE - 1))
                    split_wq(0, 1)
                    split_wo(0, 0)
                    steps(eng, split_step)
                if attn:
                    rstd(i - 1, ln3, ln3r, TT)
                if nxt:
                    rstd(i + 1, ln1, ln1r, TT)
                if mamba:
                    if attn:
                        eng.wait_ge(wod.sem, wod.upto(i - 1, PAIRS - 1))
                    eng.wait_ge(pid.sem, pid.upto(i, 0))
                    hold(eng)
                    for t in range(TT):
                        eng.indirect_dma_start(
                            out=tab[:, t, :], out_offset=None, in_=a["rotary"],
                            in_offset=bass.IndirectOffsetOnAxis(ap=posu[:, t:t + 1], axis=0)).then_inc(s_tab, 16)
                    rstd(i, ln2, ln2r, TT)

            iterations(eng, one)

        @block.scalar
        def _(eng):
            lead(eng, xnr, cv0, xcr, ssqd, sstr, dtv, spe, spl, dar, rop, qrd, krd, vrdy, y0r, scf, exd, ptr, ordy,
                 x3r, rqr, rex, zgr, szr, qTr)
            S = nc.scalar
            eng.wait_ge(s_const, 16 * 8)
            S.activation(aneg[:, :, :], aneg[:, :, :], ACT.Exp).then_inc(s_aneg, 1)

            def evacuate(to, banks, done, ready, b):
                for k in range(KE):
                    eng.wait_ge(done.sem, done.upto(b, k))
                    S.activation(to[:, k, :], banks(k), ACT.Copy).then_inc(ready.sem, 1)

            def convolve(b):
                for s in range(DT_TILES + 1):
                    if s < DT_TILES:
                        eng.wait_ge(inx.sem, inx.upto(b, s))
                        S.activation(xc[:, s, :], acc[:, s % 4, :], ACT.Identity, bias=chan[:, 0, s:s + 1],
                                     scale=cw[:, s, KC - 1:KC]).then_inc(cv0.sem, 1)
                    if s >= 1:
                        eng.wait_ge(cv.sem, cv.upto(b, s - 1))
                        S.activation(xc[:, s - 1, :], xc[:, s - 1, :], ACT.Silu).then_inc(xcr.sem, 1)

            evacuate(xnT, bank, ln1t, xnr, 0)
            convolve(0)

            def one(i, mamba, attn, nxt):
                blk = i - 1

                def swap_q(jj, o):
                    eng.wait_ge(qd.sem, qd.upto(blk, o) + jj * 2)
                    eng.wait_ge(qrdy.sem, qrdy.upto(blk, o - 1) + jj * 2)
                    S.activation(qr[0:64, :, :], pq[64:128, :, :], ACT.Copy)
                    S.activation(qr[64:128, :, :], pq[0:64, :, :], ACT.Copy).then_inc(qrd.sem, 1)

                def swap_k(g):
                    eng.wait_ge(kd.sem, kd.upto(blk, 0) + g)
                    eng.wait_ge(krdy.sem, krdy.upto(blk, -1) + g)
                    S.activation(kr[0:64, :], pk[64:128, 0, :], ACT.Copy, scale=float(D) ** -0.5)
                    S.activation(kr[64:128, :], pk[0:64, 0, :], ACT.Copy,
                                 scale=float(D) ** -0.5).then_inc(krd.sem, 1)

                def evac_v(g):
                    eng.wait_ge(vd.sem, vd.upto(blk, 0) + g)
                    eng.wait_ge(pvd.sem, pvd.upto(blk, -1) + g * 2)
                    S.activation(vt[:, :, :], pk[:, 1, :].rearrange("p (t d) -> p t d", d=D),
                                 ACT.Copy).then_inc(vrdy.sem, 1)

                def prefill(jj, o):
                    eng.wait_ge(exd.sem, exd.upto(blk, o - 1) + jj * 2)
                    S.activation(sc[:, :, :], zeros[:, :].rearrange("p (b k) -> p b k", k=SEQ), ACT.Copy,
                                 bias=MASKED).then_inc(scf.sem, 1)

                def exps(jj, o):
                    eng.wait_ge(smx.sem, smx.upto(blk, o) + jj * 2)
                    for b in range(NB):
                        ins = S.activation(pr[:, b, :], sc[:, b, :], ACT.Exp, bias=mx[:, b:b + 1],
                                           accum_out=sm[:, b:b + 1])
                    ins.then_inc(exd.sem, 1)

                def evac_pt(jj, p):
                    eng.wait_ge(ptd.sem, ptd.upto(blk, p) + jj * 2)
                    eng.wait_ge(pvd.sem, pvd.upto(blk, p - 1) + jj * 2)
                    for b in range(2):
                        ins = S.activation(pz[b * 64:(b + 1) * 64, :, b, :],
                                           pk[b * 64:(b + 1) * 64, p, :].rearrange("p (t r) -> p t r", r=P),
                                           ACT.Copy)
                    ins.then_inc(ptr.sem, 1)

                def evac_o(jj, p):
                    eng.wait_ge(pvd.sem, pvd.upto(blk, p) + jj * 2)
                    eng.wait_ge(wod.sem, wod.upto(blk, p - 1) + jj * 2)
                    o_ps = pk[:, :, :].rearrange("p c (x h q) -> p (c x) h q", h=2, q=SEQ)
                    to = oT if mamba else oT2[0]
                    for h in range(2):
                        ins = S.activation(to[:, h, :].rearrange("p (x q) -> p x q", q=SEQ), o_ps[:, :, h, :],
                                           ACT.Copy)
                    ins.then_inc(ordy.sem, 1)

                def decay(jj, p, c):
                    eng.wait_ge(scd.sem, scd.upto(i, NCH * p + c - 2) + jj * (2 * NCH))
                    for d in range(2):
                        s = 2 * c + d
                        to = dA[:, c % 2, d * T:(d + 1) * T].rearrange("p (b t) -> p b t", t=SEQ)
                        ins = S.activation(to[:, :, 1:SEQ],
                                           dt[:, s, :].rearrange("p (b t) -> p b t", t=SEQ)[:, :, 1:SEQ],
                                           ACT.Exp, scale=aneg[:, s, bass.ds(jj * 2 + p, 1)])
                    ins.then_inc(dar.sem, 1)

                def step(jj, p, tail):
                    last = tail and p == 1
                    if attn:
                        evac_pt(jj, p)
                    if mamba:
                        decay(jj, p, 2)
                        decay(jj, p, 3)
                    if attn and not last:
                        exps(jj, p + 1)
                    if mamba and not last:
                        decay(jj, p + 1, 0)
                    if attn:
                        evac_o(jj, p)
                    if mamba and not last:
                        decay(jj, p + 1, 1)
                    if attn and not tail:
                        swap_q(jj, p + 2)
                        if p == 0:
                            swap_k(jj + 1)
                        else:
                            evac_v(jj + 1)
                        prefill(jj, p + 2)

                if not mamba:
                    eng.wait_ge(s_ctx, blk * 16 + 16)
                    S.activation(ctxT2[0][:, :, :], ctxT[:, :, :], ACT.Copy).then_inc(s_acth, 1)
                    eng.wait_ge(yr.sem, yr.upto(blk, DT_TILES - 1))
                    eng.wait_ge(qTr.sem, qTr.upto(blk, KE - 1))
                    S.activation(qT2[0][:, :, :], qT[:, :, :], ACT.Copy).then_inc(s_acth, 1)
                if attn:
                    prefill(0, 0)
                if mamba:
                    eng.wait_ge(ssd.sem, ssd.upto(i, 0))
                    S.activation(ssq[:, :, :], acc[:, 0, 0:TT * SSM].rearrange("p (t c) -> p t c", c=SSM),
                                 ACT.Square).then_inc(ssqd.sem, 1)
                if attn:
                    eng.wait_ge(rot.sem, rot.upto(blk, 0))
                    S.activation(cosT[:, :], pq[:, 0, :], ACT.Copy)
                    S.activation(sinT[:, :], pq[:, 1, :], ACT.Copy).then_inc(rop.sem, 1)
                    swap_k(0)
                    evac_v(0)
                    swap_q(0, 0)
                if mamba:
                    eng.wait_ge(sst.sem, sst.upto(i, 0))
                    S.activation(ssmT[:, :], acc[0:SSM, 1, :], ACT.Copy).then_inc(sstr.sem, 1)
                    for s in range(DT_TILES):
                        eng.wait_ge(dtd.sem, dtd.upto(i, s))
                        S.activation(u[:, s, :], acc[:, s % 4, :], ACT.Abs, bias=chan[:, 1, s:s + 1])
                        if s == 0 and attn and (not isinstance(i, int) or i > 1):
                            eng.wait_ge(s_out, blk * 16 + LEAD)
                        S.activation(dt[:, s, :], acc[:, s % 4, :], ACT.Relu,
                                     bias=chan[:, 1, s:s + 1]).then_inc(dtv.sem, 1)
                if attn:
                    exps(0, 0)
                    swap_q(0, 1)
                    prefill(0, 1)
                if mamba:
                    eng.wait_ge(dtv.sem, dtv.upto(i, DT_TILES - 1))
                    for c in range(NCH):
                        S.activation(u[:, 2 * c:2 * c + 2, :], u[:, 2 * c:2 * c + 2, :], ACT.Exp,
                                     scale=-1.0).then_inc(spe.sem, 1)
                    for c in range(NCH):
                        eng.wait_ge(spe.sem, spe.upto(i, c))
                        S.activation(hs[:, c, :], u[:, 2 * c:2 * c + 2, :].rearrange("p d t -> p (d t)"),
                                     ACT.Ln, bias=1.0).then_inc(spl.sem, 1)
                    eng.wait_ge(yr.sem, yr.upto(i, -1))
                    for s in range(4):
                        eng.wait_ge(inz.sem, inz.upto(i, s))
                        S.activation(silu_z(s), acc[:, s % 4, :], ACT.Silu).then_inc(szr.sem, 1)
                    for c in range(NCH):
                        eng.wait_ge(ur.sem, ur.upto(i, c))
                        if c < 2:
                            decay(0, 0, c)
                        for d in (2 * c, 2 * c + 1):
                            ins = S.activation(xc[:, d, :], xc[:, d, :], ACT.Copy, scale=chan[:, 2, d:d + 1])
                        ins.then_inc(y0r.sem, 1)
                    eng.wait_ge(inz.sem, inz.upto(i, DT_TILES - 1))
                    for s in range(4, DT_TILES):
                        S.activation(silu_z(s), acc[:, s % 4, :], ACT.Silu).then_inc(szr.sem, 1)
                steps(eng, step)
                if attn:
                    evacuate(x3T, lambda k: acc[:, k, :], ln3t, x3r, blk)
                if nxt:
                    eng.wait_ge(yr.sem, yr.upto(i, DT_TILES - 1))
                    evacuate(xnT, bank, ln1t, xnr, i + 1)
                if attn:
                    eng.wait_ge(rqd.sem, rqd.upto(blk, 0))
                    S.activation(rq, pq[0:RD, 0, :], ACT.Copy).then_inc(rqr.sem, 1)
                    eng.wait_ge(rmd.sem, rmd.upto(blk, 0))
                    for t in range(TT):
                        ins = S.activation(gex[:, t, :], pq[:, 1, t * EXPERTS:(t + 1) * EXPERTS], ACT.Exp,
                                           bias=negm[:, t:t + 1])
                    ins.then_inc(rex.sem, 1)
                if nxt:
                    convolve(i + 1)
                if attn:
                    evacuate(zgT, bank, zgt, zgr, blk)
                if mamba:
                    evacuate(qT, lambda k: acc[:, k, :], ln2t, qTr, i)

            iterations(eng, one)

        @block.vector
        def _(eng):
            lead(eng, ln1, ln1n, cv, ssv, ssnd, spd, ur, ch_n, ch_c, ch_f, scd, hcd, yad, pid, qt1, qt2, kt1, kt2, qrdy,
                 krdy, srd, smx, rcp, prdy, x2r, ln3, ln3n, rmd, zgd, outr, ch_p, ch_a, yr, x1r,
                 ln2, ln2n, ch_m, olo)
            V = nc.vector
            eng.wait_ge(s_init, 4)
            eng.wait_ge(s_aneg, 1)
            V.tensor_scalar(aneg[:, :, :], aneg[:, :, :], -1.0, None, ALU.mult).then_inc(s_aneg, 1)

            def norm(ch, x, to, b, variance, rstd, done):
                for t in range(TT):
                    ch(V.bn_stats(stats[:, t, :], x[:, t, :]))
                for t in range(TT):
                    ch.wait()
                    hold(eng)
                    ch(V.bn_aggr(mv[:, t, :], stats[:, t, :]))
                ch.wait()
                V.tensor_scalar(ve[:, 0:TT], mv[:, :, 1], LN_EPS, None, ALU.add).then_inc(variance.sem, 1)
                eng.wait_ge(rstd.sem, rstd.upto(b, 0))
                for t in range(TT):
                    V.tensor_scalar(to[:, t, :], x[:, t, :], mv[:, t, 0:1], rs[:, t:t + 1], ALU.subtract,
                                    ALU.mult).then_inc(done.sem, 1)

            def norm_in(b):
                ch = Chain(eng, ch_n, b)
                eng.wait_ge(s_x, b * 16 + 16)
                eng.wait_ge(ln1t.sem, ln1t.upto(b, -1))
                norm(ch, xm, xn1, b, ln1, ln1r, ln1n)
                ch.end()

            def convolve(b):
                ch = Chain(eng, ch_c, b)
                for s in range(DT_TILES):
                    eng.wait_ge(cv0.sem, cv0.upto(b, s))
                    x3 = acc[:, s % 4, :].rearrange("p (b t) -> p b t", t=SEQ)
                    y3 = xc[:, s, :].rearrange("p (b t) -> p b t", t=SEQ)
                    for d in range(1, KC):
                        ins = V.scalar_tensor_tensor(
                            out=y3[:, :, d:SEQ], in0=x3[:, :, 0:SEQ - d], scalar=cw[:, s, KC - 1 - d:KC - d],
                            in1=y3[:, :, d:SEQ], op0=ALU.mult, op1=ALU.add)
                        if d < KC - 1:
                            ch(ins)
                            ch.wait()
                    ins.then_inc(cv.sem, 1)
                ch.end()

            def ssm_rows(i, ch):
                eng.wait_ge(ssqd.sem, ssqd.upto(i, 0))
                ch(V.tensor_reduce(ss[:, :, 0], ssq[:, :, 0:R], AX.X, ALU.add))
                ch(V.tensor_reduce(ss[:, :, 1:3], ssq[:, :, R:SSM].rearrange("p t (c n) -> p t c n", n=NS), AX.X,
                                   ALU.add))
                ch.wait()
                ve3 = ve[:, 0:3 * TT].rearrange("p (t c) -> p t c", c=3)
                ch(V.tensor_scalar(ve3[:, :, 0], ss[:, :, 0], 1.0 / R, RMS_EPS, ALU.mult, ALU.add))
                V.tensor_scalar(ve3[:, :, 1:3], ss[:, :, 1:3], 1.0 / NS, RMS_EPS, ALU.mult,
                                ALU.add).then_inc(ssv.sem, 1)
                ch.wait()
                eng.wait_ge(ssr.sem, ssr.upto(i, 0))
                rs3 = rs[:, 0:3 * TT].rearrange("p (t c) -> p t c", c=3)
                ps3 = acc[:, 0, 0:TT * SSM].rearrange("p (t c) -> p t c", c=SSM)
                ch(V.tensor_tensor(ssn[:, :, 0:R], ps3[:, :, 0:R], rs3[:, :, 0:1].to_broadcast([P, TT, R]),
                                   ALU.mult))
                for c in range(2):
                    at = R + c * NS
                    ch(V.tensor_tensor(ssn[:, :, at:at + NS], ps3[:, :, at:at + NS],
                                       rs3[:, :, 1 + c:2 + c].to_broadcast([P, TT, NS]), ALU.mult))
                ch.wait()
                V.tensor_tensor(ssn[:, :, :], ssn[:, :, :], lnw[:, :].unsqueeze(1).to_broadcast([P, TT, SSM]),
                                ALU.mult).then_inc(ssnd.sem, 1)

            def softplus(i, ch):
                for c in range(NCH):
                    two = slice(2 * c, 2 * c + 2)
                    e, l, v = u[:, two, :], hs[:, c, :].rearrange("p (d t) -> p d t", t=T), oT[:, :, :]
                    eng.wait_ge(spe.sem, spe.upto(i, c))
                    ch(V.tensor_scalar(v, e, 1.0, 1.0, ALU.add, ALU.subtract))
                    eng.wait_ge(spl.sem, spl.upto(i, c))
                    ch(V.scalar_tensor_tensor(out=l, in0=e, scalar=2.0 ** -24, in1=l, op0=ALU.is_gt,
                                              op1=ALU.mult))
                    ch.wait()
                    ch(V.tensor_tensor(e, e, v, ALU.subtract))
                    ch.wait()
                    ch(V.tensor_tensor(l, l, e, ALU.add))
                    ch.wait()
                    V.tensor_tensor(dt[:, two, :], dt[:, two, :], l, ALU.add).then_inc(spd.sem, 1)
                    eng.wait_ge(spd.sem, spd.upto(i, c))
                    V.tensor_tensor(u[:, two, :], dt[:, two, :], xc[:, two, :], ALU.mult).then_inc(ur.sem, 1)

            def scan(i, jj, p, c):
                at = jj * (2 * NCH)
                eng.wait_ge(inr.sem, inr.upto(i, NCH * p + c) + at)
                eng.wait_ge(dar.sem, dar.upto(i, NCH * p + c) + at)
                V.tensor_tensor_scan(out=hs[:, c, :], data0=dA[:, c % 2, :], data1=hs[:, c, :], initial=0.0,
                                     op0=ALU.mult, op1=ALU.add).then_inc(scd.sem, 1)

            def times_c(i, jj, p, c):
                eng.wait_ge(scd.sem, scd.upto(i, NCH * p + c) + jj * (2 * NCH))
                h3 = hs[:, c, :].rearrange("p (d t) -> p d t", t=T)
                V.tensor_tensor(h3, h3, bc[:, p, 1:2, :].to_broadcast([P, 2, T]), ALU.mult).then_inc(hcd.sem, 1)

            def add_y(i, jj, p, c):
                eng.wait_ge(hcd.sem, hcd.upto(i, NCH * p + c) + jj * (2 * NCH))
                V.tensor_tensor(xc[:, 2 * c:2 * c + 2, :], xc[:, 2 * c:2 * c + 2, :],
                                hs[:, c, :].rearrange("p (d t) -> p d t", t=T), ALU.add).then_inc(yad.sem, 1)

            def attention_of(blk):
                def rope(x_ps, scale, swapped, to, cos, sin, t1, t2, ready, at):
                    if scale is None:
                        V.tensor_tensor(to, x_ps, cos, ALU.mult).then_inc(t1.sem, 1)
                    else:
                        V.scalar_tensor_tensor(out=to, in0=x_ps, scalar=scale, in1=cos, op0=ALU.mult,
                                               op1=ALU.mult).then_inc(t1.sem, 1)
                    V.tensor_tensor(swapped, swapped, sin, ALU.mult).then_inc(t2.sem, 1)
                    eng.wait_ge(t1.sem, at(t1))
                    eng.wait_ge(t2.sem, at(t2))
                    V.tensor_tensor(to, to, swapped, ALU.add).then_inc(ready.sem, 1)

                def rope_q(jj, o):
                    eng.wait_ge(qrd.sem, qrd.upto(blk, o) + jj * 2)
                    eng.wait_ge(sd.sem, sd.upto(blk, o - 1) + jj * 2)

                    def seqs(x):
                        return x.rearrange("p h (b q) -> p h b q", q=SEQ)

                    two = [P, 2, T]
                    rope(seqs(pq[:, :, :]), None, seqs(qr[:, :, :]), qp[:, :, :].rearrange("p b (h q) -> p h b q", h=2),
                         seqs(cosT[:, :].unsqueeze(1).to_broadcast(two)),
                         seqs(sinT[:, :].unsqueeze(1).to_broadcast(two)), qt1, qt2, qrdy,
                         lambda s: s.upto(blk, o) + jj * 2)

                def rope_k(g):
                    eng.wait_ge(krd.sem, krd.upto(blk, 0) + g)
                    eng.wait_ge(sd.sem, sd.upto(blk, -1) + g * 2)
                    rope(pk[:, 0, :], float(D) ** -0.5, kr[:, :], kT[:, :], cosT[:, :], sinT[:, :], kt1, kt2, krdy,
                         lambda s: s.upto(blk, 0) + g)

                def mask_scores(jj, o):
                    eng.wait_ge(sd.sem, sd.upto(blk, o) + jj * 2)
                    eng.wait_ge(scf.sem, scf.upto(blk, o) + jj * 2)
                    hold(eng)
                    V.copy_predicated(sc[:, :, :], mask[:, :, :],
                                      pq[:, 0, :].rearrange("p (b k) -> p b k", k=SEQ)).then_inc(srd.sem, 1)

                def max_scores(jj, o):
                    eng.wait_ge(srd.sem, srd.upto(blk, o) + jj * 2)
                    V.tensor_reduce(mx[:, :], sc[:, :, :], AX.X, ALU.max, negate=True).then_inc(smx.sem, 1)

                def invert_sum(jj, o):
                    eng.wait_ge(exd.sem, exd.upto(blk, o) + jj * 2)
                    V.reciprocal(sm[:, :], sm[:, :]).then_inc(rcp.sem, 1)

                def probs(jj, o):
                    eng.wait_ge(rcp.sem, rcp.upto(blk, o) + jj * 2)
                    V.tensor_tensor(pr[:, :, :], pr[:, :, :], sm[:, :].unsqueeze(2).to_broadcast([P, NB, SEQ]),
                                    ALU.mult).then_inc(prdy.sem, 1)

                return rope_q, rope_k, mask_scores, max_scores, invert_sum, probs

            norm_in(0)
            convolve(0)

            def one(i, mamba, attn, nxt):
                blk = i - 1
                rope_q, rope_k, mask_scores, max_scores, invert_sum, probs = attention_of(blk)
                if not mamba:
                    eng.wait_ge(opd.sem, opd.upto(blk, TT - 1))
                    for n, (x, two) in enumerate([(ctxT, ctxT2), (qT, qT2)]):
                        eng.wait_ge(s_acth, n + 1)
                        V.tensor_tensor(two[1][:, :, :], x[:, :, :], two[0][:, :, :].bitcast(F32),
                                        ALU.subtract).then_inc(s_actl, 1)
                if mamba:
                    ch = Chain(eng, ch_f, i)
                    ssm_rows(i, ch)
                if attn:
                    eng.wait_ge(s_mask, blk * 32 + 32)
                    eng.wait_ge(rop.sem, rop.upto(blk, 0))
                    rope_k(0)
                    rope_q(0, 0)
                    for part in (mask_scores, max_scores, invert_sum, probs):
                        part(0, 0)
                    rope_q(0, 1)
                if mamba:
                    softplus(i, ch)
                    ch.end()
                    eng.wait_ge(y0r.sem, y0r.upto(i, NCH - 1))
                    hold(eng)

                def o_low(jj, p):
                    eng.wait_ge(ordy.sem, ordy.upto(blk, p) + jj * 2)
                    o_ps = pk[:, :, :].rearrange("p c (x h q) -> p (c x) h q", h=2, q=SEQ)
                    for h in range(2):
                        ins = V.tensor_tensor(oT2[1][:, h, :].rearrange("p (x q) -> p x q", q=SEQ), o_ps[:, :, h, :],
                                              oT2[0][:, h, :].bitcast(F32).rearrange("p (x q) -> p x q", q=SEQ),
                                              ALU.subtract)
                    ins.then_inc(olo.sem, 1)

                def step(jj, p, tail):
                    soft = attn and not (tail and p == 1)
                    if mamba:
                        scan(i, jj, p, 0)
                        scan(i, jj, p, 1)
                        times_c(i, jj, p, 0)
                    if soft:
                        mask_scores(jj, p + 1)
                    if mamba:
                        times_c(i, jj, p, 1)
                    if soft:
                        max_scores(jj, p + 1)
                    if mamba and attn:
                        add_y(i, jj, p, 0)
                        add_y(i, jj, p, 1)
                    if mamba:
                        scan(i, jj, p, 2)
                        scan(i, jj, p, 3)
                    if mamba:
                        times_c(i, jj, p, 2)
                    if soft:
                        invert_sum(jj, p + 1)
                    if mamba:
                        times_c(i, jj, p, 3)
                    if soft:
                        probs(jj, p + 1)
                    if mamba and attn:
                        add_y(i, jj, p, 2)
                        add_y(i, jj, p, 3)
                    if not mamba:
                        o_low(jj, p)
                    if attn and not tail:
                        rope_q(jj, p + 2)
                        if p == 0:
                            rope_k(jj + 1)

                steps(eng, step)
                if mamba:
                    eng.wait_ge(yad.sem, yad.upto(i, NS * NCH - 1))
                    eng.wait_ge(szr.sem, szr.upto(i, DT_TILES - 1))
                    if not attn:
                        for s in range(DT_TILES):
                            V.tensor_tensor(xc[:, s, :], xc[:, s, :], y_bank(s), ALU.add).then_inc(s_ysum, 1)
                    for s in range(DT_TILES):
                        if not attn:
                            eng.wait_ge(s_ysum, s + 1)
                        V.tensor_tensor(xc[:, s, :], xc[:, s, :], silu_z(s), ALU.mult).then_inc(yr.sem, 1)
                if mamba:
                    cp = Chain(eng, ch_p, i)
                    eng.wait_ge(s_pos, i * 16 + 16)
                    cp(V.tensor_scalar(posf[:, 0, :], posi[:, :], 0.0, float(MAXPOS), ALU.is_lt, ALU.mult))
                    cp.wait()
                    cp(V.tensor_tensor(posf[:, 1, :], posi[:, :], posf[:, 0, :], ALU.add))
                    cp.wait()
                    V.tensor_scalar(posu[:, :], posf[:, 1, :], 0.0, float(MAXPOS - 1), ALU.max,
                                    ALU.min).then_inc(pid.sem, 1)
                    cp.end()
                if attn:
                    ca = Chain(eng, ch_a, blk)
                    eng.wait_ge(wod.sem, wod.upto(blk, PAIRS - 1))
                    eng.wait_ge(s_xa, blk * 16 + 16)
                    for t in range(TT):
                        V.tensor_tensor(xa[:, t, :], xa[:, t, :], acc[:, t, :], ALU.add).then_inc(x2r.sem, 1)
                    eng.wait_ge(x2r.sem, x2r.upto(blk, TT - 1))
                    norm(ca, xa, xn, blk, ln3, ln3r, ln3n)
                if nxt:
                    norm_in(i + 1)
                if mamba:
                    cm = Chain(eng, ch_m, i)
                    eng.wait_ge(s_xr, i * 16 + 16)
                    for t in range(TT):
                        eng.wait_ge(opd.sem, opd.upto(i, t))
                        V.tensor_tensor(xr[:, t, :], xr[:, t, :], bank(t), ALU.add).then_inc(x1r.sem, 1)
                    eng.wait_ge(x1r.sem, x1r.upto(i, TT - 1))
                    norm(cm, xr, xn2, i, ln2, ln2r, ln2n)
                    cm.end()
                if attn:
                    eng.wait_ge(rsd.sem, rsd.upto(blk, 0))
                    hold(eng)
                    for t in range(TT):
                        raw = pq[:, 1, t * EXPERTS:(t + 1) * EXPERTS]
                        ca(V.max(top[:, t, 0:8], raw))
                        ca.wait()
                        hold(eng)
                        ca(V.match_replace(rsc[:, t, :], top[:, t, 0:8], raw, NEG))
                        ca.wait()
                        hold(eng)
                        ca(V.max(top[:, t, 8:16], rsc[:, t, :]))
                        ca.wait()
                        hold(eng)
                        ca(V.match_replace(rsc[:, t, :], top[:, t, 8:16], rsc[:, t, :], NEG))
                    ca.wait()
                    V.tensor_scalar(negm[:, :], top[:, :, 0], -1.0, None, ALU.mult).then_inc(rmd.sem, 1)
                    eng.wait_ge(rex.sem, rex.upto(blk, 0))
                    for t in range(TT):
                        ca(V.scalar_tensor_tensor(out=gate[:, t, :], in0=rsc[:, t, :], scalar=NEG,
                                                  in1=gex[:, t, :], op0=ALU.is_equal, op1=ALU.mult))
                    ca.wait()
                    ca(V.tensor_reduce(gs[:, :], gate, AX.X, ALU.add))
                    ca.wait()
                    ca(V.reciprocal(gs[:, :], gs[:, :]))
                    ca.wait()
                    for t in range(TT):
                        ca(V.tensor_scalar(gate[:, t, :], gate[:, t, :], gs[:, t:t + 1], SCALING, ALU.mult,
                                           ALU.mult))
                    ca.wait()
                if nxt:
                    convolve(i + 1)
                if attn:
                    for t in range(TT):
                        eng.wait_ge(awd.sem, awd.upto(blk, t))
                        V.tensor_tensor(zg[:, t, :].rearrange("p (e r) -> p e r", r=RANK),
                                        (bank(t) if nxt else acc[:, t, :]).rearrange("p (e r) -> p e r", r=RANK),
                                        gate[:, t, :].unsqueeze(2).to_broadcast([P, EXPERTS, RANK]),
                                        ALU.mult).then_inc(zgd.sem, 1)
                if attn:
                    for t in range(TT):
                        eng.wait_ge(bwd.sem, bwd.upto(blk, t))
                        ins = V.tensor_tensor(xn[:, t, :], xa[:, t, :], bank(t), ALU.add)
                    ins.then_inc(outr.sem, 1)
                    ca.end()

            iterations(eng, one)

        @block.tensor
        def _(eng):
            lead(eng, ln1t, inx, ssd, sst, dtd, rot, ac0, qd, kd, vd, sd, ptd, pvd, wod, ln3t, rqd, rsd, awd, zgt,
                 bwd, inz, opd, ln2t, wad, wbd)
            M = nc.tensor
            eng.wait_ge(s_ident, 2)
            eng.wait_ge(s_init, 4)
            eng.wait_ge(s_const, 16 * 8)

            def accs(k):
                return acc[:, k, :]

            def turn(x, banks, normed, done, b):
                for k in range(KE):
                    for t in range(TT):
                        if k == 0:
                            eng.wait_ge(normed.sem, normed.upto(b, t))
                        ins = M.transpose(banks(k)[:, t * P:(t + 1) * P], x[:, t, k * P:(k + 1) * P], ident[:, :])
                    ins.then_inc(done.sem, 1)

            def wa4(p):
                return wa[:, p, :].rearrange("p (k c) -> p k c", k=KE)

            def project_in(b, loaded, banks, free, done):
                for s in range(DT_TILES):
                    if s % 2 == 0:
                        loaded(s // 2)
                    free(s)
                    for k in range(KE):
                        ins = M.matmul(banks(s % 4), wa4((s // 2) % 2)[:, k, (s % 2) * P:(s % 2 + 1) * P],
                                       xnT[:, k, :], start=(k == 0), stop=(k == KE - 1))
                    ins.then_inc(done.sem, 1)
                    if s % 2 == 1:
                        eng.wait_ge(done.sem, done.upto(b, s))
                        eng.sem_inc(wad, 1)

            def free_conv(b):
                def free(s):
                    if s >= 4:
                        eng.wait_ge(cv.sem, cv.upto(b, s - 4))
                return free

            turn(xn1, bank, ln1n, ln1t, 0)
            eng.wait_ge(xnr.sem, xnr.upto(0, KE - 1))
            project_in(0, lambda n: eng.wait_ge(s_wa[n % 2], 16 * (n // 2 + 1)), accs, free_conv(0), inx)

            def one(i, mamba, attn, nxt):
                blk = i - 1
                at_z, at_x, at_a = wa_places(mamba, attn, nxt)
                at_o, at_b = wb_places(mamba, attn)

                def use_wa(at):
                    eng.wait_ge(s_wa[at % 2], (wa_half(i) + (at // 2 + 1)) * 16)

                def use_wb(at):
                    eng.wait_ge(s_wb[at % 2], (wb_half(i) + (at // 2 + 1)) * 16)

                def wb2(p):
                    return wb[:, p, :].rearrange("p (h c) -> p h c", h=2)

                evacuated, o_blk = (ordy, blk) if mamba else (olo, 0)

                def project_q(jj, o):
                    p = o % 2
                    if not mamba:
                        eng.wait_ge(wqs.sem, wqs.upto(0, o) + jj * 2)
                        for h in range(2):
                            for k in range(KE):
                                wcol = slice(k * 2 * P + h * P, k * 2 * P + (h + 1) * P)
                                for n, (a_w, a_x) in enumerate(PASSES):
                                    ins = M.matmul(pq[:, h, :], wq2[p][a_w][:, wcol], qT2[a_x][:, k, :],
                                                   start=(k == 0 and n == 0), stop=(k == KE - 1 and n == 2))
                        ins.then_inc(qd.sem, 1)
                        return
                    z_loads = W_DT // 2 if o >= 2 else 0
                    eng.wait_ge(s_wa[p], (wa_half(i) + (o // 2 + 1 + z_loads) + jj) * 16)
                    for h in range(2):
                        for k in range(KE):
                            ins = M.matmul(pq[:, h, :], wa4(p)[:, k, h * P:(h + 1) * P], qT[:, k, :],
                                           start=(k == 0), stop=(k == KE - 1))
                    ins.then_inc(qd.sem, 1)

                def free_wa(jj, o):
                    if not mamba:
                        return
                    eng.wait_ge(qd.sem, qd.upto(blk, o) + jj * 2)
                    eng.sem_inc(wad, 1)

                def project_k(g):
                    if not mamba:
                        eng.wait_ge(wks.sem, wks.upto(0, 0) + g)
                        for k in range(KE):
                            for n, (a_w, a_x) in enumerate(PASSES):
                                ins = M.matmul(pk[:, 0, :], wk2[a_w][:, k, :], ctxT2[a_x][:, k, :],
                                               start=(k == 0 and n == 0), stop=(k == KE - 1 and n == 2))
                        ins.then_inc(kd.sem, 1)
                        return
                    eng.wait_ge(s_wk, blk * (16 * KVH) + g * 16 + 16)
                    for k in range(KE):
                        ins = M.matmul(pk[:, 0, :], wk[:, k, :], ctxT[:, k, :], start=(k == 0),
                                       stop=(k == KE - 1))
                    ins.then_inc(kd.sem, 1)

                def project_v(g):
                    eng.wait_ge(s_wv, blk * (16 * KVH) + g * 16 + 16)
                    for t in range(TT):
                        for k in range(KE):
                            ins = M.matmul(pk[:, 1, t * D:(t + 1) * D], ctxT[:, k, t * P:(t + 1) * P],
                                           wv[:, k, :], start=(k == 0), stop=(k == KE - 1))
                    ins.then_inc(vd.sem, 1)

                def scores(jj, o):
                    eng.wait_ge(qrdy.sem, qrdy.upto(blk, o) + jj * 2)
                    eng.wait_ge(krdy.sem, krdy.upto(blk, o // 2) + jj)
                    for b in range(NB):
                        ins = M.matmul(pq[:, 0, b * SEQ:(b + 1) * SEQ], qp[:, b, :],
                                       kT[:, b * SEQ:(b + 1) * SEQ], start=True, stop=True)
                    ins.then_inc(sd.sem, 1)

                def turn_probs(jj, p, last):
                    eng.wait_ge(prdy.sem, prdy.upto(blk, p) + jj * 2)
                    if last:
                        eng.wait_ge(evacuated.sem, evacuated.upto(o_blk, p - 1) + jj * 2)
                    flat = pr[:, :, :].rearrange("p b k -> p (b k)")
                    for t in range(TT):
                        ins = M.transpose(pk[:, p, t * P:(t + 1) * P], flat[:, t * P:(t + 1) * P], ident[:, :])
                    ins.then_inc(ptd.sem, 1)

                def values(jj, p):
                    eng.wait_ge(ptr.sem, ptr.upto(blk, p) + jj * 2)
                    eng.wait_ge(vrdy.sem, vrdy.upto(blk, 0) + jj)
                    for t in range(TT):
                        ins = M.matmul(pk[:, t // 2, (t % 2) * 2 * P:(t % 2 + 1) * 2 * P], vt[:, t, :],
                                       pz[:, t, :, :], start=True, stop=True)
                    ins.then_inc(pvd.sem, 1)

                def project_o(jj, o, half, stop):
                    if not mamba:
                        if half == 0:
                            eng.wait_ge(olo.sem, olo.upto(0, o) + jj * 2)
                            eng.wait_ge(wos.sem, wos.upto(0, o) + jj * 2)
                        for t in (2 * half, 2 * half + 1):
                            for h in range(2):
                                for n, (a_w, a_x) in enumerate(PASSES):
                                    ins = M.matmul(acc[:, t, :], oT2[a_x][:, h, t * P:(t + 1) * P],
                                                   wo2[o % 2][a_w][:, h * E:(h + 1) * E], start=False,
                                                   stop=(stop and h == 1 and n == 2))
                        if half == 1:
                            ins.then_inc(wod.sem, 1)
                        return
                    if half == 0:
                        eng.wait_ge(ordy.sem, ordy.upto(blk, o) + jj * 2)
                        eng.wait_ge(s_wb[o % 2], (wb_half(i) + (o // 2 + 1) + jj) * 16)
                    for t in (2 * half, 2 * half + 1):
                        for h in range(2):
                            ins = M.matmul(acc[:, t, :], oT[:, h, t * P:(t + 1) * P], wb2(o % 2)[:, h, :],
                                           start=False, stop=(stop and h == 1))
                    if half == 1:
                        ins.then_inc(wod.sem, 1)

                def free_wb(jj, o):
                    if not mamba:
                        return
                    eng.wait_ge(wod.sem, wod.upto(blk, o) + jj * 2)
                    eng.sem_inc(wbd, 1)

                def step(jj, p, tail, first=False):
                    last = tail and p == 1
                    turn_probs(jj, p, last)
                    if not first:
                        project_o(jj, p - 1, 0, False)
                    late = not mamba and p == 1
                    if not last and not late:
                        scores(jj, p + 1)
                    if not first:
                        project_o(jj, p - 1, 1, False)
                    if not last and late:
                        scores(jj, p + 1)
                    values(jj, p)
                    if not first:
                        free_wb(jj, p - 1)
                    if not tail:
                        eng.wait_ge(srd.sem, srd.upto(blk, p + 1) + jj * 2)
                        project_q(jj, p + 2)
                        eng.wait_ge(evacuated.sem, evacuated.upto(o_blk, p) + jj * 2)
                        if p == 0:
                            project_k(jj + 1)
                        else:
                            project_v(jj + 1)
                        free_wa(jj, p + 2)
                    if last:
                        project_o(jj, p, 0, True)
                        project_o(jj, p, 1, True)
                        free_wb(jj, p)

                if mamba:
                    eng.wait_ge(qTr.sem, qTr.upto(i, -1))
                    eng.wait_ge(xcr.sem, xcr.upto(i, DT_TILES - 1))
                    for t in range(TT):
                        for s in range(DT_TILES):
                            ins = M.matmul(acc[:, 0, t * SSM:(t + 1) * SSM], xc[:, s, t * P:(t + 1) * P],
                                           xpw[:, s, :], start=(s == 0), stop=(s == DT_TILES - 1))
                    ins.then_inc(ssd.sem, 1)
                if attn:
                    eng.wait_ge(outr.sem, outr.upto(blk, -1))
                    eng.wait_ge(s_tab, blk * (16 * TT) + 16 * TT)
                    hold(eng)
                    for c in range(2):
                        for t in range(TT):
                            ins = M.transpose(pq[:, c, t * P:(t + 1) * P], tab[:, t, c * D:(c + 1) * D],
                                              ident[:, :])
                    ins.then_inc(rot.sem, 1)
                    eng.wait_ge(s_ctx, blk * 16 + 16)
                    if not mamba:
                        eng.wait_ge(s_actl, 2)
                    project_k(0)
                    project_v(0)
                    eng.wait_ge(rop.sem, rop.upto(blk, 0))
                    eng.wait_ge(qTr.sem, qTr.upto(blk, KE - 1))
                    project_q(0, 0)
                    free_wa(0, 0)
                if mamba:
                    eng.wait_ge(ssnd.sem, ssnd.upto(i, 0))
                    hold(eng)
                    for t in range(TT):
                        ins = M.transpose(acc[0:SSM, 1, t * P:(t + 1) * P], ssn[:, t, :], ident[:, :])
                    ins.then_inc(sst.sem, 1)
                    eng.wait_ge(sstr.sem, sstr.upto(i, 0))
                    for s in range(DT_TILES):
                        if s >= 4:
                            eng.wait_ge(dtv.sem, dtv.upto(i, s - 4))
                        M.matmul(acc[:, s % 4, :], dtw[:, s * P:(s + 1) * P], ssmT[0:R, :], start=True,
                                 stop=True).then_inc(dtd.sem, 1)
                if attn:
                    scores(0, 0)
                    eng.wait_ge(srd.sem, srd.upto(blk, 0))
                    project_q(0, 1)
                    free_wa(0, 1)
                if mamba:
                    eng.wait_ge(dtv.sem, dtv.upto(i, DT_TILES - 1))

                    def free_z(s):
                        if s >= 4:
                            eng.wait_ge(szr.sem, szr.upto(i, s - 4))

                    project_in(i, lambda n: use_wa(at_z + n), accs, free_z, inz)
                if not attn:
                    eng.wait_ge(szr.sem, szr.upto(i, DT_TILES - 1))
                    for s in range(DT_TILES):
                        M.matmul(y_bank(s), zeros[:, 0:P], zeros[:, :], start=True, stop=False)

                    def sum_y(jj, p, tail):
                        for c in range(NCH):
                            eng.wait_ge(hcd.sem, hcd.upto(i, NCH * p + c) + jj * (2 * NCH))
                            for d in range(2):
                                ins = M.matmul(y_bank(2 * c + d), ident[:, :], hs[:, c, d * T:(d + 1) * T],
                                               start=False, stop=(tail and p == 1))
                            ins.then_inc(yad.sem, 1)

                    steps(eng, sum_y)
                    eng.wait_ge(yr.sem, yr.upto(i, DT_TILES - 1))
                if attn:
                    step(0, 0, False, first=True)
                    if mamba:
                        eng.wait_ge(szr.sem, szr.upto(i, DT_TILES - 1))
                    for t in range(TT):
                        M.matmul(acc[:, t, :], zeros[:, 0:P], zeros[:, :], start=True, stop=False)
                    step(0, 1, False)
                    with eng.Fori(1, NS // 2 - 1) as jj:
                        step(jj, 0, False)
                        step(jj, 1, False)
                    step(NS // 2 - 1, 0, True)
                    step(NS // 2 - 1, 1, True)
                if mamba:
                    if attn:
                        eng.wait_ge(ordy.sem, ordy.upto(blk, PAIRS - 1))
                    for s in range(DT_TILES):
                        eng.wait_ge(yr.sem, yr.upto(i, s))
                        if s % 2 == 0:
                            use_wb(at_o + s // 2)
                        for t in range(TT):
                            ins = M.matmul(bank(t), xc[:, s, t * P:(t + 1) * P], wb2((s // 2) % 2)[:, s % 2, :],
                                           start=(s == 0), stop=(s == DT_TILES - 1))
                            if s == DT_TILES - 1:
                                ins.then_inc(opd.sem, 1)
                        if s % 2 == 1:
                            eng.drain().then_inc(wbd, 1)
                if attn:
                    turn(xn, accs, ln3n, ln3t, blk)
                if mamba:
                    eng.wait_ge(x1r.sem, x1r.upto(i, TT - 1))
                if nxt:
                    turn(xn1, bank, ln1n, ln1t, i + 1)
                    eng.wait_ge(xnr.sem, xnr.upto(i + 1, KE - 1))
                if attn:
                    eng.wait_ge(x3r.sem, x3r.upto(blk, KE - 1))
                    for k in range(KE):
                        ins = M.matmul(pq[0:RD, 0, :], rqw[:, k, :], x3T[:, k, :], start=(k == 0),
                                       stop=(k == KE - 1))
                    ins.then_inc(rqd.sem, 1)
                    eng.wait_ge(rqr.sem, rqr.upto(blk, 0))
                    for t in range(TT):
                        ins = M.matmul(pq[:, 1, t * EXPERTS:(t + 1) * EXPERTS], rq[:, t * P:(t + 1) * P],
                                       rkw[:, :], start=True, stop=True)
                    ins.then_inc(rsd.sem, 1)
                if nxt:
                    if not attn:
                        eng.wait_ge(szr.sem, szr.upto(i, DT_TILES - 1))
                    project_in(i + 1, lambda n: use_wa(at_x + n), accs, free_conv(i + 1), inx)
                if attn:
                    if nxt:
                        eng.wait_ge(rex.sem, rex.upto(blk, 0))
                    for k in range(KE):
                        if k % 2 == 0:
                            use_wa(at_a + k // 2)
                        for t in range(TT):
                            ins = M.matmul(bank(t) if nxt else acc[:, t, :], x3T[:, k, t * P:(t + 1) * P],
                                           wb2_of_wa(k // 2)[:, k % 2, :], start=(k == 0), stop=(k == KE - 1))
                            if k == KE - 1:
                                ins.then_inc(awd.sem, 1)
                        if k % 2 == 1:
                            eng.drain().then_inc(wad, 1)
                    turn(zg, bank, zgd, zgt, blk)
                    eng.wait_ge(zgr.sem, zgr.upto(blk, KE - 1))
                    for k in range(KE):
                        if k % 2 == 0:
                            use_wb(at_b + k // 2)
                        for t in range(TT):
                            ins = M.matmul(bank(t), zgT[:, k, t * P:(t + 1) * P], wb2(k // 2)[:, k % 2, :],
                                           start=(k == 0), stop=(k == KE - 1))
                            if k == KE - 1:
                                ins.then_inc(bwd.sem, 1)
                        if k % 2 == 1:
                            eng.drain().then_inc(wbd, 1)
                if mamba:
                    if nxt:
                        eng.wait_ge(cv.sem, cv.upto(i + 1, DT_TILES - 1))
                    turn(xn2, accs, ln2n, ln2t, i)

            def wb2_of_wa(p):
                return wa[:, p, :].rearrange("p (h c) -> p h c", h=2)

            iterations(eng, one)


_KC = np.ascontiguousarray


def _tables():
    inv = (np.float32(1.0) / np.float32(THETA) ** (np.arange(0, D, 2, dtype=np.float32) / np.float32(D))).astype(
        np.float32)
    f = np.arange(MAXPOS, dtype=np.float32)[:, None] * inv[None, :]
    c, s = np.cos(f), np.sin(f)
    return np.concatenate([c, c, -s, s], axis=1).astype(np.float32)


def kernel(**inputs):
    import concourse.bacc as _bacc
    from concourse.bass_utils import run_bass_kernel_spmd as _run

    w = {k: np.asarray(v) for k, v in inputs.items()}

    def cols(m, width):
        return _KC(m.reshape(KE, P, -1, width).transpose(2, 1, 0, 3))

    def rows2(m):
        return _KC(m.reshape(-1, 2, P, E).transpose(0, 2, 1, 3))

    inw = w["L0_attn_in_proj_w"]
    arrays = {
        "x": _KC(w["x"].reshape(NBLK, TT, P, E).transpose(0, 2, 1, 3)),
        "ctx": _KC(w["ctx_4096"].reshape(NBLK, T, KE, P).transpose(0, 3, 2, 1)),
        "pos": _KC(w["pos_BxS2"].reshape(NBLK, TT, P).transpose(0, 2, 1)),
        "mask": _KC(w["mask_BxSxS2_ik0"].reshape(NBLK, NB, SEQ, SEQ).transpose(0, 2, 1, 3)),
        "wx": cols(inw[:, :DIN], 2 * P), "wz": cols(inw[:, DIN:], 2 * P),
        "wq": cols(w["L0_xattn_Wq"], 2 * P), "wk": cols(w["L0_xattn_Wk"], D), "wv": cols(w["L0_xattn_Wv"], D),
        "wo": rows2(w["L0_xattn_Wo"]), "ow": rows2(w["L0_attn_out_proj_w"].T),
        "aw": rows2(w["L0_ffn_A_w"].T), "bw": rows2(w["L0_ffn_B_w"].T),
        "xpw": _KC(w["L0_attn_x_proj_w"].T.reshape(DT_TILES, P, SSM).transpose(1, 0, 2)),
        "dtw": _KC(w["L0_attn_dt_proj_w"].T),
        "rqw": _KC(w["L0_ffn_Wq_w"].T.reshape(KE, P, RD).transpose(1, 0, 2)),
        "rkw": _KC(w["L0_ffn_keys"].T),
        "lnw": _KC(np.broadcast_to(np.concatenate(
            [w["L0_attn_dt_ln_w"], w["L0_attn_B_ln_w"], w["L0_attn_C_ln_w"]])[None, :], (P, SSM))),
        "cw": _KC(w["L0_attn_conv_w"].reshape(DT_TILES, P, KC).transpose(1, 0, 2)),
        "chan": _KC(np.stack([w["L0_attn_conv_b"], w["L0_attn_dt_bias"], w["L0_attn_D_param"]]).reshape(
            3, DT_TILES, P).transpose(2, 0, 1)),
        "alog": _KC(w["L0_attn_A_log"].reshape(DT_TILES, P, NS).transpose(1, 0, 2)),
        "rotary": _tables(),
    }
    nc = _bacc.Bacc("TRN2", target_bir_lowering=False, num_devices=1)
    aps = {}
    for name, arr in arrays.items():
        aps[name] = nc.dram_tensor(f"in_{name}", arr.shape, mybir.dt.from_np(arr.dtype), kind="ExternalInput").ap()
    for name in ("wx", "wz", "wq", "wo", "ow", "aw", "bw"):
        aps[name] = aps[name].rearrange("n p k c -> n p (k c)")
    out = nc.dram_tensor("out", (NBLK, TT, P, E), F32, kind="ExternalOutput").ap()
    build(nc, aps, out.rearrange("b t p e -> b p t e"))
    r = _run(nc, [{f"in_{k}": v for k, v in arrays.items()}], core_ids=[0])
    return r.results[0]["out"].reshape(BATCH, SEQ, E)
```
